# Optimizing a Trainium2 kernel written in Bass

```python
import numpy as np
import jax
import jax.numpy as jnp

def _softmax(x, axis=-1):
    return jax.nn.softmax(x, axis=axis)

def _gelu(x):
    return jax.nn.gelu(x, approximate=True)

def _silu(x):
    return jax.nn.silu(x)

def _sigmoid(x):
    return jax.nn.sigmoid(x)

def _layernorm(x, axis=-1, eps=1e-05):
    m = jnp.mean(x, axis=axis, keepdims=True)
    v = jnp.var(x, axis=axis, keepdims=True)
    return (x - m) / jnp.sqrt(v + eps)

def _scatter_add(tgt, idx, src, axis=0):
    return tgt.at[idx].add(src)

def _segment_sum(src, seg, n):
    return jax.ops.segment_sum(src, seg, n)
kernel_name = 'mk_hybrid_d1_jaxref_r4_1b2991'

def setup_inputs(seed: int=0):
    np.random.seed(seed)
    _w = jnp.asarray

    def _L0_attn_a_setup():
        import jax, jax.numpy as jnp
        import numpy as np
        N_HEAD = 32
        ROPE_BASE = 10000.0

        def _rope_cos_sin(T, n_elem, dtype):
            theta = 1.0 / ROPE_BASE ** (jnp.arange(0, n_elem, 2, dtype=dtype) / n_elem)
            seq_idx = jnp.arange(T, dtype=dtype)
            idx_theta = jnp.outer(seq_idx, theta)
            idx_theta2 = jnp.concatenate([idx_theta, idx_theta], axis=-1)
            return (jnp.cos(idx_theta2), jnp.sin(idx_theta2))

        def _apply_rope(x, cos, sin):
            d2 = x.shape[-1] // 2
            rot = jnp.concatenate([-x[..., d2:], x[..., :d2]], axis=-1)
            return x * cos + rot * sin
        key = jax.random.key(seed)
        k1, k2, k3, k4 = jax.random.split(key, 4)
        B, T, C = (1, 512, 1024)
        s_in = 1.0 / np.sqrt(C)
        return {'x': jax.random.normal(k1, (B, T, C), jnp.float32), 'w_attn': jax.random.normal(k2, (3 * C, C), jnp.float32) * s_in, 'w_proj': jax.random.normal(k3, (C, C), jnp.float32) * s_in, 'adapter_wte': jax.random.normal(k4, (10, C), jnp.float32), 'gating': jnp.ones((1,), jnp.float32)}
    _L0_attn_a_in = _L0_attn_a_setup()

    def _L0_attn_b_setup():
        import jax, jax.numpy as jnp
        import numpy as np
        B, N, D = (8, 256, 1024)
        H = 8
        HEAD_DIM = D // H
        E = HEAD_DIM // H
        key = jax.random.key(seed)
        ks = jax.random.split(key, 7)
        s = 0.02
        return {'x': jax.random.normal(ks[0], (B, N, D), dtype=jnp.float32), 'Wqk_w': jax.random.normal(ks[1], (2 * HEAD_DIM, D), dtype=jnp.float32) * s, 'Wqk_b': jnp.zeros((2 * HEAD_DIM,), dtype=jnp.float32), 'Wv_w': jax.random.normal(ks[2], (HEAD_DIM, D), dtype=jnp.float32) * s, 'Wv_b': jnp.zeros((HEAD_DIM,), dtype=jnp.float32), 'Wo_w': jax.random.normal(ks[3], (D, HEAD_DIM), dtype=jnp.float32) * s, 'Wo_b': jnp.zeros((D,), dtype=jnp.float32)}
    _L0_attn_b_in = _L0_attn_b_setup()

    def _L0_ffn_setup():
        import jax, jax.numpy as jnp
        import numpy as np

        def sparsemax(z):
            E = z.shape[-1]
            z_sorted = -jnp.sort(-z, axis=-1)
            z_cum = jnp.cumsum(z_sorted, axis=-1)
            k = jnp.arange(1, E + 1, dtype=z.dtype)
            support = 1.0 + k * z_sorted > z_cum
            k_z = jnp.sum(support, axis=-1, keepdims=True)
            tau_sum = jnp.take_along_axis(z_cum, k_z.astype(jnp.int32) - 1, axis=-1)
            tau = (tau_sum - 1.0) / k_z.astype(z.dtype)
            return jnp.maximum(z - tau, 0.0)
        key = jax.random.key(seed)
        ks = jax.random.split(key, 6)
        B, S, D_IN, D_OUT, E, R = (8, 512, 1024, 1024, 8, 16)
        x = jax.random.normal(ks[0], (B, S, D_IN), dtype=jnp.float32)
        W_base = jax.random.normal(ks[1], (D_OUT, D_IN), dtype=jnp.float32) * D_IN ** (-0.5)
        b_base = jax.random.normal(ks[2], (D_OUT,), dtype=jnp.float32) * 0.01
        W_router = jax.random.normal(ks[3], (E, D_IN), dtype=jnp.float32) * D_IN ** (-0.5)
        b_router = jnp.zeros((E,), dtype=jnp.float32)
        lora_A = jax.random.normal(ks[4], (E, D_IN, R), dtype=jnp.float32) * D_IN ** (-0.5)
        lora_B = jnp.zeros((E, R, D_OUT), dtype=jnp.float32)
        return {'x': x, 'W_base': W_base, 'b_base': b_base, 'W_router': W_router, 'b_router': b_router, 'lora_A': lora_A, 'lora_B': lora_B}
    _L0_ffn_in = _L0_ffn_setup()
    _d = {'L0_attn_a_x': _L0_attn_a_in['x'], 'L0_attn_a_w_attn': _L0_attn_a_in['w_attn'], 'L0_attn_a_w_proj': _L0_attn_a_in['w_proj'], 'L0_attn_a_adapter_wte': _L0_attn_a_in['adapter_wte'], 'L0_attn_a_gating': _L0_attn_a_in['gating'], 'L0_attn_b_Wqk_w': _L0_attn_b_in['Wqk_w'], 'L0_attn_b_Wqk_b': _L0_attn_b_in['Wqk_b'], 'L0_attn_b_Wv_w': _L0_attn_b_in['Wv_w'], 'L0_attn_b_Wv_b': _L0_attn_b_in['Wv_b'], 'L0_attn_b_Wo_w': _L0_attn_b_in['Wo_w'], 'L0_attn_b_Wo_b': _L0_attn_b_in['Wo_b'], 'L0_ffn_W_base': _L0_ffn_in['W_base'], 'L0_ffn_b_base': _L0_ffn_in['b_base'], 'L0_ffn_W_router': _L0_ffn_in['W_router'], 'L0_ffn_b_router': _L0_ffn_in['b_router'], 'L0_ffn_lora_A': _L0_ffn_in['lora_A'], 'L0_ffn_lora_B': _L0_ffn_in['lora_B']}
    _x0 = _d['L0_attn_a_x']
    _d['L0_attn_a_x'] = jax.random.normal(jax.random.fold_in(jax.random.key(seed), 1), (2, 1024, 1024), dtype=_x0.dtype)
    del _x0
    return _d

def reference(L0_attn_a_x, L0_attn_a_w_attn, L0_attn_a_w_proj, L0_attn_a_adapter_wte, L0_attn_a_gating, L0_attn_b_Wqk_w, L0_attn_b_Wqk_b, L0_attn_b_Wv_w, L0_attn_b_Wv_b, L0_attn_b_Wo_w, L0_attn_b_Wo_b, L0_ffn_W_base, L0_ffn_b_base, L0_ffn_W_router, L0_ffn_b_router, L0_ffn_lora_A, L0_ffn_lora_B):

    def _L0_attn_a_ref(x, w_attn, w_proj, adapter_wte, gating):
        import jax, jax.numpy as jnp
        import numpy as np
        N_HEAD = 32
        ROPE_BASE = 10000.0

        def _rope_cos_sin(T, n_elem, dtype):
            theta = 1.0 / ROPE_BASE ** (jnp.arange(0, n_elem, 2, dtype=dtype) / n_elem)
            seq_idx = jnp.arange(T, dtype=dtype)
            idx_theta = jnp.outer(seq_idx, theta)
            idx_theta2 = jnp.concatenate([idx_theta, idx_theta], axis=-1)
            return (jnp.cos(idx_theta2), jnp.sin(idx_theta2))

        def _apply_rope(x, cos, sin):
            d2 = x.shape[-1] // 2
            rot = jnp.concatenate([-x[..., d2:], x[..., :d2]], axis=-1)
            return x * cos + rot * sin
        B, T, C = x.shape
        H = N_HEAD
        hd = C // H
        qkv = jnp.einsum('btc,oc->bto', x, w_attn)
        q, k, v = jnp.split(qkv, 3, axis=-1)
        q = q.reshape(B, T, H, hd).transpose(0, 2, 1, 3)
        k = k.reshape(B, T, H, hd).transpose(0, 2, 1, 3)
        v = v.reshape(B, T, H, hd).transpose(0, 2, 1, 3)
        cos, sin = _rope_cos_sin(T, hd, x.dtype)
        q = _apply_rope(q, cos, sin)
        k = _apply_rope(k, cos, sin)
        scores = jnp.einsum('bhqd,bhkd->bhqk', q, k) / jnp.sqrt(jnp.asarray(hd, x.dtype))
        causal = jnp.tril(jnp.ones((T, T), bool))
        scores = jnp.where(causal, scores, jnp.asarray(-jnp.inf, x.dtype))
        attn = jax.nn.softmax(scores, axis=-1)
        y = jnp.einsum('bhqk,bhkd->bhqd', attn, v)
        aT = adapter_wte.shape[0]
        prefix = adapter_wte[None]
        aqkv = jnp.einsum('btc,oc->bto', prefix, w_attn)
        _, ak, av = jnp.split(aqkv, 3, axis=-1)
        ak = ak.reshape(1, aT, H, hd).transpose(0, 2, 1, 3)
        av = av.reshape(1, aT, H, hd).transpose(0, 2, 1, 3)
        ascores = jnp.einsum('bhqd,xhkd->bhqk', q, ak) / jnp.sqrt(jnp.asarray(C, x.dtype))
        ascores = gating[0] * jax.nn.softmax(ascores.astype(jnp.float32), axis=-1).astype(q.dtype)
        y = y + jnp.einsum('bhqk,xhkd->bhqd', ascores, av)
        y = y.transpose(0, 2, 1, 3).reshape(B, T, C)
        return jnp.einsum('btc,oc->bto', y, w_proj)

    def _L0_attn_b_ref(x, Wqk_w, Wqk_b, Wv_w, Wv_b, Wo_w, Wo_b):
        import jax, jax.numpy as jnp
        import numpy as np
        B, N, D = (8, 256, 1024)
        H = 8
        HEAD_DIM = D // H
        E = HEAD_DIM // H
        b, n, _ = x.shape
        qk = (x @ Wqk_w.T + Wqk_b).reshape(b, n, H, E, 2)
        q = jnp.transpose(qk[..., 0], (0, 2, 1, 3))
        k = jnp.transpose(qk[..., 1], (0, 2, 1, 3))
        v = (x @ Wv_w.T + Wv_b).reshape(b, n, H, E)
        v = jnp.transpose(v, (0, 2, 1, 3))
        scores = jnp.einsum('bhqd,bhkd->bhqk', q, k)
        attn = jax.nn.softmax(scores, axis=-1) / jnp.asarray(HEAD_DIM ** 0.5, x.dtype)
        out = jnp.einsum('bhsl,bhlv->bhsv', attn, v)
        out = jnp.transpose(out, (0, 2, 1, 3)).reshape(b, n, H * E)
        return out @ Wo_w.T + Wo_b

    def _L0_ffn_ref(x, W_base, b_base, W_router, b_router, lora_A, lora_B):
        import jax, jax.numpy as jnp
        import numpy as np

        def sparsemax(z):
            E = z.shape[-1]
            z_sorted = -jnp.sort(-z, axis=-1)
            z_cum = jnp.cumsum(z_sorted, axis=-1)
            k = jnp.arange(1, E + 1, dtype=z.dtype)
            support = 1.0 + k * z_sorted > z_cum
            k_z = jnp.sum(support, axis=-1, keepdims=True)
            tau_sum = jnp.take_along_axis(z_cum, k_z.astype(jnp.int32) - 1, axis=-1)
            tau = (tau_sum - 1.0) / k_z.astype(z.dtype)
            return jnp.maximum(z - tau, 0.0)
        base_out = jnp.einsum('bsd,od->bso', x, W_base) + b_base
        logits = jnp.einsum('bsd,ed->bse', x, W_router) + b_router
        weights = sparsemax(logits)
        h = jnp.einsum('bsd,edr->bser', x, lora_A)
        expert_out = jnp.einsum('bser,bse,ero->bso', h, weights, lora_B)
        return base_out + expert_out
    x = L0_attn_a_x
    x = x + _L0_attn_a_ref(_layernorm(x, axis=-1), L0_attn_a_w_attn, L0_attn_a_w_proj, L0_attn_a_adapter_wte, L0_attn_a_gating)
    x = x + _L0_ffn_ref(_layernorm(x, axis=-1), L0_ffn_W_base, L0_ffn_b_base, L0_ffn_W_router, L0_ffn_b_router, L0_ffn_lora_A, L0_ffn_lora_B)
    x = x + _L0_attn_b_ref(_layernorm(x, axis=-1), L0_attn_b_Wqk_w, L0_attn_b_Wqk_b, L0_attn_b_Wv_w, L0_attn_b_Wv_b, L0_attn_b_Wo_w, L0_attn_b_Wo_b)
    x = x + _L0_ffn_ref(_layernorm(x, axis=-1), L0_ffn_W_base, L0_ffn_b_base, L0_ffn_W_router, L0_ffn_b_router, L0_ffn_lora_A, L0_ffn_lora_B)
    return x

_drawn_inputs = setup_inputs


def setup_inputs(seed=0):
    import zlib

    import numpy as np

    out = dict(_drawn_inputs(seed))
    spreads = {'L0_attn_b_Wqk_b': (0.0, 0.8),
     'L0_attn_b_Wv_b': (0.0, 0.8),
     'L0_attn_b_Wo_b': (0.0, 0.1),
     'L0_ffn_b_router': (0.0, 0.441),
     'L0_ffn_lora_B': (0.0, 0.1)}
    factors = {'L0_attn_b_Wqk_w': 8.0,
     'L0_attn_b_Wv_w': 8.0,
     'L0_attn_b_Wo_w': 8.0,
     'L0_ffn_b_base': 6.499}
    for name, (base, spread) in spreads.items():
        noise = np.random.default_rng([zlib.crc32(name.encode()), seed]).standard_normal(out[name].shape)
        drawn = base * np.exp(spread * noise) if base else spread * noise
        out[name] = jnp.asarray(drawn.astype(out[name].dtype))
    for name, factor in factors.items():
        out[name] = (out[name] * factor).astype(out[name].dtype)
    return out
```

```python
from contextlib import ExitStack

import concourse.bass as bass
from concourse import mybir

F32 = mybir.dt.float32
F32R = mybir.dt.float32r
BF16 = mybir.dt.bfloat16
ALU = mybir.AluOpType
ACT = mybir.ActivationFunctionType
AX = mybir.AxisListType

P = 128
B = 2
T = 1024
C = 1024
TT = T // P
CC = C // P
HALF = 512
NH, HD = 32, 32
G = NH * HD // P
AK = 10
NE, R = 8, 16
NHB, HDB = 8, 16
GB = NHB // 4
EPS = 1e-5
MASKED = -1e30
SCALE_A = HD ** -0.5
SCALE_ADAPTER = C ** -0.5
SCALE_B_OUT = (NHB * HDB) ** -0.5
LAG = 3
RING = 4
AH = 3
PHASES = 11
PRODUCTS = ((0, 0), (0, 1), (1, 0))


class Heads:

    def __init__(self, causal):
        if causal:
            order = ((0, 1), (1, 1), (7, 1), (0, 0), (2, 1), (6, 1), (3, 1), (2, 0), (5, 1), (4, 1), (1, 0), (3, 0))
        else:
            order = ((0, 1), *((t + h, h) for t in range(TT - 1) for h in (1, 0)), (TT - 1, 0))
        self.main = [(t, max(t * P, h * HALF) if causal else h * HALF, (h + 1) * HALF) for t, h in order]
        if causal:
            order = ((2, 0), (3, 0), (4, 0), (0, 0), (5, 0), (6, 0), (6, 1), (1, 0), (7, 0), (5, 1), (4, 1), (7, 1))
            self.max = [(t, h * HALF, min((h + 1) * HALF, (t + 1) * P), t if h == 0 else 4 + t) for t, h in order]
        else:
            self.max = [(t, h * HALF, (h + 1) * HALF, t + TT * h) for t in range(TT) for h in range(2)]
        self.causal = causal
        self.n = len(self.main)
        self.items = self.n + 1
        self.slots = 4 * self.n
        self.groups = G if causal else GB
        self.heads = 4 * self.groups
        self.pair = 1 if causal else 2
        self.lead = self.n + 6
        self.scale = SCALE_A if causal else 1.0
        self.last = [max(i for i, c in enumerate(self.main) if c[1] // HALF == h) for h in range(2)]


HA, HB = Heads(True), Heads(False)


def build_program(nc, x_in, w_qkv, w_proj, adapter, gating, rope_cos, rope_sin, w_base, b_base, w_lora_in,
                  b_router, w_lora_out, wb_qkv, bb_qkv, wb_out, bb_out, out):
    with ExitStack() as ctx:
        top = nc.sbuf_usable_end

        class Region:

            def __init__(self, start):
                self.at = start

            def __call__(self, name, shape, dtype):
                n = 2 if dtype == BF16 else 4
                for s in shape[1:]:
                    n *= s
                t = nc.alloc_sbuf_tensor_at(name, shape, dtype, offset=self.at)
                self.at += (n + 31) // 32 * 32
                assert self.at <= top, (name, self.at, top)
                return t

            def split(self, name, shape):
                return [self(f"{name}_{s}", shape, F32R) for s in ("hi", "lo")]

        def sem(name):
            return ctx.enter_context(nc.semaphore(name))

        def scratch(name, shape):
            return nc.dram_tensor(name, shape, F32, kind="Internal").ap()

        def raw(ap):
            return ap.bitcast(F32)

        keep = Region((nc.sbuf_base + 31) // 32 * 32)
        ident = keep("ident", [P, P], F32)
        ident16 = keep("ident16", [P, P], BF16)
        mask_main = keep("mask_main", [P, P], BF16)
        mask_max = keep("mask_max", [P, P], BF16)
        ak_all = keep("ak_all", [P, G, 2, 4 * AK], F32R)
        gate = keep("gate", [P, 1], F32)
        b_rout = keep("b_rout", [NE, 1], F32)
        b_qkv = keep("b_qkv", [P, 3], F32)
        xt = keep.split("xt", [P, CC, T])
        dense = Region(keep.at)
        X = dense("X", [P, TT, C], F32)
        over_w = dense.at
        w = dense.split("w", [P, CC, HALF])
        w_raw = dense("w_raw", [P, CC, HALF], F32)
        lb = dense.split("lb", [P, C])
        lb_raw = dense("lb_raw", [P, C], F32)
        la = dense.split("la", [P, CC, P + NE])
        la_raw = dense("la_raw", [P, CC, P + NE], F32)
        h_sb = dense("h_sb", [P, T], F32)
        hw = dense.split("hw", [P, T])
        bias_row = dense("bias_row", [P, C], F32)
        sp_buf = dense("sp_buf", [P, 8, TT * NE], F32)
        pairs = dense("pairs", [P, 2, TT, NE, NE], F32)
        logit_t = dense("logit_t", [NE, T], F32)
        early = Region(over_w + 3 * CC * HALF * 4)
        at_raw = early("at_raw", [P, CC, AK], F32)
        at = early.split("at", [P, CC, AK])
        akv = early("akv", [AK, 2, C], F32)
        avs = early.split("avs", [AK, C])
        zeros = early("zeros", [P, G * P], F32)
        norm = Region(over_w)
        xn = norm("xn", [P, 2, C], F32)
        stats = norm("stats", [P, TT, 2, 6], F32)
        mv = norm("mv", [P, TT, 2], F32)
        rs = norm("rs", [P, 4, TT], F32)
        adp = Region(over_w)
        asc = adp("asc", [P, AH, T], F32)
        av = adp.split("av", [P, G, P])
        pa = adp.split("pa", [P, AH, T])
        a_e = adp("a_e", [P, 2, NH, AK], F32)
        a_s = adp("a_s", [P, 2, 4, NH], F32)
        yt_in_sb = adp("yt_in_sb", [P, 2, T], F32)
        y_sum = adp("y_sum", [P, 2, T], F32)
        att = Region(keep.at)
        cos = att("cos", [P, T], F32)
        sin = att("sin", [P, T], F32)
        wq = [att.split(f"wq{p}", [P, CC, P]) for p in range(3)]
        wq_raw = att("wq_raw", [P, CC, P], F32)
        qst = att("qst", [98, 4, T], F32R)
        kst = att("kst", [98, 4, T], F32R)
        prob = att("prob", [P, 3, HALF], F32)
        phl = att.split("prob", [P, 3, HALF])
        vst = att("vst", [P, TT, 4, 96], F32R)
        src = [att.split(f"src{p}", [P, T]) for p in "qk"]
        turn = att("turn", [P, T], F32)
        rot = att("rot", [P, T], F32)
        vt = att("vt", [P, T], F32)
        y = att("y", [P, T], F32)
        den = att("den", [P, T], F32)
        rden = vt
        y_tmp = att("y_tmp", [32, HALF], F32)
        ak_cur = att("ak_cur", [P, 2, 4 * AK], F32R)
        m_part = att("m_part", [P, 2, 16], F32)
        m_row = att.split("m_row", [TT, 2, P])
        d_col = att("d_col", [P, 32], F32)
        r_col = att("r_col", [P, 32], F32)
        over = Region(keep.at)
        vsb = over("vsb", [P, TT, NHB, 96], F32R)
        assert over.at <= keep.at + 2 * T * 4 + 2 * CC * P * 4 + 2 * CC * P * 4, "vsb must end before wq2"

        banks = ctx.enter_context(nc.psum_tensor("banks", [P, 8, HALF], F32))
        AUX = banks[:, 0:2, :].rearrange("p b n -> p (b n)")

        yt_dram = scratch("yt_dram", [B, G, P, T])
        asc_dram = scratch("asc_dram", [B, G * 4 * AK, T])
        rd_dram = scratch("rd_dram", [B, G, 4, T])
        av_dram = [scratch(f"av_dram_{s}", [P, G, P]) for s in ("hi", "lo")]
        x_dram = scratch("x_dram", [B, P, TT, C])

        phase_done = sem("phase_done")
        setup_done = sem("setup_done")
        passed = sem("passed")
        c_set = sem("c_set")
        c_in, at_in = sem("c_in"), sem("at_in")
        sw_in, sw_hi, sw_lo = sem("sw_in"), sem("sw_hi"), sem("sw_lo")
        s_mm, s_ev, s_tr, s_av = sem("s_mm"), sem("s_ev"), sem("s_tr"), sem("s_av")
        s_zero, s_avd = sem("s_zero"), sem("s_avd")
        x_ld = [sem(f"x_ld{t}") for t in range(4)]
        ln_dve, ln_root, ln_xn = sem("ln_dve"), sem("ln_root"), sem("ln_xn")
        ln_tr, ln_hi, ln_lo = sem("ln_tr"), sem("ln_hi"), sem("ln_lo")
        x_sv = sem("x_sv")
        LN_DVE = 8
        class AttentionSems:
            def __init__(self, n):
                self.max_ready, self.max_used = sem(f"{n}max_ready"), sem(f"{n}max_used")
                self.m_ready, self.mh_done = sem(f"{n}m_ready"), sem(f"{n}mh_done")
                self.aug_in = [sem(f"{n}aug_in{i}") for i in range(2)]
                self.stk_in = [sem(f"{n}stk_in{i}") for i in range(4)]
                self.st_ready, self.exp_done = sem(f"{n}st_ready"), sem(f"{n}exp_done")
                self.hi_done, self.lo_done = sem(f"{n}hi_done"), sem(f"{n}lo_done")
                self.pv_done, self.y_tmp, self.y_done = sem(f"{n}pv_done"), sem(f"{n}y_tmp"), sem(f"{n}y_done")
                self.aux, self.w_in = sem(f"{n}aux"), sem(f"{n}w_in")
                self.w_hi, self.w_lo = sem(f"{n}w_hi"), sem(f"{n}w_lo")
                self.proj_done, self.raw_in = sem(f"{n}proj_done"), sem(f"{n}raw_in")
                self.src_hi, self.src_lo = sem(f"{n}src_hi"), sem(f"{n}src_lo")
                self.v_hi, self.v_lo = sem(f"{n}v_hi"), sem(f"{n}v_lo")
                self.fill = sem(f"{n}fill")
        a_vt_in = sem("a_vt_in")
        SA, SB = AttentionSems("a_"), AttentionSems("b_")
        tab_in = sem("tab_in")
        turned, sin_done, cos_done, rope_done = sem("turned"), sem("sin_done"), sem("cos_done"), sem("rope_done")
        asc_ready, asc_in, asc_out, ak_in = sem("asc_ready"), sem("asc_in"), sem("asc_out"), sem("ak_in")
        den_in, r_done, rd_out, rden_in = sem("den_in"), sem("r_done"), sem("rd_out"), sem("rden_in")
        y_mul, yt_out = sem("y_mul"), sem("yt_out")
        by_r, by_y, by_hi, by_lo = sem("by_r"), sem("by_y"), sem("by_hi"), sem("by_lo")
        ad_in, av_in = sem("ad_in"), sem("av_in")
        ad_tr, ad_mx, ad_sub, ad_exp, ad_sum = sem("ad_tr"), sem("ad_mx"), sem("ad_sub"), sem("ad_exp"), sem("ad_sum")
        ad_rec, ad_gate, ad_p = sem("ad_rec"), sem("ad_gate"), sem("ad_p")
        ad_pt, ad_phi, ad_plo = sem("ad_pt"), sem("ad_phi"), sem("ad_plo")
        ad_yin = [sem(f"ad_yin{i}") for i in range(2)]
        ad_mm, ad_y, ad_hi, ad_lo = sem("ad_mm"), sem("ad_y"), sem("ad_hi"), sem("ad_lo")

        class DenseSems:
            def __init__(self, n, parts):
                self.w_in = [sem(f"{n}w_in{i}") for i in range(parts)]
                self.w_hi, self.w_lo = sem(f"{n}w_hi"), sem(f"{n}w_lo")
                self.tile, self.added = sem(f"{n}tile"), sem(f"{n}added")
        w_free = sem("w_free")
        SD, SO = DenseSems("d_", 4), DenseSems("o_", 1)
        px_in, ox_in, o_bias = sem("px_in"), sem("ox_in"), sem("o_bias")
        f_in = [sem(f"f_in{i}") for i in range(3)]
        f_hi, f_lo, f_h, f_hsb, f_lg = sem("f_hi"), sem("f_lo"), sem("f_h"), sem("f_hsb"), sem("f_lg")
        f_zt, f_dve, f_wt, f_hw, f_hwhi, f_hwlo = (sem(n) for n in ("f_zt", "f_dve", "f_wt", "f_hw", "f_hwhi", "f_hwlo"))
        f_bias = sem("f_bias")
        F_DVE = 14
        out_st = sem("out_st")

        def settle(eng):
            eng.sem_inc(passed, 1)

        def phase_end(eng, b, ph):
            settle(eng)
            eng.drain().then_inc(phase_done, 1)
            eng.wait_ge(phase_done, 5 * PHASES * b + 5 * (ph + 1))
            settle(eng)

        def setup_end(eng):
            eng.drain().then_inc(setup_done, 1)
            eng.wait_ge(setup_done, 5)

        def sp_norm(sp, b, n):
            if n == 0:
                for t in range(4):
                    sp.dma_start(X[:, 2 * t:2 * t + 2, :],
                                 x_in[b, 2 * t * P:2 * (t + 1) * P, :].rearrange("(t p) c -> p t c", p=P)).then_inc(x_ld[t], 16)
            if n == 2:
                sp.dma_start(x_dram[b], X[:]).then_inc(x_sv, 16)
                sp.wait_ge(x_sv, 16 * b + 16)

        def dve_norm(dve, b, n):
            i = 4 * b + n
            for t in range(TT):
                if n == 0:
                    dve.wait_ge(x_ld[t // 2], 16 * b + 16)
                for h in range(2):
                    last = dve.bn_stats(stats[:, t, h, :], X[:, t, h * HALF:(h + 1) * HALF])
            last.then_inc(ln_dve, 1)
            dve.wait_ge(ln_dve, LN_DVE * i + 1)
            settle(dve)
            for t in range(TT):
                last = dve.bn_aggr(mv[:, t, :], stats[:, t, :, :].rearrange("p h s -> p (h s)"))
            last.then_inc(ln_dve, 1)
            dve.wait_ge(ln_dve, LN_DVE * i + 2)
            var, root, inv, tmp = (rs[:, j, :] for j in range(4))
            dve.tensor_scalar(var, mv[:, :, 1], EPS, None, ALU.add).then_inc(ln_dve, 1)
            dve.wait_ge(ln_root, i + 1)
            dve.reciprocal(inv, root).then_inc(ln_dve, 1)
            dve.wait_ge(ln_dve, LN_DVE * i + 4)
            dve.tensor_tensor(tmp, inv, inv, ALU.mult).then_inc(ln_dve, 1)
            dve.wait_ge(ln_dve, LN_DVE * i + 5)
            dve.tensor_tensor(tmp, tmp, var, ALU.mult).then_inc(ln_dve, 1)
            dve.wait_ge(ln_dve, LN_DVE * i + 6)
            dve.tensor_scalar(tmp, tmp, -0.5, 1.5, ALU.mult, ALU.add).then_inc(ln_dve, 1)
            dve.wait_ge(ln_dve, LN_DVE * i + 7)
            dve.tensor_tensor(inv, inv, tmp, ALU.mult).then_inc(ln_dve, 1)
            dve.wait_ge(ln_dve, LN_DVE * i + 8)
            for t in range(TT + 1):
                if t < TT:
                    if t >= 2:
                        dve.wait_ge(ln_tr, TT * i + t - 1)
                    dve.tensor_scalar(xn[:, t % 2, :], X[:, t, :], mv[:, t, 0:1], inv[:, t:t + 1],
                                      ALU.subtract, ALU.mult).then_inc(ln_xn, 1)
                if t >= 1:
                    s = t - 1
                    dve.wait_ge(ln_hi, TT * i + s + 1)
                    dve.tensor_tensor(xt[1][:, :, s * P:(s + 1) * P], norm_bank(s),
                                      raw(xt[0][:, :, s * P:(s + 1) * P]), ALU.subtract).then_inc(ln_lo, 1)

        def norm_bank(t):
            q = 2 * (t % 4)
            return banks[:, q:q + 2, :].rearrange("p b (c t) -> p (b c) t", t=P)

        def act_norm(act, b, n):
            i = 4 * b + n
            act.wait_ge(ln_dve, LN_DVE * i + 3)
            act.activation(rs[:, 1, :], rs[:, 0, :], ACT.Sqrt).then_inc(ln_root, 1)
            for t in range(TT):
                act.wait_ge(ln_tr, TT * i + t + 1)
                act.copy(xt[0][:, :, t * P:(t + 1) * P], norm_bank(t)).then_inc(ln_hi, 1)

        def pe_norm(pe, b, n):
            i = 4 * b + n
            for t in range(TT):
                pe.wait_ge(ln_xn, TT * i + t + 1)
                if t >= 4:
                    pe.wait_ge(ln_lo, TT * i + t - 3)
                for c in range(CC):
                    last = pe.transpose(norm_bank(t)[:, c, :], xn[:, t % 2, c * P:(c + 1) * P], ident[:])
                last.then_inc(ln_tr, 1)

        def main_bank(k):
            return banks[:, 4 + k % 2, :]

        def max_index(H, j, i, first):
            if i == 0:
                return 0 if first and j == 0 else H.items * j - 1
            return H.items * j + i

        def turn_index(H, j, last):
            return H.items * j - (1 if last and j == 4 else 0)

        def max_bank(i):
            return banks[:, 2 + i % 2, :]

        def pe_max(pe, H, S, b, g, v, first=False, last=False):
            j, i = divmod(v, H.n)
            if last and v > H.slots + 1:
                return
            if i == 1 and not (first and v == 1):
                n = turn_index(H, j, last)
                pe.wait_ge(S.m_ready, H.heads * b + 4 * g + j)
                pe.wait_ge(S.max_used, H.items * (H.heads * b + 4 * g) + n - 1)
                pe.transpose(max_bank(n)[0:TT, 0:P], m_part[:, (j - 1) % 2, 0:TT], ident[:]).then_inc(S.max_ready, 1)
            if last and j >= 4:
                return
            n = max_index(H, j, i, first)
            if i == 0:
                pe.wait_ge(S.stk_in[j % 4], 96 * (H.groups * b + g + j // 4 + 1))
            if not (first and n < 2):
                pe.wait_ge(S.max_used, H.items * (H.heads * b + 4 * g) + n - 1)
            qt, k0, k1, _ = H.max[i]
            diag = H.causal and k1 == (qt + 1) * P
            bank = max_bank(n)
            mm = pe.matmul(bank[:, 0:k1 - k0], qst[0:96, j % 4, qt * P:(qt + 1) * P], kst[0:96, j % 4, k0:k1],
                           start=True, stop=True)
            if diag:
                mm = pe.matmul(bank[:, k1 - k0 - P:k1 - k0], ident16[:], mask_max[:], start=False, stop=True,
                               skip_group_check=True)
            mm.then_inc(S.max_ready, 1)

        def dve_max(dve, H, S, b, g, v, first=False, last=False):
            j, i = divmod(v, H.n)
            if last and v > H.slots + 1:
                return
            hb = H.heads * b + 4 * g
            if i == 1 and not (first and v == 1):
                n, h = turn_index(H, j, last), j - 1
                dve.wait_ge(S.max_ready, H.items * hb + n + 1)
                if not (first and h < 2):
                    dve.wait_ge(S.aug_in[h % 2], 32 * (H.heads // 2 * b + 2 * g + h // 2))
                bank = max_bank(n)[0:TT, 0:P]
                dve.tensor_scalar(m_row[0][:, h % 2, :], bank, -1.0, None, ALU.mult).then_inc(S.mh_done, 1)
                dve.wait_ge(S.mh_done, hb + h + 1)
                dve.scalar_tensor_tensor(out=m_row[1][:, h % 2, :], in0=bank, scalar=-1.0,
                                         in1=raw(m_row[0][:, h % 2, :]), op0=ALU.mult,
                                         op1=ALU.subtract).then_inc(S.max_used, 1)
            if last and j >= 4:
                return
            n = max_index(H, j, i, first)
            _, k0, k1, col = H.max[i]
            dve.wait_ge(S.max_ready, H.items * hb + n + 1)
            dve.tensor_reduce(m_part[:, j % 2, col:col + 1], max_bank(n)[:, 0:k1 - k0], AX.X,
                              ALU.max).then_inc(S.max_used, 1)
            if i == H.n - 1:
                lo, n2 = (4, 4) if H.causal else (0, TT)
                dve.wait_ge(S.max_used, H.items * hb + n + 1)
                dve.tensor_tensor(m_part[:, j % 2, lo:lo + n2], m_part[:, j % 2, lo:lo + n2],
                                  m_part[:, j % 2, 8:8 + n2], ALU.max).then_inc(S.m_ready, 1)

        def sp_max_rows(sp, H, S, b, g, h, last=False):
            sp.wait_ge(S.max_used, H.items * (H.heads * b + 4 * g) + turn_index(H, h + 1, last) + 1)
            settle(sp)
            for s in range(2):
                sp.dma_start(raw(qst[96 + s:97 + s, h % 4, :]), raw(m_row[s][:, h % 2, :])).then_inc(S.aug_in[h % 2], 16)

        def sp_stack(sp, H, S, b, g, h, first=False):
            width = HD if H.causal else HDB
            at_row = h * width if H.causal else (4 * g + h) * width
            rows = slice(at_row, at_row + width)
            if H.causal:
                sp.wait_ge(S.src_lo, 2 * H.groups * b + 2 * g + 2)
            else:
                sp.wait_ge(S.src_lo, 2 * b + 2)
            if not first:
                settle(sp)
                sp.wait_ge(S.pv_done, H.slots * (H.groups * b + g - 1) + H.n * (h + 1))
            settle(sp)
            for stack, part, order in ((qst, 0, (0, 1, 0)), (kst, 1, (0, 0, 1))):
                for i, s in enumerate(order):
                    sp.dma_start(raw(stack[32 * i:32 * i + width, h, :]),
                                 raw(src[part][s][rows, :])).then_inc(S.stk_in[h], 16)

        def pe_scores(pe, H, S, b, g, k, first=False):
            j, c = divmod(k, H.n)
            u = H.slots * (H.groups * b + g) + k
            if c == 0:
                pe.wait_ge(S.aug_in[j % 2], 32 * (H.heads // 2 * b + 2 * g + j // 2 + 1))
            if not (first and k < 2):
                pe.wait_ge(S.exp_done, u - 1)
            kt, q0, q1 = H.main[c]
            diag = H.causal and q0 == kt * P
            bank = main_bank(k)
            mm = pe.matmul(bank[:, 0:q1 - q0], kst[:, j % 4, kt * P:(kt + 1) * P], qst[:, j % 4, q0:q1],
                           start=True, stop=True)
            if diag:
                mm = pe.matmul(bank[:, 0:P], ident16[:], mask_main[:], start=False, stop=True, skip_group_check=True)
            mm.then_inc(S.st_ready, 1)

        def act_exp(act, H, S, b, g, k, ring, first=False):
            kt, q0, q1 = H.main[k % H.n]
            u = H.slots * (H.groups * b + g) + k
            act.wait_ge(S.st_ready, u + 1)
            if not (first and k < 3):
                act.wait_ge(S.lo_done, u - 2)
            act.activation(prob[:, (ring + k) % 3, 0:q1 - q0], main_bank(k)[:, 0:q1 - q0], ACT.Exp,
                           scale=H.scale).then_inc(S.exp_done, 1)

        def act_hi(act, H, S, b, g, k, ring, first=False):
            kt, q0, q1 = H.main[k % H.n]
            u = H.slots * (H.groups * b + g) + k
            act.wait_ge(S.exp_done, u + 1)
            if not (first and k < 3):
                act.wait_ge(S.pv_done, u - 2)
            act.copy(phl[0][:, (ring + k) % 3, 0:q1 - q0], prob[:, (ring + k) % 3, 0:q1 - q0]).then_inc(S.hi_done, 1)

        def dve_lo(dve, H, S, b, g, k, ring):
            kt, q0, q1 = H.main[k % H.n]
            u = H.slots * (H.groups * b + g) + k
            dve.wait_ge(S.hi_done, u + 1)
            dve.tensor_tensor(phl[1][:, (ring + k) % 3, 0:q1 - q0], prob[:, (ring + k) % 3, 0:q1 - q0],
                              raw(phl[0][:, (ring + k) % 3, 0:q1 - q0]), ALU.subtract).then_inc(S.lo_done, 1)

        def pe_pv(pe, H, S, b, g, k, ring, first=False):
            if k < 0:
                g, k, ring = g - 1, k + H.slots, ring - H.slots
            j, c = divmod(k, H.n)
            kt, q0, q1 = H.main[c]
            half = q0 // HALF
            u = H.slots * (H.groups * b + g) + k
            pe.wait_ge(S.lo_done, u + 1)
            if H.causal:
                v_stat = vst[:, kt, j, :]
                if c == 0 and j in (0, 3):
                    pe.wait_ge(S.v_lo, 2 * (H.groups * b + g) + (1 if j == 0 else 2))
            else:
                v_stat = vsb[:, kt, 4 * g + j, :]
            if kt == 0 and j % H.pair == 0 and not (first and j == 0):
                pe.wait_ge(S.y_done, y_index(H, b, g, j, half) - 1)
            for s in range(2):
                mm = pe.matmul(banks[0:96, 6 + half, q0 - half * HALF:q1 - half * HALF], v_stat,
                               phl[s][:, (ring + k) % 3, 0:q1 - q0], start=(kt == 0 and s == 0 and j % H.pair == 0),
                               stop=True,
                               skip_group_check=True)
            mm.then_inc(S.pv_done, 1)

        def y_index(H, b, g, j, half):
            per = H.heads // H.pair
            return 2 * (per * b + 4 // H.pair * g + j // H.pair) + 1 - half

        def act_y(act, H, S, b, g, j, half, first=False):
            n = y_index(H, b, g, j, half)
            act.wait_ge(S.pv_done, H.slots * (H.groups * b + g) + H.n * j + H.last[half] + 1)
            if not (first and j // H.pair == 0 and half == 1):
                act.wait_ge(S.y_done, n)
            row = 32 * (j % 4) if H.causal else 32 * ((4 * g + j) // 2)
            act.copy(y_tmp[:], banks[32:64, 6 + half, :])
            act.copy(den[row:row + 32, half * HALF:(half + 1) * HALF], banks[64:96, 6 + half, :]).then_inc(S.y_tmp, 1)

        def dve_y(dve, H, S, b, g, j, half):
            n = y_index(H, b, g, j, half)
            dve.wait_ge(S.y_tmp, n + 1)
            row = 32 * (j % 4) if H.causal else 32 * ((4 * g + j) // 2)
            dve.tensor_tensor(y[row:row + 32, half * HALF:(half + 1) * HALF], banks[0:32, 6 + half, :], y_tmp[:],
                              ALU.add).then_inc(S.y_done, 1)

        def pe_project(part):
            for c in range(CC):
                for a, x in PRODUCTS:
                    for h in range(2):
                        yield (AUX[:, h * HALF:(h + 1) * HALF], wq[part][a][:, c, :],
                               xt[x][:, c, h * HALF:(h + 1) * HALF], c == 0 and (a, x) == (0, 0),
                               c == CC - 1 and (a, x) == PRODUCTS[-1])

        Q_SLOTS, K_SLOTS, V_SLOTS = range(2, 10), range(11, 19), range(21, 29)
        COPY_OUT = (10, 19, 29, 37)
        ROPE_DVE, ROPE_HI = (12, 21), (15, 24)
        ADAPTER, TURN_V = 36, 40
        Y_CHUNK = ((1, 0), (0, 2))
        RECIPROCALS = 5
        WEIGHTS, STACKS = (0, 32, 37), (26, 27, 38, 1)
        DENOMINATORS, STORE, ADAPTER_STORE = 4, 12, 39
        PROJECTION = 6 * CC

        def pe_a_part(pe, b, g, p, first=False):
            pe.wait_ge(SA.w_lo, 3 * G * b + 3 * g + p + 1)
            if p == 0:
                if not first:
                    pe.wait_ge(SA.v_lo, 2 * (G * b + g))
            else:
                pe.wait_ge(SA.raw_in, 2 * G * b + 2 * g + p)

        def pe_a_adapter(pe, b, g):
            pe.wait_ge(ak_in, G * b + g + 1)
            pe.wait_ge(SA.src_lo, 2 * G * b + 2 * g + 1)
            pe.wait_ge(a_vt_in, G * b + g + 1)
            for h in range(2):
                for n, (a, x) in enumerate(PRODUCTS):
                    mm = pe.matmul(AUX[0:4 * AK, h * HALF:(h + 1) * HALF], ak_cur[:, a, :],
                                   src[0][x][:, h * HALF:(h + 1) * HALF], start=n == 0, stop=n == 2)
            mm.then_inc(asc_ready, 1)

        def dve_a_adapter_keys(dve, b, g, first=False):
            dve.wait_ge(asc_ready, G * b + g)
            dve.tensor_copy(ak_cur[:], raw(ak_all[:, g, :, :])).then_inc(ak_in, 1)

        def pe_a_values(pe, b, g):
            pe.wait_ge(asc_in, G * b + g + 1)
            for t in range(TT):
                mm = pe.transpose(AUX[:, t * P:(t + 1) * P], vt[:, t * P:(t + 1) * P], ident[:])
            mm.then_inc(SA.aux, 1)

        def turned_values(part):
            heads = slice(0, 3) if part == 0 else slice(3, 4)
            return heads, AUX.rearrange("p (t j d) -> p t j d", t=TT, d=HD)[:, :, heads, :]

        def act_a_values(act, b, g, part, first=False):
            act.wait_ge(SA.aux, G * b + g + 1)
            if not first:
                act.wait_ge(SA.pv_done, HA.slots * (G * b + g - 1) + HA.n * (3 + part))
            if part:
                act.wait_ge(SA.v_lo, 2 * (G * b + g) + 1)
            heads, values = turned_values(part)
            act.copy(vst[:, :, heads, 0:HD], values).then_inc(SA.v_hi, 1)

        def dve_a_values(dve, b, g, part):
            dve.wait_ge(SA.v_hi, 2 * (G * b + g) + part + 1)
            heads, values = turned_values(part)
            dve.tensor_tensor(vst[:, :, heads, HD:2 * HD], values, raw(vst[:, :, heads, 0:HD]),
                              ALU.subtract).then_inc(SA.v_lo, 1)

        def act_a_copy_out(act, b, g, p, first=False):
            if p < 3:
                act.wait_ge(SA.proj_done, 3 * G * b + 3 * g + p + 1)
            else:
                act.wait_ge(asc_ready, G * b + g + 1)
            if p == 2:
                if not first:
                    act.wait_ge(yt_out, 16 * (G * b + g - 1))
                act.copy(vt[:], AUX).then_inc(a_vt_in, 1)
                return
            if p == 0:
                act.wait_ge(asc_out, 16 * (G * b + g))
                act.copy(turn[:], AUX).then_inc(SA.raw_in, 1)
            elif p == 1:
                act.wait_ge(SA.src_lo, 2 * G * b + 2 * g + 1)
                act.copy(turn[:], AUX).then_inc(SA.raw_in, 1)
            else:
                act.wait_ge(SA.src_lo, 2 * G * b + 2 * g + 2)
                act.copy(turn[0:4 * AK, :], AUX[0:4 * AK, :]).then_inc(asc_in, 1)

        def act_a_rope_hi(act, b, g, p):
            act.wait_ge(rope_done, 2 * G * b + 2 * g + p + 1)
            act.wait_ge(SA.stk_in[3], 96 * (G * b + g))
            act.copy(src[p][0][:], turn[:]).then_inc(SA.src_hi, 1)

        def dve_a_rope(dve, b, g, p):
            n = 2 * G * b + 2 * g + p
            dve.wait_ge(SA.raw_in, n + 1)
            dve.wait_ge(rope_done, n)
            settle(dve)
            dve.stream_shuffle(rot[:], turn[:], [(i + HD // 2) % HD for i in range(HD)]).then_inc(turned, 1)
            dve.wait_ge(turned, n + 1)
            dve.tensor_tensor(rot[:], rot[:], sin[:], ALU.mult).then_inc(sin_done, 1)

        def pool_a_rope(pool, b, g, p):
            n = 2 * G * b + 2 * g + p
            pool.wait_ge(turned, n + 1)
            pool.tensor_tensor(turn[:], turn[:], cos[:], ALU.mult).then_inc(cos_done, 1)
            pool.wait_ge(cos_done, n + 1)
            pool.wait_ge(sin_done, n + 1)
            pool.tensor_tensor(turn[:], turn[:], rot[:], ALU.add).then_inc(rope_done, 1)
            pool.wait_ge(SA.src_hi, n + 1)
            pool.tensor_tensor(src[p][1][:], turn[:], raw(src[p][0][:]), ALU.subtract).then_inc(SA.src_lo, 1)

        def sp_a_weights(sp, b, g, p):
            n = 3 * G * b + 3 * g + p
            sp.wait_ge(SA.w_lo, n)
            settle(sp)
            sp.dma_start(wq_raw[:], w_qkv[g, p]).then_inc(SA.w_in, 16)

        def pool_a_weights(pool, b, g, p, first=False):
            n = 3 * G * b + 3 * g + p
            pool.wait_ge(SA.w_in, 16 * n + 16)
            if not first:
                pool.wait_ge(SA.proj_done, n - 2)
            settle(pool)
            pool.tensor_copy(wq[p][0][:], wq_raw[:]).then_inc(SA.w_hi, 1)
            pool.wait_ge(SA.w_hi, n + 1)
            pool.tensor_tensor(wq[p][1][:], wq_raw[:], raw(wq[p][0][:]), ALU.subtract).then_inc(SA.w_lo, 1)

        def sp_a_result_denominators(sp, b, g):
            n = G * b + g
            sp.wait_ge(SA.y_done, 8 * n + 8)
            settle(sp)
            sp.dma_start(d_col[:], den[0:P:32, :]).then_inc(den_in, 16)
            sp.wait_ge(r_done, n + 1)
            settle(sp)
            sp.dma_start(rd_dram[b, g], r_col[:]).then_inc(rd_out, 16)
            sp.wait_ge(rd_out, 16 * n + 16)
            settle(sp)
            sp.wait_ge(yt_out, 16 * n)
            settle(sp)
            for j in range(4):
                sp.dma_start(rden[32 * j:32 * j + 32, :],
                             rd_dram[b, g, j:j + 1, :].broadcast_to([32, T])).then_inc(rden_in, 16)

        def dve_a_result_reciprocals(dve, b, g):
            n = G * b + g
            dve.wait_ge(den_in, 16 * n + 16)
            dve.wait_ge(rd_out, 16 * n)
            dve.reciprocal(r_col[:], d_col[:]).then_inc(r_done, 1)

        def pool_a_result(pool, b, g):
            n = G * b + g
            pool.wait_ge(rden_in, 64 * n + 64)
            pool.tensor_tensor(rden[:], y[:], rden[:], ALU.mult).then_inc(y_mul, 1)

        def sp_a_result_store(sp, b, g):
            n = G * b + g
            sp.wait_ge(y_mul, n + 1)
            settle(sp)
            sp.dma_start(yt_dram[b, g], rden[:]).then_inc(yt_out, 16)

        def sp_a_adapter_store(sp, b, g):
            sp.wait_ge(asc_in, G * b + g + 1)
            settle(sp)
            sp.dma_start(asc_dram[b, bass.ts(g, 4 * AK), :], turn[0:4 * AK, :]).then_inc(asc_out, 16)

        def pe_a_group(pe, b, g, first, more):
            parts = []
            if more >= 1:
                parts = [(slots, p, pe_project(p)) for slots, p in ((Q_SLOTS, 0), (K_SLOTS, 1), (V_SLOTS, 2))]
            for k in range(HA.slots):
                if k + 1 < HA.slots or more:
                    pe_scores(pe, HA, SA, b, g, k + 1)
                pe_max(pe, HA, SA, b, g, k + HA.lead, last=not more)
                for slots, p, products in parts:
                    if k not in slots:
                        continue
                    if k == slots[0]:
                        pe_a_part(pe, b, g + 1, p)
                    at, n = slots.index(k), len(slots)
                    for _ in range(PROJECTION * at // n, PROJECTION * (at + 1) // n):
                        o, a, x, start, stop = next(products)
                        mm = pe.matmul(o, a, x, start=start, stop=stop)
                    if k == slots[-1]:
                        mm.then_inc(SA.proj_done, 1)
                if k == ADAPTER and more:
                    pe_a_adapter(pe, b, g + 1)
                if k == TURN_V and more:
                    pe_a_values(pe, b, g + 1)
                if k > 1 or not first:
                    pe_pv(pe, HA, SA, b, g, k - 2, 0, first)

        def act_a_group(act, b, g, first, more):
            for k in range(HA.slots):
                if k + 1 < HA.slots or more:
                    act_exp(act, HA, SA, b, g, k + 1, 0, first)
                act_hi(act, HA, SA, b, g, k, 0, first)
                for at_k, p in zip(COPY_OUT, range(4)):
                    if k == at_k and more:
                        act_a_copy_out(act, b, g + 1, p, first)
                j, c = divmod(k, HA.n)
                for half, at_c in Y_CHUNK:
                    if c == at_c and j > 0:
                        if j == 1 and half == 1 and not first:
                            act.wait_ge(den_in, 16 * (G * b + g))
                        act_y(act, HA, SA, b, g, j - 1, half, first)
                    elif c == at_c and not first:
                        act_y(act, HA, SA, b, g - 1, 3, half)
                if k == 1 and not first:
                    act_a_values(act, b, g, 1)
                if k == TURN_V + 1 and more:
                    act_a_values(act, b, g + 1, 0)
                if more:
                    for at_k, p in zip(ROPE_HI, range(2)):
                        if k == at_k:
                            act_a_rope_hi(act, b, g + 1, p)

        def dve_a_group(dve, b, g, first, more):
            for k in range(HA.slots):
                dve_max(dve, HA, SA, b, g, k + HA.lead, last=not more)
                dve_lo(dve, HA, SA, b, g, k, 0)
                j, c = divmod(k, HA.n)
                for half, at_c in Y_CHUNK:
                    if c == at_c and j > 0:
                        if j == 1 and half == 1 and not first:
                            dve.wait_ge(y_mul, G * b + g)
                        dve_y(dve, HA, SA, b, g, j - 1, half)
                    elif c == at_c and not first:
                        dve_y(dve, HA, SA, b, g - 1, 3, half)
                if k == 1 and not first:
                    dve_a_values(dve, b, g, 1)
                if k == TURN_V + 1 and more:
                    dve_a_values(dve, b, g + 1, 0)
                if k == RECIPROCALS and not first:
                    dve_a_result_reciprocals(dve, b, g - 1)
                if more:
                    if k in ROPE_DVE:
                        dve_a_rope(dve, b, g + 1, ROPE_DVE.index(k))
                    if k == 30:
                        dve_a_adapter_keys(dve, b, g + 1)

        def pool_a_group(pool, b, g, first, more):
            if not first:
                pool_a_result(pool, b, g - 1)
            for p in range(2):
                if more:
                    pool_a_rope(pool, b, g + 1, p)
            for p in range(3):
                if more >= 2:
                    pool_a_weights(pool, b, g + 2, p)

        def sp_a_group(sp, b, g, first, more):
            for k in range(HA.slots):
                if k in WEIGHTS and more >= 2:
                    sp_a_weights(sp, b, g + 2, WEIGHTS.index(k))
                if k == STACKS[3]:
                    sp_stack(sp, HA, SA, b, g, 3, first)
                if k == DENOMINATORS and not first:
                    sp_a_result_denominators(sp, b, g - 1)
                if k == STORE and not first:
                    sp_a_result_store(sp, b, g - 1)
                if k in STACKS[:3] and more:
                    sp_stack(sp, HA, SA, b, g + 1, STACKS.index(k))
                if (k + 5) % HA.n == 0 and ((k + 5) // HA.n < 4 or more):
                    sp_max_rows(sp, HA, SA, b, g, (k + 5) // HA.n, last=not more)
                if k == ADAPTER_STORE and more:
                    sp_a_adapter_store(sp, b, g + 1)

        def groups(eng, b, body):
            body(eng, b, 0, True, G - 1)
            with eng.Fori(1, G - 2) as g:
                body(eng, b, g, False, 2)
            body(eng, b, G - 2, False, 1)
            body(eng, b, G - 1, False, 0)

        def sp_a(sp, b):
            sp.dma_start(cos[:], rope_cos).then_inc(tab_in, 16)
            sp.dma_start(sin[:], rope_sin).then_inc(tab_in, 16)
            for g in range(2):
                for p in range(3):
                    sp_a_weights(sp, b, g, p)
            sp_a_adapter_store(sp, b, 0)
            for h in range(3):
                sp_stack(sp, HA, SA, b, 0, h, first=True)
            sp_max_rows(sp, HA, SA, b, 0, 0)
            groups(sp, b, sp_a_group)
            sp_a_result_denominators(sp, b, G - 1)
            sp_a_result_store(sp, b, G - 1)
            sp.wait_ge(yt_out, 16 * (G * b + G))
            settle(sp)
            sp.wait_ge(asc_out, 16 * (G * b + G))

        def pool_a(pool, b):
            pool.memset(raw(kst[96:98, :, :]), 1.0).then_inc(SA.fill, 1)
            pool.wait_ge(SA.fill, 2 * b + 1)
            settle(pool)
            pool.memset(raw(vst[:, :, :, 2 * HD:3 * HD]), 1.0).then_inc(SA.fill, 1)
            for p in range(3):
                pool_a_weights(pool, b, 0, p, first=True)
            pool.wait_ge(tab_in, 32 * b + 32)
            for p in range(2):
                pool_a_rope(pool, b, 0, p)
            for p in range(3):
                pool_a_weights(pool, b, 1, p)
            groups(pool, b, pool_a_group)
            pool_a_result(pool, b, G - 1)

        def pe_a(pe, b):
            for p in range(3):
                pe_a_part(pe, b, 0, p, first=True)
                for o, a, x, start, stop in pe_project(p):
                    mm = pe.matmul(o, a, x, start=start, stop=stop)
                mm.then_inc(SA.proj_done, 1)
            pe_a_adapter(pe, b, 0)
            pe_a_values(pe, b, 0)
            pe.wait_ge(SA.fill, 2 * b + 2)
            for v in range(HA.lead):
                pe_max(pe, HA, SA, b, 0, v, first=True)
            pe_scores(pe, HA, SA, b, 0, 0, first=True)
            groups(pe, b, pe_a_group)
            for k in (-2, -1):
                pe_pv(pe, HA, SA, b, G, k, 0)

        def act_a(act, b):
            act_a_copy_out(act, b, 0, 0)
            act_a_rope_hi(act, b, 0, 0)
            act_a_copy_out(act, b, 0, 1)
            act_a_rope_hi(act, b, 0, 1)
            act_a_copy_out(act, b, 0, 2, first=True)
            act_a_copy_out(act, b, 0, 3)
            for part in range(2):
                act_a_values(act, b, 0, part, first=True)
            act_exp(act, HA, SA, b, 0, 0, 0, first=True)
            groups(act, b, act_a_group)
            for half in (1, 0):
                act_y(act, HA, SA, b, G - 1, 3, half)

        def dve_a(dve, b):
            dve.wait_ge(tab_in, 32 * b + 32)
            for p in range(2):
                dve_a_rope(dve, b, 0, p)
            dve_a_adapter_keys(dve, b, 0)
            for part in range(2):
                dve_a_values(dve, b, 0, part)
            for v in range(HA.lead):
                dve_max(dve, HA, SA, b, 0, v, first=True)
            groups(dve, b, dve_a_group)
            for half in (1, 0):
                dve_y(dve, HA, SA, b, G - 1, 3, half)
            dve_a_result_reciprocals(dve, b, G - 1)

        CH_ROWS = [min(3, G - 3 * c) * 4 * AK for c in range(AH)]

        def sp_adapter(sp, b):
            for c in range(AH):
                sp.dma_start(asc[0:CH_ROWS[c], c, :],
                             asc_dram[b, 12 * AK * c:12 * AK * c + CH_ROWS[c], :]).then_inc(ad_in, 16)
            for s in range(2):
                sp.dma_start(raw(av[s][:]), av_dram[s]).then_inc(av_in, 16)
            for g in range(G):
                if g >= 2:
                    sp.wait_ge(ad_y, G * b + g - 1)
                    settle(sp)
                sp.dma_start(yt_in_sb[:, g % 2, :], yt_dram[b, g]).then_inc(ad_yin[g % 2], 16)

        def pe_adapter(pe, b):
            pe.wait_ge(ad_in, 48 * b + 48)
            for t in range(TT + 1):
                if t < TT:
                    if t >= 2:
                        pe.wait_ge(ad_sub, TT * b + t - 1)
                    for c in range(AH):
                        mm = pe.transpose(banks[:, t % 2, 12 * AK * c:12 * AK * c + CH_ROWS[c]],
                                          asc[0:CH_ROWS[c], c, t * P:(t + 1) * P], ident[0:CH_ROWS[c], 0:CH_ROWS[c]])
                    mm.then_inc(ad_tr, 1)
                if t >= 1:
                    s = t - 1
                    pe.wait_ge(ad_p, TT * b + s + 1)
                    if s >= 2:
                        pe.wait_ge(ad_plo, TT * b + s - 1)
                    p_tile = a_e[:, s % 2, :, :].rearrange("p h k -> p (h k)")
                    for c in range(AH):
                        mm = pe.transpose(banks[0:CH_ROWS[c], 2 + s % 2, c * P:(c + 1) * P],
                                          p_tile[:, 12 * AK * c:12 * AK * c + CH_ROWS[c]], ident[:])
                    mm.then_inc(ad_pt, 1)
            pe.wait_ge(av_in, 32 * b + 32)
            pe.wait_ge(ad_plo, TT * b + TT)
            for g in range(G):
                c, rows = g // 3, CH_ROWS[g // 3]
                if g >= 2:
                    pe.wait_ge(ad_y, G * b + g - 1)
                for h in range(2):
                    for n, (a, x) in enumerate(PRODUCTS):
                        mm = pe.matmul(banks[:, 4 + 2 * (g % 2) + h, :], av[a][0:rows, g, :],
                                       pa[x][0:rows, c, h * HALF:(h + 1) * HALF], start=n == 0, stop=n == 2)
                mm.then_inc(ad_mm, 1)

        def dve_adapter(dve, b):
            for t in range(TT):
                n = TT * b + t
                s_bank = banks[:, t % 2, 0:NH * AK].rearrange("p (h k) -> p h k", k=AK)
                e, st = a_e[:, t % 2, :, :], [a_s[:, t % 2, i, :] for i in range(4)]
                dve.wait_ge(ad_tr, n + 1)
                dve.tensor_reduce(st[0], s_bank, AX.X, ALU.max).then_inc(ad_mx, 1)
                dve.wait_ge(ad_mx, n + 1)
                if t >= 2:
                    dve.wait_ge(ad_pt, n - 1)
                dve.tensor_tensor(e, s_bank, st[0].unsqueeze(2).broadcast_to([P, NH, AK]),
                                  ALU.subtract).then_inc(ad_sub, 1)
                dve.wait_ge(ad_exp, n + 1)
                dve.tensor_reduce(st[1], e, AX.X, ALU.add).then_inc(ad_sum, 1)
                dve.wait_ge(ad_sum, n + 1)
                dve.reciprocal(st[2], st[1]).then_inc(ad_rec, 1)
                dve.wait_ge(ad_rec, n + 1)
                dve.tensor_scalar(st[3], st[2], gate[:, 0:1], None, ALU.mult).then_inc(ad_gate, 1)
                dve.wait_ge(ad_gate, n + 1)
                dve.tensor_tensor(e, e, st[3].unsqueeze(2).broadcast_to([P, NH, AK]), ALU.mult).then_inc(ad_p, 1)
                if t >= 1:
                    dve_adapter_lo(dve, b, t - 1)
            dve_adapter_lo(dve, b, TT - 1)
            for g in range(G):
                dve.wait_ge(ad_mm, G * b + g + 1)
                dve.wait_ge(ad_yin[g % 2], 16 * (G // 2 * b + g // 2 + 1))
                if g >= 2:
                    dve.wait_ge(ad_lo, G * b + g - 1)
                q = 4 + 2 * (g % 2)
                dve.tensor_tensor(y_sum[:, g % 2, :], banks[:, q:q + 2, :].rearrange("p b n -> p (b n)"),
                                  yt_in_sb[:, g % 2, :], ALU.add).then_inc(ad_y, 1)

        def adapter_views(t, which):
            r = CH_ROWS[0]
            full = (banks[0:r, 2 + t % 2, 0:2 * P].rearrange("p (c t) -> p c t", c=2),
                    pa[which][0:r, 0:2, t * P:(t + 1) * P])
            r = CH_ROWS[2]
            short = (banks[0:r, 2 + t % 2, 2 * P:3 * P], pa[which][0:r, 2, t * P:(t + 1) * P])
            return full, short

        def dve_adapter_lo(dve, b, t):
            dve.wait_ge(ad_phi, TT * b + t + 1)
            for (bank, lo), (_, hi) in zip(adapter_views(t, 1), adapter_views(t, 0)):
                last = dve.tensor_tensor(lo, bank, raw(hi), ALU.subtract)
            last.then_inc(ad_plo, 1)

        def act_adapter(act, b):
            for t in range(TT):
                n = TT * b + t
                e = a_e[:, t % 2, :, :]
                act.wait_ge(ad_sub, n + 1)
                act.activation(e, e, ACT.Exp, scale=SCALE_ADAPTER).then_inc(ad_exp, 1)
                act.wait_ge(ad_pt, n + 1)
                for bank, hi in adapter_views(t, 0):
                    last = act.copy(hi, bank)
                last.then_inc(ad_phi, 1)
            for g in range(G):
                act.wait_ge(ad_y, G * b + g + 1)
                act.copy(xt[0][:, g, :], y_sum[:, g % 2, :]).then_inc(ad_hi, 1)

        def pool_adapter(pool, b):
            for g in range(G):
                pool.wait_ge(ad_hi, G * b + g + 1)
                pool.tensor_tensor(xt[1][:, g, :], y_sum[:, g % 2, :], raw(xt[0][:, g, :]),
                                   ALU.subtract).then_inc(ad_lo, 1)

        class Dense:
            def __init__(self, name, b, f=0):
                self.ffn = name == "ffn"
                self.wide = name != "wo"
                self.S = SD if self.wide else SO
                self.cc = CC if self.wide else 1
                self.parts = 4 if self.wide else 1
                self.loads = 2 if self.wide else 1
                self.i = 3 * b + (0 if name == "proj" else 1 + f) if self.wide else b
                self.f = 2 * b + f
                self.dram = {"proj": w_proj, "ffn": w_base, "wo": wb_out}[name]
                self.name = name
                self.lag = LAG if self.ffn else 0

            def chunks(self, part, s=None):
                t = w_raw if s is None else w[s]
                return t[:, 2 * part:2 * part + 2, :]

            def weights(self, s, c, o):
                return w[s][:, c, :] if self.wide else w[s][:, o, :]

        def sp_dense(sp, b, d):
            if d.ffn:
                sp.dma_start(la_raw[:], w_lora_in).then_inc(f_in[0], 16)
            for o in range(d.loads):
                for q in range(d.parts):
                    if o:
                        sp.wait_ge(d.S.w_lo, d.parts * (d.loads * d.i + o - 1) + q + 1)
                        settle(sp)
                    src_ap = d.dram[o, :, 2 * q:2 * q + 2, :] if d.wide else d.dram
                    sp.dma_start(d.chunks(q), src_ap).then_inc(d.S.w_in[q], 16)
                if o == 0:
                    if d.ffn:
                        sp.dma_start(lb_raw[:], w_lora_out).then_inc(f_in[1], 16)
                        sp.dma_start(bias_row[:], b_base.broadcast_to([P, C])).then_inc(f_in[2], 16)
                    elif d.name == "proj":
                        sp.dma_start(X[:], x_in[b].rearrange("(t p) c -> p t c", p=P)).then_inc(px_in, 16)
                    else:
                        sp.dma_start(X[:], x_dram[b]).then_inc(ox_in, 16)
                        sp.dma_start(bias_row[:], bb_out.broadcast_to([P, C])).then_inc(ox_in, 16)

        def sp_output(sp, b):
            i = 3 * b + 2
            for t in range(TT):
                sp.wait_ge(SD.added, 2 * TT * i + TT + t + 1)
                settle(sp)
                sp.dma_start(out[b, t * P:(t + 1) * P, :], X[:, t, :]).then_inc(out_st, 16)
            sp.wait_ge(out_st, 16 * TT * (b + 1))

        def pool_dense(pool, b, d):
            if d.name == "proj":
                return
            if d.ffn:
                pool.wait_ge(f_in[2], 16 * d.f + 16)
            else:
                pool.wait_ge(ox_in, 32 * b + 32)
            for t in range(TT):
                pool.tensor_tensor(X[:, t, :], X[:, t, :], bias_row[:], ALU.add).then_inc(f_bias if d.ffn else o_bias, 1)

        def act_dense(act, b, d):
            if d.ffn:
                act.wait_ge(f_in[0], 16 * d.f + 16)
                act.copy(la[0][:], la_raw[:]).then_inc(f_hi, 1)
            act_dense_weights(act, d, 0)
            if d.ffn:
                act.wait_ge(f_in[1], 16 * d.f + 16)
                act.copy(lb[0][:], lb_raw[:]).then_inc(f_hi, 1)
                act.wait_ge(f_h, d.f + 1)
                act.activation(logit_t[:], banks[0:NE, 2:4, :].rearrange("p b n -> p (b n)"), ACT.Identity,
                               bias=b_rout[:, 0:1]).then_inc(f_lg, 1)
                act.copy(h_sb[:], AUX).then_inc(f_hsb, 1)
                act.wait_ge(f_hw, d.f + 1)
                act.copy(hw[0][:], h_sb[:]).then_inc(f_hwhi, 1)
            for o in range(1, d.loads):
                act_dense_weights(act, d, o)

        def act_dense_weights(act, d, o):
            for q in range(d.parts):
                n = d.parts * (d.loads * d.i + o) + q
                act.wait_ge(d.S.w_in[q], 16 * (d.loads * d.i + o) + 16)
                if o:
                    act.wait_ge(w_free, d.parts * d.i + q + 1)
                act.copy(d.chunks(q, 0), d.chunks(q)).then_inc(d.S.w_hi, 1)

        def dve_dense_weights(dve, d, o, parts=None):
            for q in parts or range(d.parts):
                n = d.parts * (d.loads * d.i + o) + q
                dve.wait_ge(d.S.w_hi, n + 1)
                dve.tensor_tensor(d.chunks(q, 1), d.chunks(q), raw(d.chunks(q, 0)), ALU.subtract).then_inc(d.S.w_lo, 1)

        def dve_routing(dve, f):
            step = [0]

            def done(ins):
                step[0] += 1
                ins.then_inc(f_dve, 1)
                dve.wait_ge(f_dve, F_DVE * f + step[0])

            z, cum, cnt, t0, t1, k1, s1, tau = (sp_buf[:, i, :] for i in range(8))

            def by_tile(a):
                return a.rearrange("p (t e) -> p t e", e=NE)

            ge, zge = pairs[:, 0], pairs[:, 1]
            dve.wait_ge(f_zt, f + 1)
            done(dve.tensor_copy(z, banks[:, 2, 0:TT * NE]))
            zi = by_tile(z).unsqueeze(3).broadcast_to([P, TT, NE, NE])
            zj = by_tile(z).unsqueeze(2).broadcast_to([P, TT, NE, NE])
            done(dve.tensor_tensor(ge, zj, zi, ALU.is_ge))
            dve.tensor_reduce(cnt, ge.rearrange("p t i j -> p (t i) j"), AX.X, ALU.add)
            done(dve.tensor_tensor(zge, ge, zj, ALU.mult))
            done(dve.tensor_reduce(cum, zge.rearrange("p t i j -> p (t i) j"), AX.X, ALU.add))
            done(dve.tensor_tensor(t0, cnt, z, ALU.mult))
            done(dve.tensor_scalar(t0, t0, 1.0, None, ALU.add))
            done(dve.tensor_tensor(t0, t0, cum, ALU.is_gt))
            done(dve.tensor_tensor(t1, t0, z, ALU.mult))
            dve.tensor_reduce(k1[:, 0:TT], by_tile(t0), AX.X, ALU.add)
            done(dve.tensor_reduce(s1[:, 0:TT], by_tile(t1), AX.X, ALU.add))
            done(dve.reciprocal(k1[:, TT:2 * TT], k1[:, 0:TT]))
            done(dve.scalar_tensor_tensor(out=tau[:, 0:TT], in0=s1[:, 0:TT], scalar=-1.0, in1=k1[:, TT:2 * TT],
                                          op0=ALU.add, op1=ALU.mult))
            done(dve.tensor_tensor(by_tile(t1), by_tile(z), tau[:, 0:TT].unsqueeze(2).broadcast_to([P, TT, NE]),
                                   ALU.subtract))
            done(dve.tensor_scalar(t0, t1, 0.0, None, ALU.max))
            spread = pairs[:].rearrange("p a t i j -> p (a t i j)")
            done(dve.tensor_copy(spread.rearrange("p (e r) -> p e r", r=R),
                                 t0.unsqueeze(2).broadcast_to([P, TT * NE, R])))
            assert step[0] == F_DVE, step[0]

        def dve_dense(dve, b, d):
            if d.ffn:
                dve.wait_ge(f_hi, 2 * d.f + 1)
                dve.tensor_tensor(la[1][:], la_raw[:], raw(la[0][:]), ALU.subtract).then_inc(f_lo, 1)
            dve_dense_weights(dve, d, 0)
            if d.ffn:
                dve.wait_ge(f_hi, 2 * d.f + 2)
                dve.tensor_tensor(lb[1][:], lb_raw[:], raw(lb[0][:]), ALU.subtract).then_inc(f_lo, 1)
                dve_routing(dve, d.f)
                dve.wait_ge(f_wt, d.f + 1)
                dve.wait_ge(f_hsb, d.f + 1)
                dve.tensor_tensor(h_sb[:], AUX, h_sb[:], ALU.mult).then_inc(f_hw, 1)
                dve.wait_ge(f_hwhi, d.f + 1)
                dve.tensor_tensor(hw[1][:], h_sb[:], raw(hw[0][:]), ALU.subtract).then_inc(f_hwlo, 1)
            n = 2 * TT
            for i in range(n + d.lag):
                if d.loads == 2 and i in (TT - 1, TT):
                    dve_dense_weights(dve, d, 1, range(d.parts - 1) if i < TT else (d.parts - 1,))
                if i < d.lag:
                    continue
                o, t = divmod(i - d.lag, TT)
                if i == d.lag:
                    if d.name == "proj":
                        dve.wait_ge(px_in, 16 * b + 16)
                    else:
                        dve.wait_ge(f_bias if d.ffn else o_bias, TT * (d.f + 1) if d.ffn else TT * (b + 1))
                dve.wait_ge(d.S.tile, n * d.i + i - d.lag + 1)
                x = X[:, t, o * HALF:(o + 1) * HALF]
                dve.tensor_tensor(x, banks[:, 4 + (i - d.lag) % RING, :], x, ALU.add).then_inc(d.S.added, 1)

        def pe_lora_in(pe, f):
            pe.wait_ge(f_lo, 2 * f + 1)
            for bank, rows in ((2, slice(P, P + NE)), (0, slice(0, P))):
                m = rows.stop - rows.start
                for c in range(CC):
                    for a, x in PRODUCTS:
                        for h in range(2):
                            mm = pe.matmul(banks[0:m, bank + h, :], la[a][:, c, rows], xt[x][:, c, h * HALF:(h + 1) * HALF],
                                           start=c == 0 and (a, x) == (0, 0), stop=c == CC - 1 and (a, x) == PRODUCTS[-1])
            mm.then_inc(f_h, 1)

        def pe_turn_logits(pe, f):
            pe.wait_ge(f_lg, f + 1)
            settle(pe)
            for t in range(TT):
                mm = pe.transpose(banks[:, 2, t * NE:(t + 1) * NE], logit_t[:, t * P:(t + 1) * P], ident[0:NE, 0:NE])
            mm.then_inc(f_zt, 1)

        def pe_turn_weights(pe, f):
            pe.wait_ge(f_dve, F_DVE * (f + 1))
            pe.wait_ge(f_hsb, f + 1)
            spread = pairs[:].rearrange("p a t i j -> p (a t i j)")
            for t in range(TT):
                mm = pe.transpose(AUX[:, t * P:(t + 1) * P], spread[:, t * P:(t + 1) * P], ident[:])
            mm.then_inc(f_wt, 1)

        def pe_dense(pe, b, d):
            if d.ffn:
                pe_lora_in(pe, d.f)
            n = 2 * TT
            for i in range(n + d.lag):
                if i < n:
                    o, t = divmod(i, TT)
                    if i >= RING:
                        pe.wait_ge(d.S.added, n * d.i + i - RING + 1)
                    for q in range(d.parts):
                        part = d.parts * (d.loads * d.i + min(o, d.loads - 1)) + q + 1
                        if t == 0:
                            pe.wait_ge(d.S.w_lo, part)
                        for c in range(q * d.cc // d.parts, (q + 1) * d.cc // d.parts):
                            for m, (x, a) in enumerate(PRODUCTS):
                                mm = pe.matmul(banks[:, 4 + i % RING, :], xt[x][:, c, t * P:(t + 1) * P], d.weights(a, c, o),
                                               start=c == 0 and m == 0, stop=not d.ffn and c == d.cc - 1 and m == 2)
                                if i == TT and c == 0 and m == 0 and d.loads == 2:
                                    mm.then_inc(w_free, 1)
                        if i == TT - 1 and d.loads == 2 and q < d.parts - 1:
                            mm.then_inc(w_free, 1)
                    if not d.ffn:
                        mm.then_inc(d.S.tile, 1)
                if d.ffn and i == 0:
                    pe_turn_logits(pe, d.f)
                if d.ffn and i == d.lag - 1:
                    pe_turn_weights(pe, d.f)
                if d.ffn and i >= d.lag:
                    o, t = divmod(i - d.lag, TT)
                    if i == d.lag:
                        pe.wait_ge(f_hwlo, d.f + 1)
                        pe.wait_ge(f_lo, 2 * d.f + 2)
                    for m, (x, a) in enumerate(PRODUCTS):
                        mm = pe.matmul(banks[:, 4 + (i - d.lag) % RING, :], hw[x][:, t * P:(t + 1) * P],
                                       lb[a][:, o * HALF:(o + 1) * HALF], start=False, stop=m == 2)
                    mm.then_inc(d.S.tile, 1)

        def sp_b(sp, b):
            for p in range(3):
                sp.wait_ge(SB.w_lo, 3 * b + p)
                settle(sp)
                sp.dma_start(wq_raw[:], wb_qkv[p]).then_inc(SB.w_in, 16)
            sp.wait_ge(SB.fill, 8 * (b + 1))
            settle(sp)
            for h in range(4):
                sp_stack(sp, HB, SB, b, 0, h, first=True)
            sp_max_rows(sp, HB, SB, b, 0, 0)
            for g in range(GB):
                for k in range(HB.slots):
                    if g + 1 < GB and k in (18, 34, 50):
                        sp_stack(sp, HB, SB, b, g + 1, (18, 34, 50).index(k))
                    if g and k == 1:
                        sp_stack(sp, HB, SB, b, g, 3)
                    if (k + 5) % HB.n == 0 and ((k + 5) // HB.n < 4 or g + 1 < GB):
                        sp_max_rows(sp, HB, SB, b, g, (k + 5) // HB.n, last=g + 1 == GB)

        def pool_b(pool, b):
            for i, (part, value) in enumerate(((qst[0:96, :, :], 0.0), (kst[0:96, :, :], 0.0), (kst[96:98, :, :], 1.0))):
                pool.memset(raw(part), value).then_inc(SB.fill, 1)
                pool.wait_ge(SB.fill, 8 * b + i + 1)
                settle(pool)
            pool.memset(raw(vsb[:]), 0.0).then_inc(SB.fill, 1)
            pool.wait_ge(SB.fill, 8 * b + 4)
            settle(pool)
            for odd in range(2):
                c0 = 64 + HDB * odd
                pool.memset(raw(vsb[:, :, odd::2, c0:c0 + HDB]), 1.0).then_inc(SB.fill, 2)

        def pe_b(pe, b):
            for p in range(3):
                pe.wait_ge(SB.w_lo, 3 * b + p + 1)
                if p:
                    pe.wait_ge(SB.raw_in, 3 * b + p)
                for o, a, x, start, stop in pe_project(2):
                    mm = pe.matmul(o, a, x, start=start, stop=stop)
                mm.then_inc(SB.proj_done, 1)
            pe.wait_ge(SB.raw_in, 3 * b + 3)
            for t in range(TT):
                mm = pe.transpose(AUX[:, t * P:(t + 1) * P], vt[:, t * P:(t + 1) * P], ident[:])
            mm.then_inc(SB.aux, 1)
            pe.wait_ge(SB.fill, 8 * b + 8)
            for v in range(HB.lead):
                pe_max(pe, HB, SB, b, 0, v, first=True)
            pe_scores(pe, HB, SB, b, 0, 0, first=True)
            pe.wait_ge(SB.v_lo, b + 1)
            for g in range(GB):
                for k in range(HB.slots):
                    if k + 1 < HB.slots or g + 1 < GB:
                        pe_scores(pe, HB, SB, b, g, k + 1)
                    pe_max(pe, HB, SB, b, g, k + HB.lead, last=g == GB - 1)
                    if k > 1 or g:
                        pe_pv(pe, HB, SB, b, g, k - 2, HB.slots * g, g == 0)
            for k in (-2, -1):
                pe_pv(pe, HB, SB, b, GB, k, HB.slots * GB)

        def act_b(act, b):
            for p in range(3):
                act.wait_ge(SB.w_in, 16 * (3 * b + p) + 16)
                if p:
                    act.wait_ge(SB.proj_done, 3 * b + p)
                act.copy(wq[2][0][:], wq_raw[:]).then_inc(SB.w_hi, 1)
                act.wait_ge(SB.proj_done, 3 * b + p + 1)
                if p == 1:
                    act.wait_ge(SB.src_lo, 2 * b + 1)
                dst = vt if p == 2 else turn
                act.activation(dst[:], AUX, ACT.Identity, bias=b_qkv[:, p:p + 1]).then_inc(SB.raw_in, 1)
                if p < 2:
                    act.wait_ge(SB.raw_in, 3 * b + p + 1)
                    act.copy(src[p][0][:], turn[:]).then_inc(SB.src_hi, 1)
            act.wait_ge(SB.fill, 8 * b + 8)
            act.wait_ge(SB.aux, b + 1)
            for odd in range(2):
                act.copy(vsb[:, :, odd::2, HDB * odd:HDB * odd + HDB], turned_b(odd)).then_inc(SB.v_hi, 1)
            act_exp(act, HB, SB, b, 0, 0, 0, first=True)
            for g in range(GB):
                ring = HB.slots * g % 3
                for k in range(HB.slots):
                    if k + 1 < HB.slots or g + 1 < GB:
                        act_exp(act, HB, SB, b, g, k + 1, ring, g == 0)
                    act_hi(act, HB, SB, b, g, k, ring, g == 0)
                    for half, at_c in Y_CHUNK:
                        if k % (2 * HB.n) == at_c and (k > at_c or g):
                            act_y(act, HB, SB, b, *((g, k // HB.n - 1) if k > at_c else (g - 1, 3)), half, g == 0)
            for half in (1, 0):
                act_y(act, HB, SB, b, GB - 1, 3, half)
            act.wait_ge(by_y, b + 1)
            act.copy(xt[0][:, 0, :], y[:]).then_inc(by_hi, 1)

        def turned_b(odd):
            return AUX.rearrange("p (t j d) -> p t j d", t=TT, d=HDB)[:, :, odd::2, :]

        def dve_b(dve, b):
            for p in range(3):
                dve.wait_ge(SB.w_hi, 3 * b + p + 1)
                dve.tensor_tensor(wq[2][1][:], wq_raw[:], raw(wq[2][0][:]), ALU.subtract).then_inc(SB.w_lo, 1)
                if p < 2:
                    dve.wait_ge(SB.src_hi, 2 * b + p + 1)
                    dve.tensor_tensor(src[p][1][:], turn[:], raw(src[p][0][:]), ALU.subtract).then_inc(SB.src_lo, 1)
            dve.wait_ge(SB.v_hi, 2 * b + 2)
            for odd in range(2):
                c0 = HDB * odd
                last = dve.tensor_tensor(vsb[:, :, odd::2, 32 + c0:32 + c0 + HDB], turned_b(odd),
                                         raw(vsb[:, :, odd::2, c0:c0 + HDB]), ALU.subtract)
            last.then_inc(SB.v_lo, 1)
            for v in range(HB.lead):
                dve_max(dve, HB, SB, b, 0, v, first=True)
            for g in range(GB):
                ring = HB.slots * g % 3
                for k in range(HB.slots):
                    dve_max(dve, HB, SB, b, g, k + HB.lead, last=g == GB - 1)
                    dve_lo(dve, HB, SB, b, g, k, ring)
                    for half, at_c in Y_CHUNK:
                        if k % (2 * HB.n) == at_c and (k > at_c or g):
                            dve_y(dve, HB, SB, b, *((g, k // HB.n - 1) if k > at_c else (g - 1, 3)), half)
            for half in (1, 0):
                dve_y(dve, HB, SB, b, GB - 1, 3, half)
            dve.wait_ge(SB.y_done, NHB * (b + 1))
            dve.reciprocal(rden[:], den[:]).then_inc(by_r, 1)
            dve.wait_ge(by_r, b + 1)
            dve.scalar_tensor_tensor(out=y[:], in0=y[:], scalar=SCALE_B_OUT, in1=rden[:], op0=ALU.mult,
                                     op1=ALU.mult).then_inc(by_y, 1)
            dve.wait_ge(by_hi, b + 1)
            dve.tensor_tensor(xt[1][:, 0, :], y[:], raw(xt[0][:, 0, :]), ALU.subtract).then_inc(by_lo, 1)

        def sp_setup(sp):
            sp.dma_start(gate[:], gating.broadcast_to([P, 1])).then_inc(c_in, 16)
            sp.dma_start(b_rout[:], b_router).then_inc(c_in, 16)
            sp.dma_start(b_qkv[:], bb_qkv).then_inc(c_in, 16)
            sp.dma_start(at_raw[:], adapter).then_inc(at_in, 16)
            for n in range(4):
                part, gh = 1 + n // 2, n % 2
                if n:
                    sp.wait_ge(sw_lo, n + 1)
                for i in range(4):
                    sp.dma_start(w_raw[:, :, i * P:(i + 1) * P], w_qkv[4 * gh + i, part]).then_inc(sw_in, 16)
            sp.wait_ge(s_zero, 1)
            for s in range(2):
                sp.dma_start(av_dram[s], zeros[:].rearrange("p (g n) -> p g n", g=G)).then_inc(s_avd, 16)
            sp.wait_ge(s_avd, 32)
            sp.wait_ge(s_av, 2)
            for s in range(2):
                v = raw(avs[s][:]).rearrange("p (g j d) -> p g j d", g=G, d=HD)
                for g3 in range(3):
                    for j in range(4):
                        r0 = (4 * g3 + j) * AK
                        sp.dma_start(av_dram[s][r0:r0 + AK, g3::3, HD * j:HD * j + HD], v[:, g3::3, j, :]).then_inc(s_avd, 16)
            sp.wait_ge(s_avd, 32 + 24 * 16)
            sp.wait_ge(c_in, 48)

        def pool_setup(pool):
            pool.memset(ident[:], 0.0).then_inc(c_set, 1)
            pool.memset(mask_main[:], 0.0).then_inc(c_set, 1)
            pool.memset(mask_max[:], 0.0).then_inc(c_set, 1)
            pool.memset(raw(ak_all[:]), 0.0).then_inc(c_set, 1)
            pool.memset(zeros[:], 0.0).then_inc(s_zero, 1)
            pool.wait_ge(c_set, 4)
            row_minus_column = dict(base=0, pattern=[[-1, P]], channel_multiplier=1)
            pool.affine_select(out=ident[:], in_=ident[:], compare_op=ALU.not_equal, fill=1.0,
                               **row_minus_column).then_inc(c_set, 1)
            pool.affine_select(out=mask_main[:], in_=mask_main[:], compare_op=ALU.is_ge, fill=MASKED,
                               base=0, pattern=[[1, P]], channel_multiplier=-1).then_inc(c_set, 1)
            pool.affine_select(out=mask_max[:], in_=mask_max[:], compare_op=ALU.is_ge, fill=MASKED,
                               **row_minus_column).then_inc(c_set, 1)

        def act_setup(act):
            act.wait_ge(at_in, 16)
            act.copy(at[0][:], at_raw[:]).then_inc(sw_hi, 1)
            for n in range(4):
                act.wait_ge(sw_in, 64 * (n + 1))
                if n:
                    act.wait_ge(s_mm, n)
                act.copy(w[0][:], w_raw[:]).then_inc(sw_hi, 1)
                act.wait_ge(s_mm, n + 1)
                act.copy(akv[:, n // 2, (n % 2) * HALF:(n % 2 + 1) * HALF], banks[0:AK, n % 2, :]).then_inc(s_ev, 1)
            act.wait_ge(s_ev, 4)
            act.copy(avs[0][:], akv[:, 1, :]).then_inc(s_av, 1)

        def dve_setup(dve):
            dve.wait_ge(c_set, 7)
            dve.tensor_copy(ident16[:], ident[:])
            dve.wait_ge(sw_hi, 1)
            dve.tensor_tensor(at[1][:], at_raw[:], raw(at[0][:]), ALU.subtract).then_inc(sw_lo, 1)
            for n in range(4):
                dve.wait_ge(sw_hi, n + 2)
                dve.tensor_tensor(w[1][:], w_raw[:], raw(w[0][:]), ALU.subtract).then_inc(sw_lo, 1)
            dve.wait_ge(s_tr, 1)
            turned_keys = banks[:, 2, 0:G * AK].rearrange("p (g k) -> p g k", k=AK)
            for j in range(4):
                rows, cols = slice(32 * j, 32 * j + 32), slice(AK * j, AK * j + AK)
                dve.tensor_copy(ak_all[rows, :, 0, cols], turned_keys[rows]).then_inc(s_tr, 1)
            dve.wait_ge(s_tr, 5)
            for j in range(4):
                rows, cols = slice(32 * j, 32 * j + 32), slice(AK * j, AK * j + AK)
                dve.tensor_tensor(ak_all[rows, :, 1, cols], turned_keys[rows], raw(ak_all[rows, :, 0, cols]), ALU.subtract)
            dve.wait_ge(s_av, 1)
            dve.tensor_tensor(avs[1][:], akv[:, 1, :], raw(avs[0][:]), ALU.subtract).then_inc(s_av, 1)

        def pe_setup(pe):
            pe.wait_ge(c_set, 7)
            for n in range(4):
                pe.wait_ge(sw_lo, n + 2)
                if n >= 2:
                    pe.wait_ge(s_ev, n - 1)
                for c in range(CC):
                    for m, (x, a) in enumerate(PRODUCTS):
                        mm = pe.matmul(banks[0:AK, n % 2, :], at[x][:, c, :], w[a][:, c, :], start=c == 0 and m == 0,
                                       stop=c == CC - 1 and m == 2)
                mm.then_inc(s_mm, 1)
            pe.wait_ge(s_ev, 4)
            for g in range(G):
                mm = pe.transpose(banks[:, 2, g * AK:(g + 1) * AK], akv[:, 0, g * P:(g + 1) * P], ident[0:AK, 0:AK])
            mm.then_inc(s_tr, 1)

        def nothing(eng, *_):
            pass

        def program(eng, setup, norm_, attention_a, adapter_, dense_, attention_b, output=nothing):
            setup(eng)
            setup_end(eng)
            with eng.Fori(0, B) as b:
                norm_(eng, b, 0)
                phase_end(eng, b, 0)
                attention_a(eng, b)
                phase_end(eng, b, 1)
                adapter_(eng, b)
                phase_end(eng, b, 2)
                dense_(eng, b, Dense("proj", b))
                phase_end(eng, b, 3)
                norm_(eng, b, 1)
                phase_end(eng, b, 4)
                dense_(eng, b, Dense("ffn", b, 0))
                phase_end(eng, b, 5)
                norm_(eng, b, 2)
                phase_end(eng, b, 6)
                attention_b(eng, b)
                phase_end(eng, b, 7)
                dense_(eng, b, Dense("wo", b))
                phase_end(eng, b, 8)
                norm_(eng, b, 3)
                phase_end(eng, b, 9)
                dense_(eng, b, Dense("ffn", b, 1))
                output(eng, b)
                phase_end(eng, b, 10)

        block = ctx.enter_context(nc.Block())

        @block.sync
        def _(sp):
            program(sp, sp_setup, sp_norm, sp_a, sp_adapter, sp_dense, sp_b, sp_output)

        @block.gpsimd
        def _(pool):
            program(pool, pool_setup, nothing, pool_a, pool_adapter, pool_dense, pool_b)

        @block.scalar
        def _(act):
            program(act, act_setup, act_norm, act_a, act_adapter, act_dense, act_b)

        @block.vector
        def _(dve):
            program(dve, dve_setup, dve_norm, dve_a, dve_adapter, dve_dense, dve_b)

        @block.tensor
        def _(pe):
            program(pe, pe_setup, pe_norm, pe_a, pe_adapter, pe_dense, pe_b)


def kernel(L0_attn_a_x, L0_attn_a_w_attn, L0_attn_a_w_proj, L0_attn_a_adapter_wte, L0_attn_a_gating,
           L0_attn_b_Wqk_w, L0_attn_b_Wqk_b, L0_attn_b_Wv_w, L0_attn_b_Wv_b, L0_attn_b_Wo_w, L0_attn_b_Wo_b,
           L0_ffn_W_base, L0_ffn_b_base, L0_ffn_W_router, L0_ffn_b_router, L0_ffn_lora_A, L0_ffn_lora_B):
    import numpy as np
    import concourse.bacc as bacc
    from concourse.bass_utils import run_bass_kernel_spmd

    def chunked(w_t):
        return w_t.reshape(-1, P, w_t.shape[1]).transpose(1, 0, 2)

    f32 = lambda a: np.ascontiguousarray(np.asarray(a))
    w_attn = f32(L0_attn_a_w_attn).reshape(3, G, P, CC, P)
    halves = lambda w_: f32(w_).reshape(2, HALF, CC, P).transpose(0, 3, 2, 1)
    wqk = f32(L0_attn_b_Wqk_w).reshape(P, 2, C)
    bqk = f32(L0_attn_b_Wqk_b).reshape(P, 2)
    wb = [chunked(a.T) for a in (wqk[:, 0], wqk[:, 1], f32(L0_attn_b_Wv_w))]
    lora_in = np.concatenate([f32(L0_ffn_lora_A).transpose(1, 0, 2).reshape(C, NE * R), f32(L0_ffn_W_router).T], 1)
    theta = (np.float32(1.0) / np.float32(10000.0) ** (np.arange(0, HD, 2, dtype=np.float32) / np.float32(HD))).astype(np.float32)
    angle = np.outer(theta, np.arange(T, dtype=np.float32)).astype(np.float32)
    cos_t, sin_t = np.cos(angle), np.sin(angle)
    arrays = {
        "x_in": f32(L0_attn_a_x),
        "w_qkv": w_attn.transpose(1, 0, 4, 3, 2),
        "w_proj": halves(L0_attn_a_w_proj),
        "adapter": chunked(f32(L0_attn_a_adapter_wte).T),
        "gating": f32(L0_attn_a_gating).reshape(1, 1),
        "rope_cos": np.tile(np.concatenate([cos_t, cos_t]), (4, 1)),
        "rope_sin": np.tile(np.concatenate([-sin_t, sin_t]), (4, 1)),
        "w_base": halves(L0_ffn_W_base),
        "b_base": f32(L0_ffn_b_base).reshape(1, C),
        "w_lora_in": chunked(lora_in),
        "b_router": f32(L0_ffn_b_router).reshape(NE, 1),
        "w_lora_out": f32(L0_ffn_lora_B).reshape(NE * R, C),
        "wb_qkv": np.stack(wb),
        "bb_qkv": np.stack([bqk[:, 0], bqk[:, 1], f32(L0_attn_b_Wv_b)], 1),
        "wb_out": f32(L0_attn_b_Wo_w).T.reshape(P, 2, HALF),
        "bb_out": f32(L0_attn_b_Wo_b).reshape(1, C),
    }
    nc = bacc.Bacc("TRN2", target_bir_lowering=False, num_devices=1)
    args = {}
    for name, a in arrays.items():
        arrays[name] = np.ascontiguousarray(a)
        args[name] = nc.dram_tensor(name + "_dram", a.shape, F32, kind="ExternalInput").ap()
    args["out"] = nc.dram_tensor("out_dram", (B, T, C), F32, kind="ExternalOutput").ap()
    build_program(nc, **args)
    r = run_bass_kernel_spmd(nc, [{n + "_dram": a for n, a in arrays.items()}], core_ids=[0])
    return r.results[0]["out_dram"]
```

```python
from contextlib import ExitStack

import concourse.bass as bass
from concourse import mybir

F32 = mybir.dt.float32
F32R = mybir.dt.float32r
BF16 = mybir.dt.bfloat16
ALU = mybir.AluOpType
ACT = mybir.ActivationFunctionType
AX = mybir.AxisListType

P = 128
B = 2
T = 1024
C = 1024
TT = T // P
CC = C // P
HALF = 512
NH, HD = 32, 32
G = NH * HD // P
AK = 10
NE, R = 8, 16
NHB, HDB = 8, 16
GB = NHB // 4
EPS = 1e-5
MASKED = -1e30
SCALE_A = HD ** -0.5
SCALE_ADAPTER = C ** -0.5
SCALE_B_OUT = (NHB * HDB) ** -0.5
LAG = 3
RING = 4
AH = 3
PHASES = 5
PRODUCTS = ((0, 0), (0, 1), (1, 0))


class Heads:

    def __init__(self, causal):
        if causal:
            order = ((0, 1), (1, 1), (7, 1), (0, 0), (2, 1), (6, 1), (3, 1), (2, 0), (5, 1), (4, 1), (1, 0), (3, 0))
        else:
            order = ((0, 1), *((t + h, h) for t in range(TT - 1) for h in (1, 0)), (TT - 1, 0))
        self.main = [(t, max(t * P, h * HALF) if causal else h * HALF, (h + 1) * HALF) for t, h in order]
        if causal:
            order = ((2, 0), (3, 0), (4, 0), (0, 0), (5, 0), (6, 0), (6, 1), (1, 0), (7, 0), (5, 1), (4, 1), (7, 1))
            self.max = [(t, h * HALF, min((h + 1) * HALF, (t + 1) * P), t if h == 0 else 4 + t) for t, h in order]
        else:
            self.max = [(t, h * HALF, (h + 1) * HALF, t + TT * h) for t in range(TT) for h in range(2)]
        self.causal = causal
        self.n = len(self.main)
        self.items = self.n + 1
        self.slots = 4 * self.n
        self.groups = G if causal else GB
        self.heads = 4 * self.groups
        self.pair = 1 if causal else 2
        self.lead = self.n + 6
        self.scale = SCALE_A if causal else 1.0
        self.last = [max(i for i, c in enumerate(self.main) if c[1] // HALF == h) for h in range(2)]


HA, HB = Heads(True), Heads(False)


def build_program(nc, x_in, w_qkv, w_proj, adapter, gating, rope_cos, rope_sin, w_base, b_base, w_lora_in,
                  b_router, w_lora_out, wb_qkv, bb_qkv, wb_out, bb_out, out):
    with ExitStack() as ctx:
        top = nc.sbuf_usable_end

        class Region:

            def __init__(self, start):
                self.at = start

            def __call__(self, name, shape, dtype):
                n = 2 if dtype == BF16 else 4
                for s in shape[1:]:
                    n *= s
                t = nc.alloc_sbuf_tensor_at(name, shape, dtype, offset=self.at)
                self.at += (n + 31) // 32 * 32
                assert self.at <= top, (name, self.at, top)
                return t

            def split(self, name, shape):
                return [self(f"{name}_{s}", shape, F32R) for s in ("hi", "lo")]

        def sem(name):
            return ctx.enter_context(nc.semaphore(name))

        def scratch(name, shape):
            return nc.dram_tensor(name, shape, F32, kind="Internal").ap()

        def raw(ap):
            return ap.bitcast(F32)

        keep = Region((nc.sbuf_base + 31) // 32 * 32)
        ident = keep("ident", [P, P], F32)
        ident16 = keep("ident16", [P, P], BF16)
        mask_main = keep("mask_main", [P, P], BF16)
        mask_max = keep("mask_max", [P, P], BF16)
        ak_all = keep("ak_all", [P, G, 2, 4 * AK], F32R)
        gate = keep("gate", [P, 1], F32)
        b_rout = keep("b_rout", [NE, 1], F32)
        b_qkv = keep("b_qkv", [P, 3], F32)
        xt = keep.split("xt", [P, CC, T])
        dense = Region(keep.at)
        X = dense("X", [P, TT, C], F32)
        over_w = dense.at
        w = dense.split("w", [P, CC, HALF])
        w_raw = dense("w_raw", [P, CC, HALF], F32)
        lb = dense.split("lb", [P, C])
        lb_raw = dense("lb_raw", [P, C], F32)
        la = dense.split("la", [P, CC, P + NE])
        la_raw = dense("la_raw", [P, CC, P + NE], F32)
        h_sb = dense("h_sb", [P, T], F32)
        hw = dense.split("hw", [P, T])
        bias_row = dense("bias_row", [P, C], F32)
        sp_buf = dense("sp_buf", [P, 8, TT * NE], F32)
        pairs = dense("pairs", [P, 2, TT, NE, NE], F32)
        logit_t = dense("logit_t", [NE, T], F32)
        early = Region(over_w + 3 * CC * HALF * 4)
        at_raw = early("at_raw", [P, CC, AK], F32)
        at = early.split("at", [P, CC, AK])
        akv = early("akv", [AK, 2, C], F32)
        avs = early.split("avs", [AK, C])
        zeros = early("zeros", [P, G * P], F32)
        norm = Region(dense.at)
        xn = norm("xn", [P, 2, C], F32)
        stats = norm("stats", [P, TT, 2, 6], F32)
        mv = norm("mv", [P, TT, 2], F32)
        rs = norm("rs", [P, 4, TT], F32)
        adp = Region(over_w)
        asc = adp("asc", [P, AH, T], F32)
        av = adp.split("av", [P, G, P])
        pa = adp.split("pa", [P, AH, T])
        a_e = adp("a_e", [P, 2, NH, AK], F32)
        a_s = adp("a_s", [P, 2, 4, NH], F32)
        yt_in_sb = adp("yt_in_sb", [P, 2, T], F32)
        y_sum = adp("y_sum", [P, 2, T], F32)
        att = Region(keep.at)
        prob = att("prob", [P, 3, HALF], F32)
        phl = att.split("prob", [P, 3, HALF])
        y = att("y", [P, T], F32)
        den = att("den", [P, T], F32)
        y_tmp = att("y_tmp", [32, HALF], F32)
        rot = att("rot", [P, T], F32)
        over_tables = att.at
        assert over_tables >= over_w
        cos = att("cos", [P, T], F32)
        sin = att("sin", [P, T], F32)
        wq = [att.split(f"wq{p}", [P, CC, P]) for p in range(3)]
        wq_raw = att("wq_raw", [P, CC, P], F32)
        qst = att("qst", [98, 4, T], F32R)
        kst = att("kst", [98, 4, T], F32R)
        vst = att("vst", [P, TT, 4, 96], F32R)
        ak_cur = att("ak_cur", [P, 2, 4 * AK], F32R)
        m_part = att("m_part", [P, 2, 16], F32)
        m_row = att.split("m_row", [TT, 2, P])
        d_col = att("d_col", [P, 32], F32)
        r_col = att("r_col", [P, 32], F32)
        assert att.at <= dense.at, "the layer norm's own tensors lie over projected rows only"
        src = [att.split(f"src{p}", [P, T]) for p in "qk"]
        turn = att("turn", [P, T], F32)
        vt = att("vt", [P, T], F32)
        rden = vt
        over = Region(over_tables)
        vsb = over("vsb", [P, TT, NHB, 96], F32R)
        assert over.at <= over_tables + 2 * T * 4 + 4 * CC * P * 4, "vsb must end before wq2"

        banks = ctx.enter_context(nc.psum_tensor("banks", [P, 8, HALF], F32))
        AUX = banks[:, 0:2, :].rearrange("p b n -> p (b n)")

        yt_dram = scratch("yt_dram", [B, G, P, T])
        asc_dram = scratch("asc_dram", [B, G * 4 * AK, T])
        rd_dram = scratch("rd_dram", [B, G, 4, T])
        av_dram = [scratch(f"av_dram_{s}", [P, G, P]) for s in ("hi", "lo")]
        x_dram = scratch("x_dram", [B, P, TT, C])

        phase_done = sem("phase_done")
        setup_done = sem("setup_done")
        passed = sem("passed")
        c_set = sem("c_set")
        c_in, at_in = sem("c_in"), sem("at_in")
        sw_in, sw_hi, sw_lo = sem("sw_in"), sem("sw_hi"), sem("sw_lo")
        s_mm, s_ev, s_tr, s_av = sem("s_mm"), sem("s_ev"), sem("s_tr"), sem("s_av")
        s_zero, s_avd = sem("s_zero"), sem("s_avd")
        x_ld = [sem(f"x_ld{t}") for t in range(4)]
        ln_stat, ln_scale, ln_root, ln_xn = sem("ln_stat"), sem("ln_scale"), sem("ln_root"), sem("ln_xn")
        ln_tr, ln_hi, ln_lo = sem("ln_tr"), sem("ln_hi"), sem("ln_lo")
        LN_STAT, LN_SCALE = 3, 5
        class AttentionSems:
            def __init__(self, n):
                self.max_ready, self.max_used = sem(f"{n}max_ready"), sem(f"{n}max_used")
                self.m_ready, self.mh_done = sem(f"{n}m_ready"), sem(f"{n}mh_done")
                self.aug_in = [sem(f"{n}aug_in{i}") for i in range(2)]
                self.stk_in = [sem(f"{n}stk_in{i}") for i in range(4)]
                self.st_ready, self.exp_done = sem(f"{n}st_ready"), sem(f"{n}exp_done")
                self.hi_done, self.lo_done = sem(f"{n}hi_done"), sem(f"{n}lo_done")
                self.pv_done, self.y_tmp, self.y_done = sem(f"{n}pv_done"), sem(f"{n}y_tmp"), sem(f"{n}y_done")
                self.aux, self.w_in = sem(f"{n}aux"), sem(f"{n}w_in")
                self.w_hi, self.w_lo = sem(f"{n}w_hi"), sem(f"{n}w_lo")
                self.proj_done, self.raw_in = sem(f"{n}proj_done"), sem(f"{n}raw_in")
                self.src_hi, self.src_lo = sem(f"{n}src_hi"), sem(f"{n}src_lo")
                self.v_hi, self.v_lo = sem(f"{n}v_hi"), sem(f"{n}v_lo")
                self.fill = sem(f"{n}fill")
        a_vt_in = sem("a_vt_in")
        SA, SB = AttentionSems("a_"), AttentionSems("b_")
        tab_in = sem("tab_in")
        turned, sin_done, cos_done, rope_done = sem("turned"), sem("sin_done"), sem("cos_done"), sem("rope_done")
        asc_ready, asc_in, asc_out, ak_in = sem("asc_ready"), sem("asc_in"), sem("asc_out"), sem("ak_in")
        den_in, r_done, rd_out, rden_in = sem("den_in"), sem("r_done"), sem("rd_out"), sem("rden_in")
        y_mul, yt_out = sem("y_mul"), sem("yt_out")
        by_r, by_y, by_hi, by_lo = sem("by_r"), sem("by_y"), sem("by_hi"), sem("by_lo")
        ad_in, av_in = sem("ad_in"), sem("av_in")
        ad_tr, ad_mx, ad_sub, ad_exp, ad_sum = sem("ad_tr"), sem("ad_mx"), sem("ad_sub"), sem("ad_exp"), sem("ad_sum")
        ad_rec, ad_gate, ad_p = sem("ad_rec"), sem("ad_gate"), sem("ad_p")
        ad_pt, ad_phi, ad_plo = sem("ad_pt"), sem("ad_phi"), sem("ad_plo")
        ad_yin = [sem(f"ad_yin{i}") for i in range(2)]
        ad_mm, ad_y, ad_hi, ad_lo = sem("ad_mm"), sem("ad_y"), sem("ad_hi"), sem("ad_lo")

        class DenseSems:
            def __init__(self, n, parts):
                self.w_in = [sem(f"{n}w_in{i}") for i in range(parts)]
                self.w_hi, self.w_lo = sem(f"{n}w_hi"), sem(f"{n}w_lo")
                self.tile, self.added = sem(f"{n}tile"), sem(f"{n}added")
        w_free = sem("w_free")
        SD, SO = DenseSems("d_", 4), DenseSems("o_", 1)
        ox_in, o_bias = sem("ox_in"), sem("o_bias")
        f_in = [sem(f"f_in{i}") for i in range(3)]
        f_hi, f_lo, f_h, f_hsb, f_lg = sem("f_hi"), sem("f_lo"), sem("f_h"), sem("f_hsb"), sem("f_lg")
        f_zt, f_dve, f_wt, f_hw, f_hwhi, f_hwlo = (sem(n) for n in ("f_zt", "f_dve", "f_wt", "f_hw", "f_hwhi", "f_hwlo"))
        f_bias = sem("f_bias")
        F_DVE = 14
        x_out = sem("x_out")

        def settle(eng):
            eng.sem_inc(passed, 1)

        def phase_end(eng, b, ph):
            settle(eng)
            eng.drain().then_inc(phase_done, 1)
            eng.wait_ge(phase_done, 5 * PHASES * b + 5 * (ph + 1))
            settle(eng)

        def setup_end(eng):
            eng.drain().then_inc(setup_done, 1)
            eng.wait_ge(setup_done, 5)

        def dve_norm_statistics(dve, i, t):
            n = LN_STAT * (TT * i + t)
            for h in range(2):
                last = dve.bn_stats(stats[:, t, h, :], X[:, t, h * HALF:(h + 1) * HALF])
            last.then_inc(ln_stat, 1)
            dve.wait_ge(ln_stat, n + 1)
            settle(dve)
            dve.bn_aggr(mv[:, t, :], stats[:, t, :, :].rearrange("p h s -> p (h s)")).then_inc(ln_stat, 1)
            dve.wait_ge(ln_stat, n + 2)
            dve.tensor_scalar(rs[:, 0, t:t + 1], mv[:, t, 1:2], EPS, None, ALU.add).then_inc(ln_stat, 1)

        def dve_norm_scale(dve, i, t):
            n = LN_SCALE * (TT * i + t)
            var, root, inv, tmp = (rs[:, j, t:t + 1] for j in range(4))
            dve.wait_ge(ln_root, TT * i + t + 1)
            dve.reciprocal(inv, root).then_inc(ln_scale, 1)
            dve.wait_ge(ln_scale, n + 1)
            dve.tensor_tensor(tmp, inv, inv, ALU.mult).then_inc(ln_scale, 1)
            dve.wait_ge(ln_scale, n + 2)
            dve.tensor_tensor(tmp, tmp, var, ALU.mult).then_inc(ln_scale, 1)
            dve.wait_ge(ln_scale, n + 3)
            dve.tensor_scalar(tmp, tmp, -0.5, 1.5, ALU.mult, ALU.add).then_inc(ln_scale, 1)
            dve.wait_ge(ln_scale, n + 4)
            dve.tensor_tensor(inv, inv, tmp, ALU.mult).then_inc(ln_scale, 1)
            if t >= 2:
                dve.wait_ge(ln_tr, TT * i + t - 1)
            dve.wait_ge(ln_scale, n + 5)
            dve.tensor_scalar(xn[:, t % 2, :], X[:, t, :], mv[:, t, 0:1], inv,
                              ALU.subtract, ALU.mult).then_inc(ln_xn, 1)

        def dve_norm_lo(dve, i, t):
            dve.wait_ge(ln_hi, TT * i + t + 1)
            dve.tensor_tensor(xt[1][:, :, t * P:(t + 1) * P], norm_bank(t),
                              raw(xt[0][:, :, t * P:(t + 1) * P]), ALU.subtract).then_inc(ln_lo, 1)

        def dve_norm_step(dve, i, t):
            if t < TT:
                dve_norm_statistics(dve, i, t)
            if 1 <= t <= TT:
                dve_norm_scale(dve, i, t - 1)
            if t >= 2:
                dve_norm_lo(dve, i, t - 2)

        def act_norm_step(act, i, t):
            if t < TT:
                act.wait_ge(ln_stat, LN_STAT * (TT * i + t) + 3)
                act.activation(rs[:, 1, t:t + 1], rs[:, 0, t:t + 1], ACT.Sqrt).then_inc(ln_root, 1)
            if t >= 2:
                s = t - 2
                act.wait_ge(ln_tr, TT * i + s + 1)
                act.copy(xt[0][:, :, s * P:(s + 1) * P], norm_bank(s)).then_inc(ln_hi, 1)

        def pe_norm_step(pe, i, t):
            if t < 2:
                return
            s = t - 2
            pe.wait_ge(ln_xn, TT * i + s + 1)
            if s >= 2:
                pe.wait_ge(ln_lo, TT * i + s - 1)
            for c in range(CC):
                last = pe.transpose(norm_bank(s)[:, c, :], xn[:, s % 2, c * P:(c + 1) * P], ident[:])
            last.then_inc(ln_tr, 1)

        def norm_bank(t):
            q = 2 * (t % 2)
            return banks[:, q:q + 2, :].rearrange("p b (c t) -> p (b c) t", t=P)

        def sp_norm(sp, b):
            sp_load_x(sp, x_in[b].rearrange("(t p) c -> p t c", p=P))

        def sp_load_x(sp, source):
            for q in range(4):
                sp.dma_start(X[:, 2 * q:2 * q + 2, :], source[:, 2 * q:2 * q + 2, :]).then_inc(x_ld[q], 16)

        def dve_norm(dve, b):
            for t in range(TT + 2):
                if t < TT:
                    dve.wait_ge(x_ld[t // 2], 16 * (3 * b + 1))
                dve_norm_step(dve, 4 * b, t)

        def act_norm(act, b):
            for t in range(TT + 2):
                act_norm_step(act, 4 * b, t)

        def pe_norm(pe, b):
            for t in range(TT + 2):
                pe_norm_step(pe, 4 * b, t)

        def main_bank(k):
            return banks[:, 4 + k % 2, :]

        def max_index(H, j, i, first):
            if i == 0:
                return 0 if first and j == 0 else H.items * j - 1
            return H.items * j + i

        def turn_index(H, j, last):
            return H.items * j - (1 if last and j == 4 else 0)

        def max_bank(i):
            return banks[:, 2 + i % 2, :]

        def pe_max(pe, H, S, b, g, v, first=False, last=False):
            j, i = divmod(v, H.n)
            if last and v > H.slots + 1:
                return
            if i == 1 and not (first and v == 1):
                n = turn_index(H, j, last)
                pe.wait_ge(S.m_ready, H.heads * b + 4 * g + j)
                pe.wait_ge(S.max_used, H.items * (H.heads * b + 4 * g) + n - 1)
                pe.transpose(max_bank(n)[0:TT, 0:P], m_part[:, (j - 1) % 2, 0:TT], ident[:]).then_inc(S.max_ready, 1)
            if last and j >= 4:
                return
            n = max_index(H, j, i, first)
            if i == 0:
                pe.wait_ge(S.stk_in[j % 4], 96 * (H.groups * b + g + j // 4 + 1))
            if not (first and n < 2):
                pe.wait_ge(S.max_used, H.items * (H.heads * b + 4 * g) + n - 1)
            qt, k0, k1, _ = H.max[i]
            diag = H.causal and k1 == (qt + 1) * P
            bank = max_bank(n)
            mm = pe.matmul(bank[:, 0:k1 - k0], qst[0:96, j % 4, qt * P:(qt + 1) * P], kst[0:96, j % 4, k0:k1],
                           start=True, stop=True)
            if diag:
                mm = pe.matmul(bank[:, k1 - k0 - P:k1 - k0], ident16[:], mask_max[:], start=False, stop=True,
                               skip_group_check=True)
            mm.then_inc(S.max_ready, 1)

        def dve_max(dve, H, S, b, g, v, first=False, last=False):
            j, i = divmod(v, H.n)
            if last and v > H.slots + 1:
                return
            hb = H.heads * b + 4 * g
            if i == 1 and not (first and v == 1):
                n, h = turn_index(H, j, last), j - 1
                dve.wait_ge(S.max_ready, H.items * hb + n + 1)
                if not (first and h < 2):
                    dve.wait_ge(S.aug_in[h % 2], 32 * (H.heads // 2 * b + 2 * g + h // 2))
                bank = max_bank(n)[0:TT, 0:P]
                dve.tensor_scalar(m_row[0][:, h % 2, :], bank, -1.0, None, ALU.mult).then_inc(S.mh_done, 1)
                dve.wait_ge(S.mh_done, hb + h + 1)
                dve.scalar_tensor_tensor(out=m_row[1][:, h % 2, :], in0=bank, scalar=-1.0,
                                         in1=raw(m_row[0][:, h % 2, :]), op0=ALU.mult,
                                         op1=ALU.subtract).then_inc(S.max_used, 1)
            if last and j >= 4:
                return
            n = max_index(H, j, i, first)
            _, k0, k1, col = H.max[i]
            dve.wait_ge(S.max_ready, H.items * hb + n + 1)
            dve.tensor_reduce(m_part[:, j % 2, col:col + 1], max_bank(n)[:, 0:k1 - k0], AX.X,
                              ALU.max).then_inc(S.max_used, 1)
            if i == H.n - 1:
                lo, n2 = (4, 4) if H.causal else (0, TT)
                dve.wait_ge(S.max_used, H.items * hb + n + 1)
                dve.tensor_tensor(m_part[:, j % 2, lo:lo + n2], m_part[:, j % 2, lo:lo + n2],
                                  m_part[:, j % 2, 8:8 + n2], ALU.max).then_inc(S.m_ready, 1)

        def sp_max_rows(sp, H, S, b, g, h, last=False):
            sp.wait_ge(S.max_used, H.items * (H.heads * b + 4 * g) + turn_index(H, h + 1, last) + 1)
            settle(sp)
            for s in range(2):
                sp.dma_start(raw(qst[96 + s:97 + s, h % 4, :]), raw(m_row[s][:, h % 2, :])).then_inc(S.aug_in[h % 2], 16)

        def sp_stack(sp, H, S, b, g, h, first=False):
            width = HD if H.causal else HDB
            at_row = h * width if H.causal else (4 * g + h) * width
            rows = slice(at_row, at_row + width)
            if H.causal:
                sp.wait_ge(S.src_lo, 2 * H.groups * b + 2 * g + 2)
            else:
                sp.wait_ge(S.src_lo, 2 * b + 2)
            if not first:
                settle(sp)
                sp.wait_ge(S.pv_done, H.slots * (H.groups * b + g - 1) + H.n * (h + 1))
            settle(sp)
            for stack, part, order in ((qst, 0, (0, 1, 0)), (kst, 1, (0, 0, 1))):
                for i, s in enumerate(order):
                    sp.dma_start(raw(stack[32 * i:32 * i + width, h, :]),
                                 raw(src[part][s][rows, :])).then_inc(S.stk_in[h], 16)

        def pe_scores(pe, H, S, b, g, k, first=False):
            j, c = divmod(k, H.n)
            u = H.slots * (H.groups * b + g) + k
            if c == 0:
                pe.wait_ge(S.aug_in[j % 2], 32 * (H.heads // 2 * b + 2 * g + j // 2 + 1))
            if not (first and k < 2):
                pe.wait_ge(S.exp_done, u - 1)
            kt, q0, q1 = H.main[c]
            diag = H.causal and q0 == kt * P
            bank = main_bank(k)
            mm = pe.matmul(bank[:, 0:q1 - q0], kst[:, j % 4, kt * P:(kt + 1) * P], qst[:, j % 4, q0:q1],
                           start=True, stop=True)
            if diag:
                mm = pe.matmul(bank[:, 0:P], ident16[:], mask_main[:], start=False, stop=True, skip_group_check=True)
            mm.then_inc(S.st_ready, 1)

        def act_exp(act, H, S, b, g, k, ring, first=False):
            kt, q0, q1 = H.main[k % H.n]
            u = H.slots * (H.groups * b + g) + k
            act.wait_ge(S.st_ready, u + 1)
            if not (first and k < 3):
                act.wait_ge(S.lo_done, u - 2)
            act.activation(prob[:, (ring + k) % 3, 0:q1 - q0], main_bank(k)[:, 0:q1 - q0], ACT.Exp,
                           scale=H.scale).then_inc(S.exp_done, 1)

        def act_hi(act, H, S, b, g, k, ring, first=False):
            kt, q0, q1 = H.main[k % H.n]
            u = H.slots * (H.groups * b + g) + k
            act.wait_ge(S.exp_done, u + 1)
            if not (first and k < 3):
                act.wait_ge(S.pv_done, u - 2)
            act.copy(phl[0][:, (ring + k) % 3, 0:q1 - q0], prob[:, (ring + k) % 3, 0:q1 - q0]).then_inc(S.hi_done, 1)

        def dve_lo(dve, H, S, b, g, k, ring):
            kt, q0, q1 = H.main[k % H.n]
            u = H.slots * (H.groups * b + g) + k
            dve.wait_ge(S.hi_done, u + 1)
            dve.tensor_tensor(phl[1][:, (ring + k) % 3, 0:q1 - q0], prob[:, (ring + k) % 3, 0:q1 - q0],
                              raw(phl[0][:, (ring + k) % 3, 0:q1 - q0]), ALU.subtract).then_inc(S.lo_done, 1)

        def pe_pv(pe, H, S, b, g, k, ring, first=False):
            if k < 0:
                g, k, ring = g - 1, k + H.slots, ring - H.slots
            j, c = divmod(k, H.n)
            kt, q0, q1 = H.main[c]
            half = q0 // HALF
            u = H.slots * (H.groups * b + g) + k
            pe.wait_ge(S.lo_done, u + 1)
            if H.causal:
                v_stat = vst[:, kt, j, :]
                if c == 0 and j in (0, 3):
                    pe.wait_ge(S.v_lo, 2 * (H.groups * b + g) + (1 if j == 0 else 2))
            else:
                v_stat = vsb[:, kt, 4 * g + j, :]
            if kt == 0 and j % H.pair == 0 and not (first and j == 0):
                pe.wait_ge(S.y_done, y_index(H, b, g, j, half) - 1)
            for s in range(2):
                mm = pe.matmul(banks[0:96, 6 + half, q0 - half * HALF:q1 - half * HALF], v_stat,
                               phl[s][:, (ring + k) % 3, 0:q1 - q0], start=(kt == 0 and s == 0 and j % H.pair == 0),
                               stop=True,
                               skip_group_check=True)
            mm.then_inc(S.pv_done, 1)

        def y_index(H, b, g, j, half):
            per = H.heads // H.pair
            return 2 * (per * b + 4 // H.pair * g + j // H.pair) + 1 - half

        def act_y(act, H, S, b, g, j, half, first=False):
            n = y_index(H, b, g, j, half)
            act.wait_ge(S.pv_done, H.slots * (H.groups * b + g) + H.n * j + H.last[half] + 1)
            if not (first and j // H.pair == 0 and half == 1):
                act.wait_ge(S.y_done, n)
            row = 32 * (j % 4) if H.causal else 32 * ((4 * g + j) // 2)
            act.copy(y_tmp[:], banks[32:64, 6 + half, :])
            act.copy(den[row:row + 32, half * HALF:(half + 1) * HALF], banks[64:96, 6 + half, :]).then_inc(S.y_tmp, 1)

        def dve_y(dve, H, S, b, g, j, half):
            n = y_index(H, b, g, j, half)
            dve.wait_ge(S.y_tmp, n + 1)
            row = 32 * (j % 4) if H.causal else 32 * ((4 * g + j) // 2)
            dve.tensor_tensor(y[row:row + 32, half * HALF:(half + 1) * HALF], banks[0:32, 6 + half, :], y_tmp[:],
                              ALU.add).then_inc(S.y_done, 1)

        def pe_project(part):
            for c in range(CC):
                for a, x in PRODUCTS:
                    for h in range(2):
                        yield (AUX[:, h * HALF:(h + 1) * HALF], wq[part][a][:, c, :],
                               xt[x][:, c, h * HALF:(h + 1) * HALF], c == 0 and (a, x) == (0, 0),
                               c == CC - 1 and (a, x) == PRODUCTS[-1])

        Q_SLOTS, K_SLOTS, V_SLOTS = range(3, 11), range(12, 19), range(21, 29)
        COPY_OUT = (11, 19, 29, 37)
        ROPE_DVE, ROPE_HI = (12, 21), (15, 24)
        ADAPTER, TURN_V = 36, 40
        Y_CHUNK = ((1, 0), (0, 2))
        RECIPROCALS = 5
        WEIGHTS, STACKS = (18, 32, 37), (26, 27, 38, 1)
        DENOMINATORS, STORE, ADAPTER_STORE = 4, 12, 39
        PROJECTION = 6 * CC

        def pe_a_part(pe, b, g, p, first=False):
            pe.wait_ge(SA.w_lo, 3 * G * b + 3 * g + p + 1)
            if p == 0:
                if not first:
                    pe.wait_ge(SA.v_lo, 2 * (G * b + g))
            else:
                pe.wait_ge(SA.raw_in, 2 * G * b + 2 * g + p)

        def pe_a_adapter(pe, b, g):
            pe.wait_ge(ak_in, G * b + g + 1)
            pe.wait_ge(SA.src_lo, 2 * G * b + 2 * g + 1)
            pe.wait_ge(a_vt_in, G * b + g + 1)
            for h in range(2):
                for n, (a, x) in enumerate(PRODUCTS):
                    mm = pe.matmul(AUX[0:4 * AK, h * HALF:(h + 1) * HALF], ak_cur[:, a, :],
                                   src[0][x][:, h * HALF:(h + 1) * HALF], start=n == 0, stop=n == 2)
            mm.then_inc(asc_ready, 1)

        def dve_a_adapter_keys(dve, b, g, first=False):
            dve.wait_ge(asc_ready, G * b + g)
            dve.tensor_copy(ak_cur[:], raw(ak_all[:, g, :, :])).then_inc(ak_in, 1)

        def pe_a_values(pe, b, g):
            pe.wait_ge(asc_in, G * b + g + 1)
            for t in range(TT):
                mm = pe.transpose(AUX[:, t * P:(t + 1) * P], vt[:, t * P:(t + 1) * P], ident[:])
            mm.then_inc(SA.aux, 1)

        def turned_values(part):
            heads = slice(0, 3) if part == 0 else slice(3, 4)
            return heads, AUX.rearrange("p (t j d) -> p t j d", t=TT, d=HD)[:, :, heads, :]

        def act_a_values(act, b, g, part, first=False):
            act.wait_ge(SA.aux, G * b + g + 1)
            if not first:
                act.wait_ge(SA.pv_done, HA.slots * (G * b + g - 1) + HA.n * (3 + part))
            if part:
                act.wait_ge(SA.v_lo, 2 * (G * b + g) + 1)
            heads, values = turned_values(part)
            act.copy(vst[:, :, heads, 0:HD], values).then_inc(SA.v_hi, 1)

        def dve_a_values(dve, b, g, part):
            dve.wait_ge(SA.v_hi, 2 * (G * b + g) + part + 1)
            heads, values = turned_values(part)
            dve.tensor_tensor(vst[:, :, heads, HD:2 * HD], values, raw(vst[:, :, heads, 0:HD]),
                              ALU.subtract).then_inc(SA.v_lo, 1)

        def act_a_copy_out(act, b, g, p, first=False):
            if p < 3:
                act.wait_ge(SA.proj_done, 3 * G * b + 3 * g + p + 1)
            else:
                act.wait_ge(asc_ready, G * b + g + 1)
            if p == 2:
                if not first:
                    act.wait_ge(yt_out, 16 * (G * b + g - 1))
                act.copy(vt[:], AUX).then_inc(a_vt_in, 1)
                return
            if p == 0:
                act.wait_ge(asc_out, 16 * (G * b + g))
                act.copy(turn[:], AUX).then_inc(SA.raw_in, 1)
            elif p == 1:
                act.wait_ge(SA.src_lo, 2 * G * b + 2 * g + 1)
                act.copy(turn[:], AUX).then_inc(SA.raw_in, 1)
            else:
                act.wait_ge(SA.src_lo, 2 * G * b + 2 * g + 2)
                act.copy(turn[0:4 * AK, :], AUX[0:4 * AK, :]).then_inc(asc_in, 1)

        def act_a_rope_hi(act, b, g, p):
            act.wait_ge(rope_done, 2 * G * b + 2 * g + p + 1)
            act.wait_ge(SA.stk_in[3], 96 * (G * b + g))
            act.copy(src[p][0][:], turn[:]).then_inc(SA.src_hi, 1)

        def dve_a_rope(dve, b, g, p):
            n = 2 * G * b + 2 * g + p
            dve.wait_ge(SA.raw_in, n + 1)
            dve.wait_ge(rope_done, n)
            settle(dve)
            dve.stream_shuffle(rot[:], turn[:], [(i + HD // 2) % HD for i in range(HD)]).then_inc(turned, 1)
            dve.wait_ge(turned, n + 1)
            dve.tensor_tensor(rot[:], rot[:], sin[:], ALU.mult).then_inc(sin_done, 1)

        def a_rope(eng, b, g, p):
            n = 2 * G * b + 2 * g + p
            eng.wait_ge(turned, n + 1)
            eng.tensor_tensor(turn[:], turn[:], cos[:], ALU.mult).then_inc(cos_done, 1)
            eng.wait_ge(cos_done, n + 1)
            eng.wait_ge(sin_done, n + 1)
            eng.tensor_tensor(turn[:], turn[:], rot[:], ALU.add).then_inc(rope_done, 1)
            eng.wait_ge(SA.src_hi, n + 1)
            eng.tensor_tensor(src[p][1][:], turn[:], raw(src[p][0][:]), ALU.subtract).then_inc(SA.src_lo, 1)

        def sp_a_weights(sp, b, g, p):
            n = 3 * G * b + 3 * g + p
            sp.wait_ge(SA.w_lo, n)
            settle(sp)
            sp.dma_start(wq_raw[:], w_qkv[g, p]).then_inc(SA.w_in, 16)

        def pool_a_weights(pool, b, g, p, first=False):
            n = 3 * G * b + 3 * g + p
            pool.wait_ge(SA.w_in, 16 * n + 16)
            if not first:
                pool.wait_ge(SA.proj_done, n - 2)
            settle(pool)
            pool.tensor_copy(wq[p][0][:], wq_raw[:]).then_inc(SA.w_hi, 1)
            pool.wait_ge(SA.w_hi, n + 1)
            pool.tensor_tensor(wq[p][1][:], wq_raw[:], raw(wq[p][0][:]), ALU.subtract).then_inc(SA.w_lo, 1)

        def sp_a_result_denominators(sp, b, g):
            n = G * b + g
            sp.wait_ge(SA.y_done, 8 * n + 8)
            settle(sp)
            sp.dma_start(d_col[:], den[0:P:32, :]).then_inc(den_in, 16)
            sp.wait_ge(r_done, n + 1)
            settle(sp)
            sp.dma_start(rd_dram[b, g], r_col[:]).then_inc(rd_out, 16)
            sp.wait_ge(rd_out, 16 * n + 16)
            settle(sp)
            sp.wait_ge(yt_out, 16 * n)
            settle(sp)
            for j in range(4):
                sp.dma_start(rden[32 * j:32 * j + 32, :],
                             rd_dram[b, g, j:j + 1, :].broadcast_to([32, T])).then_inc(rden_in, 16)

        def dve_a_result_reciprocals(dve, b, g):
            n = G * b + g
            dve.wait_ge(den_in, 16 * n + 16)
            dve.wait_ge(rd_out, 16 * n)
            dve.reciprocal(r_col[:], d_col[:]).then_inc(r_done, 1)

        def pool_a_result(pool, b, g):
            n = G * b + g
            pool.wait_ge(rden_in, 64 * n + 64)
            pool.tensor_tensor(rden[:], y[:], rden[:], ALU.mult).then_inc(y_mul, 1)

        def sp_a_result_store(sp, b, g):
            n = G * b + g
            sp.wait_ge(y_mul, n + 1)
            settle(sp)
            sp.dma_start(yt_dram[b, g], rden[:]).then_inc(yt_out, 16)

        def sp_a_adapter_store(sp, b, g):
            sp.wait_ge(asc_in, G * b + g + 1)
            settle(sp)
            sp.dma_start(asc_dram[b, bass.ts(g, 4 * AK), :], turn[0:4 * AK, :]).then_inc(asc_out, 16)

        def pe_a_group(pe, b, g, first, more):
            parts = []
            if more >= 1:
                parts = [(slots, p, pe_project(p)) for slots, p in ((Q_SLOTS, 0), (K_SLOTS, 1), (V_SLOTS, 2))]
            for k in range(HA.slots):
                if k + 1 < HA.slots or more:
                    pe_scores(pe, HA, SA, b, g, k + 1)
                pe_max(pe, HA, SA, b, g, k + HA.lead, last=not more)
                for slots, p, products in parts:
                    if k not in slots:
                        continue
                    if k == slots[0]:
                        pe_a_part(pe, b, g + 1, p)
                    at, n = slots.index(k), len(slots)
                    for _ in range(PROJECTION * at // n, PROJECTION * (at + 1) // n):
                        o, a, x, start, stop = next(products)
                        mm = pe.matmul(o, a, x, start=start, stop=stop)
                    if k == slots[-1]:
                        mm.then_inc(SA.proj_done, 1)
                if k == ADAPTER and more:
                    pe_a_adapter(pe, b, g + 1)
                if k == TURN_V and more:
                    pe_a_values(pe, b, g + 1)
                if k > 1 or not first:
                    pe_pv(pe, HA, SA, b, g, k - 2, 0, first)

        def act_a_group(act, b, g, first, more):
            for k in range(HA.slots):
                if k + 1 < HA.slots or more:
                    act_exp(act, HA, SA, b, g, k + 1, 0, first)
                act_hi(act, HA, SA, b, g, k, 0, first)
                for at_k, p in zip(COPY_OUT, range(4)):
                    if k == at_k and more:
                        act_a_copy_out(act, b, g + 1, p, first)
                j, c = divmod(k, HA.n)
                for half, at_c in Y_CHUNK:
                    if c == at_c and j > 0:
                        if j == 1 and half == 1 and not first:
                            act.wait_ge(den_in, 16 * (G * b + g))
                        act_y(act, HA, SA, b, g, j - 1, half, first)
                    elif c == at_c and not first:
                        act_y(act, HA, SA, b, g - 1, 3, half)
                if k == 1 and not first:
                    act_a_values(act, b, g, 1)
                if k == TURN_V + 1 and more:
                    act_a_values(act, b, g + 1, 0)
                if more:
                    for at_k, p in zip(ROPE_HI, range(2)):
                        if k == at_k:
                            act_a_rope_hi(act, b, g + 1, p)

        def dve_a_group(dve, b, g, first, more):
            for k in range(HA.slots):
                dve_max(dve, HA, SA, b, g, k + HA.lead, last=not more)
                dve_lo(dve, HA, SA, b, g, k, 0)
                j, c = divmod(k, HA.n)
                for half, at_c in Y_CHUNK:
                    if c == at_c and j > 0:
                        if j == 1 and half == 1 and not first:
                            dve.wait_ge(y_mul, G * b + g)
                        dve_y(dve, HA, SA, b, g, j - 1, half)
                    elif c == at_c and not first:
                        dve_y(dve, HA, SA, b, g - 1, 3, half)
                if k == 1 and not first:
                    dve_a_values(dve, b, g, 1)
                if k == TURN_V + 1 and more:
                    dve_a_values(dve, b, g + 1, 0)
                if k == RECIPROCALS and not first:
                    dve_a_result_reciprocals(dve, b, g - 1)
                if more:
                    if k in ROPE_DVE:
                        dve_a_rope(dve, b, g + 1, ROPE_DVE.index(k))
                    if k == 30:
                        dve_a_adapter_keys(dve, b, g + 1)

        def pool_a_group(pool, b, g, first, more):
            if not first:
                pool_a_result(pool, b, g - 1)
            for p in range(2):
                if more:
                    a_rope(pool, b, g + 1, p)
            for p in range(3):
                if more >= 2:
                    pool_a_weights(pool, b, g + 2, p)

        def sp_a_group(sp, b, g, first, more):
            for k in range(HA.slots):
                if k in WEIGHTS and more >= 2:
                    sp_a_weights(sp, b, g + 2, WEIGHTS.index(k))
                if k == STACKS[3]:
                    sp_stack(sp, HA, SA, b, g, 3, first)
                if k == DENOMINATORS and not first:
                    sp_a_result_denominators(sp, b, g - 1)
                if k == STORE and not first:
                    sp_a_result_store(sp, b, g - 1)
                if k in STACKS[:3] and more:
                    sp_stack(sp, HA, SA, b, g + 1, STACKS.index(k))
                if (k + 5) % HA.n == 0 and ((k + 5) // HA.n < 4 or more):
                    sp_max_rows(sp, HA, SA, b, g, (k + 5) // HA.n, last=not more)
                if k == ADAPTER_STORE and more:
                    sp_a_adapter_store(sp, b, g + 1)

        def groups(eng, b, body):
            body(eng, b, 0, True, G - 1)
            with eng.Fori(1, G - 2) as g:
                body(eng, b, g, False, 2)
            body(eng, b, G - 2, False, 1)
            body(eng, b, G - 1, False, 0)

        def sp_a(sp, b):
            for p in range(3):
                sp_a_weights(sp, b, 0, p)
                if p == 0:
                    sp.dma_start(cos[:], rope_cos).then_inc(tab_in, 16)
                    sp.dma_start(sin[:], rope_sin).then_inc(tab_in, 16)
            for h in range(3):
                sp_stack(sp, HA, SA, b, 0, h, first=True)
            sp_a_weights(sp, b, 1, 0)
            sp_a_adapter_store(sp, b, 0)
            sp_max_rows(sp, HA, SA, b, 0, 0)
            for p in (1, 2):
                sp_a_weights(sp, b, 1, p)
            groups(sp, b, sp_a_group)
            sp_a_result_denominators(sp, b, G - 1)
            sp_a_result_store(sp, b, G - 1)
            sp.wait_ge(yt_out, 16 * (G * b + G))
            settle(sp)
            sp.wait_ge(asc_out, 16 * (G * b + G))

        def pool_a(pool, b):
            pool.memset(raw(kst[96:98, :, :]), 1.0).then_inc(SA.fill, 1)
            pool.wait_ge(SA.fill, 2 * b + 1)
            settle(pool)
            pool.memset(raw(vst[:, :, :, 2 * HD:3 * HD]), 1.0).then_inc(SA.fill, 1)
            for p in range(3):
                pool_a_weights(pool, b, 0, p, first=True)
            for p in range(3):
                pool_a_weights(pool, b, 1, p)
            groups(pool, b, pool_a_group)
            pool_a_result(pool, b, G - 1)

        def pe_a(pe, b):
            pe.wait_ge(ln_lo, TT * (4 * b + 1))
            for p in range(3):
                pe_a_part(pe, b, 0, p, first=True)
                for o, a, x, start, stop in pe_project(p):
                    mm = pe.matmul(o, a, x, start=start, stop=stop)
                mm.then_inc(SA.proj_done, 1)
            pe_a_adapter(pe, b, 0)
            pe_a_values(pe, b, 0)
            pe.wait_ge(SA.fill, 2 * b + 2)
            for v in range(HA.lead):
                pe_max(pe, HA, SA, b, 0, v, first=True)
            pe_scores(pe, HA, SA, b, 0, 0, first=True)
            groups(pe, b, pe_a_group)
            for k in (-2, -1):
                pe_pv(pe, HA, SA, b, G, k, 0)

        def act_a(act, b):
            act_a_copy_out(act, b, 0, 0)
            act_a_rope_hi(act, b, 0, 0)
            act_a_copy_out(act, b, 0, 1)
            act_a_rope_hi(act, b, 0, 1)
            act_a_copy_out(act, b, 0, 2, first=True)
            act_a_copy_out(act, b, 0, 3)
            for part in range(2):
                act_a_values(act, b, 0, part, first=True)
            act_exp(act, HA, SA, b, 0, 0, 0, first=True)
            groups(act, b, act_a_group)
            for half in (1, 0):
                act_y(act, HA, SA, b, G - 1, 3, half)

        def dve_a(dve, b):
            dve.wait_ge(tab_in, 32 * b + 32)
            for p in range(2):
                dve_a_rope(dve, b, 0, p)
                a_rope(dve, b, 0, p)
            dve_a_adapter_keys(dve, b, 0)
            for part in range(2):
                dve_a_values(dve, b, 0, part)
            for v in range(HA.lead):
                dve_max(dve, HA, SA, b, 0, v, first=True)
            groups(dve, b, dve_a_group)
            for half in (1, 0):
                dve_y(dve, HA, SA, b, G - 1, 3, half)
            dve_a_result_reciprocals(dve, b, G - 1)

        CH_ROWS = [min(3, G - 3 * c) * 4 * AK for c in range(AH)]

        def sp_adapter(sp, b):
            for c in range(AH):
                sp.dma_start(asc[0:CH_ROWS[c], c, :],
                             asc_dram[b, 12 * AK * c:12 * AK * c + CH_ROWS[c], :]).then_inc(ad_in, 16)
            for s in range(2):
                sp.dma_start(raw(av[s][:]), av_dram[s]).then_inc(av_in, 16)
            for g in range(G):
                if g >= 2:
                    sp.wait_ge(ad_y, G * b + g - 1)
                    settle(sp)
                sp.dma_start(yt_in_sb[:, g % 2, :], yt_dram[b, g]).then_inc(ad_yin[g % 2], 16)

        def pe_adapter(pe, b):
            pe.wait_ge(ad_in, 48 * b + 48)
            for t in range(TT + 1):
                if t < TT:
                    if t >= 2:
                        pe.wait_ge(ad_sub, TT * b + t - 1)
                    for c in range(AH):
                        mm = pe.transpose(banks[:, t % 2, 12 * AK * c:12 * AK * c + CH_ROWS[c]],
                                          asc[0:CH_ROWS[c], c, t * P:(t + 1) * P], ident[0:CH_ROWS[c], 0:CH_ROWS[c]])
                    mm.then_inc(ad_tr, 1)
                if t >= 1:
                    s = t - 1
                    pe.wait_ge(ad_p, TT * b + s + 1)
                    if s >= 2:
                        pe.wait_ge(ad_plo, TT * b + s - 1)
                    p_tile = a_e[:, s % 2, :, :].rearrange("p h k -> p (h k)")
                    for c in range(AH):
                        mm = pe.transpose(banks[0:CH_ROWS[c], 2 + s % 2, c * P:(c + 1) * P],
                                          p_tile[:, 12 * AK * c:12 * AK * c + CH_ROWS[c]], ident[:])
                    mm.then_inc(ad_pt, 1)
            pe.wait_ge(av_in, 32 * b + 32)
            pe.wait_ge(ad_plo, TT * b + TT)
            for g in range(G):
                c, rows = g // 3, CH_ROWS[g // 3]
                if g >= 2:
                    pe.wait_ge(ad_y, G * b + g - 1)
                for h in range(2):
                    for n, (a, x) in enumerate(PRODUCTS):
                        mm = pe.matmul(banks[:, 4 + 2 * (g % 2) + h, :], av[a][0:rows, g, :],
                                       pa[x][0:rows, c, h * HALF:(h + 1) * HALF], start=n == 0, stop=n == 2)
                mm.then_inc(ad_mm, 1)

        def dve_adapter(dve, b):
            for t in range(TT):
                n = TT * b + t
                s_bank = banks[:, t % 2, 0:NH * AK].rearrange("p (h k) -> p h k", k=AK)
                e, st = a_e[:, t % 2, :, :], [a_s[:, t % 2, i, :] for i in range(4)]
                dve.wait_ge(ad_tr, n + 1)
                dve.tensor_reduce(st[0], s_bank, AX.X, ALU.max).then_inc(ad_mx, 1)
                dve.wait_ge(ad_mx, n + 1)
                if t >= 2:
                    dve.wait_ge(ad_pt, n - 1)
                dve.tensor_tensor(e, s_bank, st[0].unsqueeze(2).broadcast_to([P, NH, AK]),
                                  ALU.subtract).then_inc(ad_sub, 1)
                dve.wait_ge(ad_exp, n + 1)
                dve.tensor_reduce(st[1], e, AX.X, ALU.add).then_inc(ad_sum, 1)
                dve.wait_ge(ad_sum, n + 1)
                dve.reciprocal(st[2], st[1]).then_inc(ad_rec, 1)
                dve.wait_ge(ad_rec, n + 1)
                dve.tensor_scalar(st[3], st[2], gate[:, 0:1], None, ALU.mult).then_inc(ad_gate, 1)
                dve.wait_ge(ad_gate, n + 1)
                dve.tensor_tensor(e, e, st[3].unsqueeze(2).broadcast_to([P, NH, AK]), ALU.mult).then_inc(ad_p, 1)
                if t >= 1:
                    dve_adapter_lo(dve, b, t - 1)
            dve_adapter_lo(dve, b, TT - 1)
            for g in range(G):
                dve.wait_ge(ad_mm, G * b + g + 1)
                dve.wait_ge(ad_yin[g % 2], 16 * (G // 2 * b + g // 2 + 1))
                if g >= 2:
                    dve.wait_ge(ad_lo, G * b + g - 1)
                q = 4 + 2 * (g % 2)
                dve.tensor_tensor(y_sum[:, g % 2, :], banks[:, q:q + 2, :].rearrange("p b n -> p (b n)"),
                                  yt_in_sb[:, g % 2, :], ALU.add).then_inc(ad_y, 1)

        def adapter_views(t, which):
            r = CH_ROWS[0]
            full = (banks[0:r, 2 + t % 2, 0:2 * P].rearrange("p (c t) -> p c t", c=2),
                    pa[which][0:r, 0:2, t * P:(t + 1) * P])
            r = CH_ROWS[2]
            short = (banks[0:r, 2 + t % 2, 2 * P:3 * P], pa[which][0:r, 2, t * P:(t + 1) * P])
            return full, short

        def dve_adapter_lo(dve, b, t):
            dve.wait_ge(ad_phi, TT * b + t + 1)
            for (bank, lo), (_, hi) in zip(adapter_views(t, 1), adapter_views(t, 0)):
                last = dve.tensor_tensor(lo, bank, raw(hi), ALU.subtract)
            last.then_inc(ad_plo, 1)

        def act_adapter(act, b):
            for t in range(TT):
                n = TT * b + t
                e = a_e[:, t % 2, :, :]
                act.wait_ge(ad_sub, n + 1)
                act.activation(e, e, ACT.Exp, scale=SCALE_ADAPTER).then_inc(ad_exp, 1)
                act.wait_ge(ad_pt, n + 1)
                for bank, hi in adapter_views(t, 0):
                    last = act.copy(hi, bank)
                last.then_inc(ad_phi, 1)
            for g in range(G):
                act.wait_ge(ad_y, G * b + g + 1)
                act.copy(xt[0][:, g, :], y_sum[:, g % 2, :]).then_inc(ad_hi, 1)

        def pool_adapter(pool, b):
            for g in range(G):
                pool.wait_ge(ad_hi, G * b + g + 1)
                pool.tensor_tensor(xt[1][:, g, :], y_sum[:, g % 2, :], raw(xt[0][:, g, :]),
                                   ALU.subtract).then_inc(ad_lo, 1)

        class Dense:
            def __init__(self, name, b, f=0):
                self.ffn = name == "ffn"
                self.wide = name != "wo"
                self.S = SD if self.wide else SO
                self.cc = CC if self.wide else 1
                self.parts = 4 if self.wide else 1
                self.loads = 2 if self.wide else 1
                self.i = 3 * b + (0 if name == "proj" else 1 + f) if self.wide else b
                self.f, self.f0 = 2 * b + f, f
                self.dram = {"proj": w_proj, "ffn": w_base, "wo": wb_out}[name]
                self.name = name
                self.norm = {"proj": 4 * b + 1, "wo": 4 * b + 3, "ffn": 4 * b + 2 if f == 0 else None}[name]

            def finished(self, i):
                return (() if i < LAG else range(LAG + 1) if i == LAG else (i,)) if self.ffn else (i,)

            def chunks(self, part, s=None):
                if not self.wide:
                    return (h_sb if s is None else hw[s])[:].rearrange("p (o n) -> p o n", o=2)
                t = w_raw if s is None else w[s]
                return t[:, 2 * part:2 * part + 2, :]

            def weights(self, s, c, o):
                return w[s][:, c, :] if self.wide else hw[s][:, o * HALF:(o + 1) * HALF]

            def load_index(self, o):
                return self.loads * self.i + o

        def sp_dense_weights(sp, d, o, first=False):
            for q in range(d.parts):
                if not first:
                    sp.wait_ge(d.S.w_lo, d.parts * (d.load_index(o) - 1) + q + 1)
                    settle(sp)
                src_ap = d.dram[o, :, 2 * q:2 * q + 2, :] if d.wide else d.dram
                sp.dma_start(d.chunks(q), src_ap).then_inc(d.S.w_in[q], 16)

        def sp_dense(sp, b, d):
            if d.name == "proj":
                sp_dense_weights(sp, d, 0, first=True)
                sp_load_x(sp, x_in[b].rearrange("(t p) c -> p t c", p=P))
                sp_lora(sp)
                sp.dma_start(bias_row[:], b_base.broadcast_to([P, C])).then_inc(f_in[2], 16)
                sp_dense_weights(sp, d, 1)
            elif d.name == "wo":
                sp_dense_weights(sp, d, 0, first=True)
                sp.dma_start(bias_row[:], bb_out.broadcast_to([P, C])).then_inc(ox_in, 16)
                sp_load_x(sp, x_dram[b])
                sp_lora(sp)
                sp_dense_weights(sp, Dense("ffn", b, 1), 0)
                sp.wait_ge(o_bias, TT * (b + 1))
                settle(sp)
                sp.dma_start(bias_row[:], b_base.broadcast_to([P, C])).then_inc(f_in[2], 16)
            else:
                if d.f0 == 0:
                    sp_dense_weights(sp, d, 0)
                sp_dense_weights(sp, d, 1)
                for t in range(TT):
                    sp.wait_ge(SD.added, 2 * TT * d.i + TT + t + 1)
                    settle(sp)
                    to = x_dram[b, :, t, :] if d.f0 == 0 else out[b, t * P:(t + 1) * P, :]
                    sp.dma_start(to, X[:, t, :]).then_inc(x_out, 16)
                sp.wait_ge(x_out, 16 * TT * (d.f + 1))

        def sp_lora(sp):
            sp.dma_start(la_raw[:], w_lora_in).then_inc(f_in[0], 16)
            sp.dma_start(lb_raw[:], w_lora_out).then_inc(f_in[1], 16)

        def pool_dense(pool, b, d):
            if d.name == "proj":
                return
            if d.ffn:
                pool.wait_ge(f_in[2], 16 * d.f + 16)
            else:
                pool.wait_ge(ox_in, 16 * b + 16)
            for t in range(TT):
                if d.ffn:
                    pool.wait_ge(ln_xn, TT * (4 * b + 1 + 2 * d.f0) + t + 1)
                else:
                    pool.wait_ge(x_ld[t // 2], 16 * (3 * b + 3))
                pool.tensor_tensor(X[:, t, :], X[:, t, :], bias_row[:], ALU.add).then_inc(f_bias if d.ffn else o_bias, 1)

        def act_dense(act, b, d):
            if d.name == "ffn":
                if d.f0 == 0:
                    act_dense_weights(act, d, 0)
                act.wait_ge(f_h, d.f + 1)
                act.activation(logit_t[:], banks[0:NE, 2:4, :].rearrange("p b n -> p (b n)"), ACT.Identity,
                               bias=b_rout[:, 0:1]).then_inc(f_lg, 1)
                act.copy(h_sb[:], AUX).then_inc(f_hsb, 1)
                act.wait_ge(f_hw, d.f + 1)
                act.copy(hw[0][:], h_sb[:]).then_inc(f_hwhi, 1)
                act_dense_weights(act, d, 1)
            else:
                act_dense_weights(act, d, 0)
                f = 2 * b + (d.name == "wo")
                for i, (hi, source) in enumerate(((la[0], la_raw), (lb[0], lb_raw))):
                    act.wait_ge(f_in[i], 16 * f + 16)
                    act.copy(hi[:], source[:]).then_inc(f_hi, 1)
                if d.name == "wo":
                    act_dense_weights(act, Dense("ffn", b, 1), 0)
                else:
                    act_dense_weights(act, d, 1)
            if d.norm is not None:
                for t in range(TT + 2):
                    act_norm_step(act, d.norm, t)

        def act_dense_weights(act, d, o):
            for q in range(d.parts):
                at_load = d.load_index(o)
                act.wait_ge(d.S.w_in[q], 16 * at_load + 16)
                if d.wide and not (d.name == "proj" and o == 0):
                    if q < d.parts - 1:
                        act.wait_ge(w_free, (d.parts - 1) * (at_load - 1) + q + 1)
                    else:
                        act.wait_ge(SD.tile, TT * at_load)
                act.copy(d.chunks(q, 0), d.chunks(q)).then_inc(d.S.w_hi, 1)

        def dve_dense_weights(dve, d, o, parts=None):
            for q in parts or range(d.parts):
                dve.wait_ge(d.S.w_hi, d.parts * d.load_index(o) + q + 1)
                dve.tensor_tensor(d.chunks(q, 1), d.chunks(q), raw(d.chunks(q, 0)), ALU.subtract).then_inc(d.S.w_lo, 1)

        def dve_routing(dve, f):
            step = [0]

            def done(ins):
                step[0] += 1
                ins.then_inc(f_dve, 1)
                dve.wait_ge(f_dve, F_DVE * f + step[0])

            z, cum, cnt, t0, t1, k1, s1, tau = (sp_buf[:, i, :] for i in range(8))

            def by_tile(a):
                return a.rearrange("p (t e) -> p t e", e=NE)

            ge, zge = pairs[:, 0], pairs[:, 1]
            dve.wait_ge(f_zt, f + 1)
            done(dve.tensor_copy(z, banks[:, 2, 0:TT * NE]))
            zi = by_tile(z).unsqueeze(3).broadcast_to([P, TT, NE, NE])
            zj = by_tile(z).unsqueeze(2).broadcast_to([P, TT, NE, NE])
            done(dve.tensor_tensor(ge, zj, zi, ALU.is_ge))
            dve.tensor_reduce(cnt, ge.rearrange("p t i j -> p (t i) j"), AX.X, ALU.add)
            done(dve.tensor_tensor(zge, ge, zj, ALU.mult))
            done(dve.tensor_reduce(cum, zge.rearrange("p t i j -> p (t i) j"), AX.X, ALU.add))
            done(dve.tensor_tensor(t0, cnt, z, ALU.mult))
            done(dve.tensor_scalar(t0, t0, 1.0, None, ALU.add))
            done(dve.tensor_tensor(t0, t0, cum, ALU.is_gt))
            done(dve.tensor_tensor(t1, t0, z, ALU.mult))
            dve.tensor_reduce(k1[:, 0:TT], by_tile(t0), AX.X, ALU.add)
            done(dve.tensor_reduce(s1[:, 0:TT], by_tile(t1), AX.X, ALU.add))
            done(dve.reciprocal(k1[:, TT:2 * TT], k1[:, 0:TT]))
            done(dve.scalar_tensor_tensor(out=tau[:, 0:TT], in0=s1[:, 0:TT], scalar=-1.0, in1=k1[:, TT:2 * TT],
                                          op0=ALU.add, op1=ALU.mult))
            done(dve.tensor_tensor(by_tile(t1), by_tile(z), tau[:, 0:TT].unsqueeze(2).broadcast_to([P, TT, NE]),
                                   ALU.subtract))
            done(dve.tensor_scalar(t0, t1, 0.0, None, ALU.max))
            spread = pairs[:].rearrange("p a t i j -> p (a t i j)")
            done(dve.tensor_copy(spread.rearrange("p (e r) -> p e r", r=R),
                                 t0.unsqueeze(2).broadcast_to([P, TT * NE, R])))
            assert step[0] == F_DVE, step[0]

        def dve_dense(dve, b, d):
            if d.ffn:
                if d.f0 == 0:
                    dve_dense_weights(dve, d, 0)
                dve_routing(dve, d.f)
                dve.wait_ge(f_wt, d.f + 1)
                dve.wait_ge(f_hsb, d.f + 1)
                dve.tensor_tensor(h_sb[:], AUX, h_sb[:], ALU.mult).then_inc(f_hw, 1)
                dve.wait_ge(f_hwhi, d.f + 1)
                dve.tensor_tensor(hw[1][:], h_sb[:], raw(hw[0][:]), ALU.subtract).then_inc(f_hwlo, 1)
            else:
                dve_dense_weights(dve, d, 0)
            n = 2 * TT
            for i in range(n):
                if i == TT - 2 and not d.ffn:
                    f = 2 * b + (d.name == "wo")
                    for j, (lo, hi, source) in enumerate(((la[1], la[0], la_raw), (lb[1], lb[0], lb_raw))):
                        dve.wait_ge(f_hi, 2 * f + j + 1)
                        dve.tensor_tensor(lo[:], source[:], raw(hi[:]), ALU.subtract).then_inc(f_lo, 1)
                if i == TT - 1:
                    if d.wide:
                        dve_dense_weights(dve, d, 1, range(d.parts - 1))
                    else:
                        dve_dense_weights(dve, Dense("ffn", b, 1), 0)
                for m in d.finished(i):
                    o, t = divmod(m, TT)
                    if o == 0:
                        if d.name == "proj":
                            dve.wait_ge(x_ld[t // 2], 16 * (3 * b + 2))
                        else:
                            dve.wait_ge(f_bias if d.ffn else o_bias, TT * (d.f if d.ffn else b) + t + 1)
                    dve.wait_ge(d.S.tile, n * d.i + m + 1)
                    x = X[:, t, o * HALF:(o + 1) * HALF]
                    dve.tensor_tensor(x, banks[:, 4 + m % RING, :], x, ALU.add).then_inc(d.S.added, 1)
                    if i == TT - 1 and d.wide:
                        dve_dense_weights(dve, d, 1, (d.parts - 1,))
                if i >= TT and d.norm is not None:
                    dve.wait_ge(d.S.added, n * d.i + i + 1)
                    dve_norm_step(dve, d.norm, i - TT)
            if d.norm is not None:
                for t in (TT, TT + 1):
                    dve_norm_step(dve, d.norm, t)

        def pe_lora_in(pe, f):
            pe.wait_ge(f_lo, 2 * f + 1)
            pe.wait_ge(ln_lo, TT * (2 * f + 2))
            for bank, rows in ((2, slice(P, P + NE)), (0, slice(0, P))):
                m = rows.stop - rows.start
                for c in range(CC):
                    for a, x in PRODUCTS:
                        for h in range(2):
                            mm = pe.matmul(banks[0:m, bank + h, :], la[a][:, c, rows], xt[x][:, c, h * HALF:(h + 1) * HALF],
                                           start=c == 0 and (a, x) == (0, 0), stop=c == CC - 1 and (a, x) == PRODUCTS[-1])
            mm.then_inc(f_h, 1)

        def pe_turn_logits(pe, f):
            pe.wait_ge(f_lg, f + 1)
            settle(pe)
            for t in range(TT):
                mm = pe.transpose(banks[:, 2, t * NE:(t + 1) * NE], logit_t[:, t * P:(t + 1) * P], ident[0:NE, 0:NE])
            mm.then_inc(f_zt, 1)

        def pe_turn_weights(pe, f):
            pe.wait_ge(f_dve, F_DVE * (f + 1))
            pe.wait_ge(f_hsb, f + 1)
            spread = pairs[:].rearrange("p a t i j -> p (a t i j)")
            for t in range(TT):
                mm = pe.transpose(AUX[:, t * P:(t + 1) * P], spread[:, t * P:(t + 1) * P], ident[:])
            mm.then_inc(f_wt, 1)

        def pe_dense(pe, b, d):
            if d.ffn:
                pe_lora_in(pe, d.f)
            n = 2 * TT
            for i in range(n):
                o, t = divmod(i, TT)
                if i >= RING:
                    pe.wait_ge(d.S.added, n * d.i + i - RING + 1)
                for q in range(d.parts):
                    if t == 0:
                        pe.wait_ge(d.S.w_lo, d.parts * d.load_index(min(o, d.loads - 1)) + q + 1)
                    for c in range(q * d.cc // d.parts, (q + 1) * d.cc // d.parts):
                        for m, (x, a) in enumerate(PRODUCTS):
                            mm = pe.matmul(banks[:, 4 + i % RING, :], xt[x][:, c, t * P:(t + 1) * P], d.weights(a, c, o),
                                           start=c == 0 and m == 0, stop=not d.ffn and c == d.cc - 1 and m == 2)
                    if t == TT - 1 and q < d.parts - 1:
                        mm.then_inc(w_free, 1)
                if not d.ffn:
                    mm.then_inc(d.S.tile, 1)
                if d.ffn and i == 0:
                    pe_turn_logits(pe, d.f)
                if d.ffn and i == LAG - 1:
                    pe_turn_weights(pe, d.f)
                if d.ffn and i == LAG:
                    pe.wait_ge(f_hwlo, d.f + 1)
                    pe.wait_ge(f_lo, 2 * d.f + 2)
                if d.ffn:
                    for m_i in d.finished(i):
                        o, t = divmod(m_i, TT)
                        for m, (x, a) in enumerate(PRODUCTS):
                            mm = pe.matmul(banks[:, 4 + m_i % RING, :], hw[x][:, t * P:(t + 1) * P],
                                           lb[a][:, o * HALF:(o + 1) * HALF], start=False, stop=m == 2)
                        mm.then_inc(d.S.tile, 1)
                if i >= TT and d.norm is not None:
                    pe_norm_step(pe, d.norm, i - TT)
            if d.norm is not None:
                for t in (TT, TT + 1):
                    pe_norm_step(pe, d.norm, t)

        def sp_b(sp, b):
            for p in range(3):
                sp.wait_ge(SB.w_lo, 3 * b + p)
                settle(sp)
                sp.dma_start(wq_raw[:], wb_qkv[p]).then_inc(SB.w_in, 16)
            sp.wait_ge(SB.fill, 8 * (b + 1))
            settle(sp)
            for h in range(4):
                sp_stack(sp, HB, SB, b, 0, h, first=True)
            sp_max_rows(sp, HB, SB, b, 0, 0)
            for g in range(GB):
                for k in range(HB.slots):
                    if g + 1 < GB and k in (18, 34, 50):
                        sp_stack(sp, HB, SB, b, g + 1, (18, 34, 50).index(k))
                    if g and k == 1:
                        sp_stack(sp, HB, SB, b, g, 3)
                    if (k + 5) % HB.n == 0 and ((k + 5) // HB.n < 4 or g + 1 < GB):
                        sp_max_rows(sp, HB, SB, b, g, (k + 5) // HB.n, last=g + 1 == GB)

        def pool_b(pool, b):
            for i, (part, value) in enumerate(((qst[0:96, :, :], 0.0), (kst[0:96, :, :], 0.0), (kst[96:98, :, :], 1.0))):
                pool.memset(raw(part), value).then_inc(SB.fill, 1)
                pool.wait_ge(SB.fill, 8 * b + i + 1)
                settle(pool)
            pool.memset(raw(vsb[:]), 0.0).then_inc(SB.fill, 1)
            pool.wait_ge(SB.fill, 8 * b + 4)
            settle(pool)
            for odd in range(2):
                c0 = 64 + HDB * odd
                pool.memset(raw(vsb[:, :, odd::2, c0:c0 + HDB]), 1.0).then_inc(SB.fill, 2)

        def pe_b(pe, b):
            for p in range(3):
                pe.wait_ge(SB.w_lo, 3 * b + p + 1)
                if p:
                    pe.wait_ge(SB.raw_in, 3 * b + p)
                for o, a, x, start, stop in pe_project(2):
                    mm = pe.matmul(o, a, x, start=start, stop=stop)
                mm.then_inc(SB.proj_done, 1)
            pe.wait_ge(SB.raw_in, 3 * b + 3)
            for t in range(TT):
                mm = pe.transpose(AUX[:, t * P:(t + 1) * P], vt[:, t * P:(t + 1) * P], ident[:])
            mm.then_inc(SB.aux, 1)
            pe.wait_ge(SB.fill, 8 * b + 8)
            for v in range(HB.lead):
                pe_max(pe, HB, SB, b, 0, v, first=True)
            pe_scores(pe, HB, SB, b, 0, 0, first=True)
            pe.wait_ge(SB.v_lo, b + 1)
            for g in range(GB):
                for k in range(HB.slots):
                    if k + 1 < HB.slots or g + 1 < GB:
                        pe_scores(pe, HB, SB, b, g, k + 1)
                    pe_max(pe, HB, SB, b, g, k + HB.lead, last=g == GB - 1)
                    if k > 1 or g:
                        pe_pv(pe, HB, SB, b, g, k - 2, HB.slots * g, g == 0)
            for k in (-2, -1):
                pe_pv(pe, HB, SB, b, GB, k, HB.slots * GB)

        def act_b(act, b):
            for p in range(3):
                act.wait_ge(SB.w_in, 16 * (3 * b + p) + 16)
                if p:
                    act.wait_ge(SB.proj_done, 3 * b + p)
                act.copy(wq[2][0][:], wq_raw[:]).then_inc(SB.w_hi, 1)
                act.wait_ge(SB.proj_done, 3 * b + p + 1)
                if p == 1:
                    act.wait_ge(SB.src_lo, 2 * b + 1)
                dst = vt if p == 2 else turn
                act.activation(dst[:], AUX, ACT.Identity, bias=b_qkv[:, p:p + 1]).then_inc(SB.raw_in, 1)
                if p < 2:
                    act.wait_ge(SB.raw_in, 3 * b + p + 1)
                    act.copy(src[p][0][:], turn[:]).then_inc(SB.src_hi, 1)
            act.wait_ge(SB.fill, 8 * b + 8)
            act.wait_ge(SB.aux, b + 1)
            for odd in range(2):
                act.copy(vsb[:, :, odd::2, HDB * odd:HDB * odd + HDB], turned_b(odd)).then_inc(SB.v_hi, 1)
            act_exp(act, HB, SB, b, 0, 0, 0, first=True)
            for g in range(GB):
                ring = HB.slots * g % 3
                for k in range(HB.slots):
                    if k + 1 < HB.slots or g + 1 < GB:
                        act_exp(act, HB, SB, b, g, k + 1, ring, g == 0)
                    act_hi(act, HB, SB, b, g, k, ring, g == 0)
                    for half, at_c in Y_CHUNK:
                        if k % (2 * HB.n) == at_c and (k > at_c or g):
                            act_y(act, HB, SB, b, *((g, k // HB.n - 1) if k > at_c else (g - 1, 3)), half, g == 0)
            for half in (1, 0):
                act_y(act, HB, SB, b, GB - 1, 3, half)
            act.wait_ge(by_y, b + 1)
            act.copy(xt[0][:, 0, :], y[:]).then_inc(by_hi, 1)

        def turned_b(odd):
            return AUX.rearrange("p (t j d) -> p t j d", t=TT, d=HDB)[:, :, odd::2, :]

        def dve_b(dve, b):
            for p in range(3):
                dve.wait_ge(SB.w_hi, 3 * b + p + 1)
                dve.tensor_tensor(wq[2][1][:], wq_raw[:], raw(wq[2][0][:]), ALU.subtract).then_inc(SB.w_lo, 1)
                if p < 2:
                    dve.wait_ge(SB.src_hi, 2 * b + p + 1)
                    dve.tensor_tensor(src[p][1][:], turn[:], raw(src[p][0][:]), ALU.subtract).then_inc(SB.src_lo, 1)
            dve.wait_ge(SB.v_hi, 2 * b + 2)
            for odd in range(2):
                c0 = HDB * odd
                last = dve.tensor_tensor(vsb[:, :, odd::2, 32 + c0:32 + c0 + HDB], turned_b(odd),
                                         raw(vsb[:, :, odd::2, c0:c0 + HDB]), ALU.subtract)
            last.then_inc(SB.v_lo, 1)
            for v in range(HB.lead):
                dve_max(dve, HB, SB, b, 0, v, first=True)
            for g in range(GB):
                ring = HB.slots * g % 3
                for k in range(HB.slots):
                    dve_max(dve, HB, SB, b, g, k + HB.lead, last=g == GB - 1)
                    dve_lo(dve, HB, SB, b, g, k, ring)
                    for half, at_c in Y_CHUNK:
                        if k % (2 * HB.n) == at_c and (k > at_c or g):
                            dve_y(dve, HB, SB, b, *((g, k // HB.n - 1) if k > at_c else (g - 1, 3)), half)
            for half in (1, 0):
                dve_y(dve, HB, SB, b, GB - 1, 3, half)
            dve.wait_ge(SB.y_done, NHB * (b + 1))
            dve.reciprocal(rden[:], den[:]).then_inc(by_r, 1)
            dve.wait_ge(by_r, b + 1)
            dve.scalar_tensor_tensor(out=y[:], in0=y[:], scalar=SCALE_B_OUT, in1=rden[:], op0=ALU.mult,
                                     op1=ALU.mult).then_inc(by_y, 1)
            dve.wait_ge(by_hi, b + 1)
            dve.tensor_tensor(xt[1][:, 0, :], y[:], raw(xt[0][:, 0, :]), ALU.subtract).then_inc(by_lo, 1)

        def sp_setup(sp):
            sp.dma_start(gate[:], gating.broadcast_to([P, 1])).then_inc(c_in, 16)
            sp.dma_start(b_rout[:], b_router).then_inc(c_in, 16)
            sp.dma_start(b_qkv[:], bb_qkv).then_inc(c_in, 16)
            sp.dma_start(at_raw[:], adapter).then_inc(at_in, 16)
            for n in range(4):
                part, gh = 1 + n // 2, n % 2
                if n:
                    sp.wait_ge(sw_lo, n + 1)
                for i in range(4):
                    sp.dma_start(w_raw[:, :, i * P:(i + 1) * P], w_qkv[4 * gh + i, part]).then_inc(sw_in, 16)
            sp.wait_ge(s_zero, 1)
            for s in range(2):
                sp.dma_start(av_dram[s], zeros[:].rearrange("p (g n) -> p g n", g=G)).then_inc(s_avd, 16)
            sp.wait_ge(s_avd, 32)
            sp.wait_ge(s_av, 2)
            for s in range(2):
                v = raw(avs[s][:]).rearrange("p (g j d) -> p g j d", g=G, d=HD)
                for g3 in range(3):
                    for j in range(4):
                        r0 = (4 * g3 + j) * AK
                        sp.dma_start(av_dram[s][r0:r0 + AK, g3::3, HD * j:HD * j + HD], v[:, g3::3, j, :]).then_inc(s_avd, 16)
            sp.wait_ge(s_avd, 32 + 24 * 16)
            sp.wait_ge(c_in, 48)

        def pool_setup(pool):
            pool.memset(ident[:], 0.0).then_inc(c_set, 1)
            pool.memset(mask_main[:], 0.0).then_inc(c_set, 1)
            pool.memset(mask_max[:], 0.0).then_inc(c_set, 1)
            pool.memset(raw(ak_all[:]), 0.0).then_inc(c_set, 1)
            pool.memset(zeros[:], 0.0).then_inc(s_zero, 1)
            pool.wait_ge(c_set, 4)
            row_minus_column = dict(base=0, pattern=[[-1, P]], channel_multiplier=1)
            pool.affine_select(out=ident[:], in_=ident[:], compare_op=ALU.not_equal, fill=1.0,
                               **row_minus_column).then_inc(c_set, 1)
            pool.affine_select(out=mask_main[:], in_=mask_main[:], compare_op=ALU.is_ge, fill=MASKED,
                               base=0, pattern=[[1, P]], channel_multiplier=-1).then_inc(c_set, 1)
            pool.affine_select(out=mask_max[:], in_=mask_max[:], compare_op=ALU.is_ge, fill=MASKED,
                               **row_minus_column).then_inc(c_set, 1)

        def act_setup(act):
            act.wait_ge(at_in, 16)
            act.copy(at[0][:], at_raw[:]).then_inc(sw_hi, 1)
            for n in range(4):
                act.wait_ge(sw_in, 64 * (n + 1))
                if n:
                    act.wait_ge(s_mm, n)
                act.copy(w[0][:], w_raw[:]).then_inc(sw_hi, 1)
                act.wait_ge(s_mm, n + 1)
                act.copy(akv[:, n // 2, (n % 2) * HALF:(n % 2 + 1) * HALF], banks[0:AK, n % 2, :]).then_inc(s_ev, 1)
            act.wait_ge(s_ev, 4)
            act.copy(avs[0][:], akv[:, 1, :]).then_inc(s_av, 1)

        def dve_setup(dve):
            dve.wait_ge(c_set, 7)
            dve.tensor_copy(ident16[:], ident[:])
            dve.wait_ge(sw_hi, 1)
            dve.tensor_tensor(at[1][:], at_raw[:], raw(at[0][:]), ALU.subtract).then_inc(sw_lo, 1)
            for n in range(4):
                dve.wait_ge(sw_hi, n + 2)
                dve.tensor_tensor(w[1][:], w_raw[:], raw(w[0][:]), ALU.subtract).then_inc(sw_lo, 1)
            dve.wait_ge(s_tr, 1)
            turned_keys = banks[:, 2, 0:G * AK].rearrange("p (g k) -> p g k", k=AK)
            for j in range(4):
                rows, cols = slice(32 * j, 32 * j + 32), slice(AK * j, AK * j + AK)
                dve.tensor_copy(ak_all[rows, :, 0, cols], turned_keys[rows]).then_inc(s_tr, 1)
            dve.wait_ge(s_tr, 5)
            for j in range(4):
                rows, cols = slice(32 * j, 32 * j + 32), slice(AK * j, AK * j + AK)
                dve.tensor_tensor(ak_all[rows, :, 1, cols], turned_keys[rows], raw(ak_all[rows, :, 0, cols]), ALU.subtract)
            dve.wait_ge(s_av, 1)
            dve.tensor_tensor(avs[1][:], akv[:, 1, :], raw(avs[0][:]), ALU.subtract).then_inc(s_av, 1)

        def pe_setup(pe):
            pe.wait_ge(c_set, 7)
            for n in range(4):
                pe.wait_ge(sw_lo, n + 2)
                if n >= 2:
                    pe.wait_ge(s_ev, n - 1)
                for c in range(CC):
                    for m, (x, a) in enumerate(PRODUCTS):
                        mm = pe.matmul(banks[0:AK, n % 2, :], at[x][:, c, :], w[a][:, c, :], start=c == 0 and m == 0,
                                       stop=c == CC - 1 and m == 2)
                mm.then_inc(s_mm, 1)
            pe.wait_ge(s_ev, 4)
            for g in range(G):
                mm = pe.transpose(banks[:, 2, g * AK:(g + 1) * AK], akv[:, 0, g * P:(g + 1) * P], ident[0:AK, 0:AK])
            mm.then_inc(s_tr, 1)

        def nothing(eng, *_):
            pass

        def program(eng, setup, norm_, attention_a, adapter_, dense_, attention_b):
            setup(eng)
            setup_end(eng)
            with eng.Fori(0, B) as b:
                norm_(eng, b)
                attention_a(eng, b)
                phase_end(eng, b, 0)
                adapter_(eng, b)
                phase_end(eng, b, 1)
                dense_(eng, b, Dense("proj", b))
                dense_(eng, b, Dense("ffn", b, 0))
                phase_end(eng, b, 2)
                attention_b(eng, b)
                phase_end(eng, b, 3)
                dense_(eng, b, Dense("wo", b))
                dense_(eng, b, Dense("ffn", b, 1))
                phase_end(eng, b, 4)

        block = ctx.enter_context(nc.Block())

        @block.sync
        def _(sp):
            program(sp, sp_setup, sp_norm, sp_a, sp_adapter, sp_dense, sp_b)

        @block.gpsimd
        def _(pool):
            program(pool, pool_setup, nothing, pool_a, pool_adapter, pool_dense, pool_b)

        @block.scalar
        def _(act):
            program(act, act_setup, act_norm, act_a, act_adapter, act_dense, act_b)

        @block.vector
        def _(dve):
            program(dve, dve_setup, dve_norm, dve_a, dve_adapter, dve_dense, dve_b)

        @block.tensor
        def _(pe):
            program(pe, pe_setup, pe_norm, pe_a, pe_adapter, pe_dense, pe_b)


def kernel(L0_attn_a_x, L0_attn_a_w_attn, L0_attn_a_w_proj, L0_attn_a_adapter_wte, L0_attn_a_gating,
           L0_attn_b_Wqk_w, L0_attn_b_Wqk_b, L0_attn_b_Wv_w, L0_attn_b_Wv_b, L0_attn_b_Wo_w, L0_attn_b_Wo_b,
           L0_ffn_W_base, L0_ffn_b_base, L0_ffn_W_router, L0_ffn_b_router, L0_ffn_lora_A, L0_ffn_lora_B):
    import numpy as np
    import concourse.bacc as bacc
    from concourse.bass_utils import run_bass_kernel_spmd

    def chunked(w_t):
        return w_t.reshape(-1, P, w_t.shape[1]).transpose(1, 0, 2)

    f32 = lambda a: np.ascontiguousarray(np.asarray(a))
    w_attn = f32(L0_attn_a_w_attn).reshape(3, G, P, CC, P)
    halves = lambda w_: f32(w_).reshape(2, HALF, CC, P).transpose(0, 3, 2, 1)
    wqk = f32(L0_attn_b_Wqk_w).reshape(P, 2, C)
    bqk = f32(L0_attn_b_Wqk_b).reshape(P, 2)
    wb = [chunked(a.T) for a in (wqk[:, 0], wqk[:, 1], f32(L0_attn_b_Wv_w))]
    lora_in = np.concatenate([f32(L0_ffn_lora_A).transpose(1, 0, 2).reshape(C, NE * R), f32(L0_ffn_W_router).T], 1)
    theta = (np.float32(1.0) / np.float32(10000.0) ** (np.arange(0, HD, 2, dtype=np.float32) / np.float32(HD))).astype(np.float32)
    angle = np.outer(theta, np.arange(T, dtype=np.float32)).astype(np.float32)
    cos_t, sin_t = np.cos(angle), np.sin(angle)
    arrays = {
        "x_in": f32(L0_attn_a_x),
        "w_qkv": w_attn.transpose(1, 0, 4, 3, 2),
        "w_proj": halves(L0_attn_a_w_proj),
        "adapter": chunked(f32(L0_attn_a_adapter_wte).T),
        "gating": f32(L0_attn_a_gating).reshape(1, 1),
        "rope_cos": np.tile(np.concatenate([cos_t, cos_t]), (4, 1)),
        "rope_sin": np.tile(np.concatenate([-sin_t, sin_t]), (4, 1)),
        "w_base": halves(L0_ffn_W_base),
        "b_base": f32(L0_ffn_b_base).reshape(1, C),
        "w_lora_in": chunked(lora_in),
        "b_router": f32(L0_ffn_b_router).reshape(NE, 1),
        "w_lora_out": f32(L0_ffn_lora_B).reshape(NE * R, C),
        "wb_qkv": np.stack(wb),
        "bb_qkv": np.stack([bqk[:, 0], bqk[:, 1], f32(L0_attn_b_Wv_b)], 1),
        "wb_out": f32(L0_attn_b_Wo_w).T.reshape(P, 2, HALF),
        "bb_out": f32(L0_attn_b_Wo_b).reshape(1, C),
    }
    nc = bacc.Bacc("TRN2", target_bir_lowering=False, num_devices=1)
    args = {}
    for name, a in arrays.items():
        arrays[name] = np.ascontiguousarray(a)
        args[name] = nc.dram_tensor(name + "_dram", a.shape, F32, kind="ExternalInput").ap()
    args["out"] = nc.dram_tensor("out_dram", (B, T, C), F32, kind="ExternalOutput").ap()
    build_program(nc, **args)
    r = run_bass_kernel_spmd(nc, [{n + "_dram": a for n, a in arrays.items()}], core_ids=[0])
    return r.results[0]["out_dram"]
```

```python
from contextlib import ExitStack

import concourse.bass as bass
from concourse import mybir

F32 = mybir.dt.float32
F32R = mybir.dt.float32r
BF16 = mybir.dt.bfloat16
ALU = mybir.AluOpType
ACT = mybir.ActivationFunctionType
AX = mybir.AxisListType

P = 128
B = 2
T = 1024
C = 1024
TT = T // P
CC = C // P
HALF = 512
NH, HD = 32, 32
G = NH * HD // P
AK = 10
NE, R = 8, 16
NHB, HDB = 8, 16
GB = NHB // 4
EPS = 1e-5
MASKED = -1e30
SCALE_A = HD ** -0.5
SCALE_ADAPTER = C ** -0.5
SCALE_B_OUT = (NHB * HDB) ** -0.5
LAG = 3
RING = 4
AH = 3
PHASES = 3
PRODUCTS = ((0, 0), (0, 1), (1, 0))


class Heads:

    def __init__(self, causal):
        if causal:
            order = ((0, 1), (1, 1), (7, 1), (0, 0), (2, 1), (6, 1), (3, 1), (2, 0), (5, 1), (4, 1), (1, 0), (3, 0))
        else:
            order = ((0, 1), *((t + h, h) for t in range(TT - 1) for h in (1, 0)), (TT - 1, 0))
        self.main = [(t, max(t * P, h * HALF) if causal else h * HALF, (h + 1) * HALF) for t, h in order]
        if causal:
            order = ((2, 0), (3, 0), (4, 0), (0, 0), (5, 0), (6, 0), (6, 1), (1, 0), (7, 0), (5, 1), (4, 1), (7, 1))
            self.max = [(t, h * HALF, min((h + 1) * HALF, (t + 1) * P), t if h == 0 else 4 + t) for t, h in order]
        else:
            self.max = [(t, h * HALF, (h + 1) * HALF, t + TT * h) for t in range(TT) for h in range(2)]
        self.causal = causal
        self.n = len(self.main)
        self.items = self.n + 1
        self.slots = 4 * self.n
        self.groups = G if causal else GB
        self.heads = 4 * self.groups
        self.pair = 1 if causal else 2
        self.lead = self.n + 6
        self.ring = 3 if causal else 4
        self.lag = self.ring - 1
        self.scale = SCALE_A if causal else 1.0
        self.last = [max(i for i, c in enumerate(self.main) if c[1] // HALF == h) for h in range(2)]
        self.result = [(h, self.last[h] + self.lag + 1 - self.n) for h in (1, 0)]


HA, HB = Heads(True), Heads(False)


def build_program(nc, x_in, w_qkv, w_proj, adapter, gating, rope_cos, rope_sin, w_base, b_base, w_lora_in,
                  b_router, w_lora_out, wb_qkv, bb_qkv, wb_out, bb_out, out):
    with ExitStack() as ctx:
        top = nc.sbuf_usable_end

        class Region:

            def __init__(self, start):
                self.at = start

            def __call__(self, name, shape, dtype):
                n = 2 if dtype == BF16 else 4
                for s in shape[1:]:
                    n *= s
                t = nc.alloc_sbuf_tensor_at(name, shape, dtype, offset=self.at)
                self.at += (n + 31) // 32 * 32
                assert self.at <= top, (name, self.at, top)
                return t

            def split(self, name, shape):
                return [self(f"{name}_{s}", shape, F32R) for s in ("hi", "lo")]

        def sem(name):
            return ctx.enter_context(nc.semaphore(name))

        def scratch(name, shape):
            return nc.dram_tensor(name, shape, F32, kind="Internal").ap()

        def raw(ap):
            return ap.bitcast(F32)

        keep = Region((nc.sbuf_base + 31) // 32 * 32)
        ident = keep("ident", [P, P], F32)
        ident16 = keep("ident16", [P, P], BF16)
        mask_main = keep("mask_main", [P, P], BF16)
        mask_max = keep("mask_max", [P, P], BF16)
        ak_all = keep("ak_all", [P, G, 2, 4 * AK], F32R)
        gate = keep("gate", [P, 1], F32)
        b_rout = keep("b_rout", [NE, 1], F32)
        b_qkv = keep("b_qkv", [P, 3], F32)
        xt = keep.split("xt", [P, CC, T])
        dense = Region(keep.at)
        X = dense("X", [P, TT, C], F32)
        over_w = dense.at
        w = dense.split("w", [P, CC, HALF])
        w_raw = dense("w_raw", [P, CC, HALF], F32)
        lb = dense.split("lb", [P, C])
        lb_raw = dense("lb_raw", [P, C], F32)
        la = dense.split("la", [P, CC, P + NE])
        la_raw = dense("la_raw", [P, CC, P + NE], F32)
        hw = dense.split("hw", [P, T])
        sp_buf = dense("sp_buf", [P, 8, TT * NE], F32)
        over_src = dense.at
        h_sb = dense("h_sb", [P, T], F32)
        bias_row = dense("bias_row", [P, C], F32)
        pairs = dense("pairs", [P, 2, TT, NE, NE], F32)
        logit_t = dense("logit_t", [NE, T], F32)
        early = Region(over_w + 3 * CC * HALF * 4)
        at_raw = early("at_raw", [P, CC, AK], F32)
        at = early.split("at", [P, CC, AK])
        akv = early("akv", [AK, 2, C], F32)
        avs = early.split("avs", [AK, C])
        zeros = early("zeros", [P, G * P], F32)
        norm = Region(dense.at)
        xn = norm("xn", [P, 2, C], F32)
        stats = norm("stats", [P, TT, 2, 6], F32)
        mv = norm("mv", [P, TT, 2], F32)
        rs = norm("rs", [P, 4, TT], F32)
        adp = Region(over_w + 3 * CC * HALF * 4)
        asc = adp("asc", [P, AH, T], F32)
        av = adp.split("av", [P, G, P])
        pa = adp.split("pa", [P, AH, T])
        over_w_lo = Region(over_w + CC * HALF * 4)
        a_e = over_w_lo("a_e", [P, 2, NH, AK], F32)
        a_s = over_w_lo("a_s", [P, 2, 3, NH], F32)
        over_x = Region(keep.at + TT // 2 * C * 4)
        yt_in_sb = over_x("yt_in_sb", [P, 2, T], F32)
        y_sum = over_x("y_sum", [P, 2, T], F32)
        att = Region(keep.at)
        prob = att("prob", [P, 3, HALF], F32)
        phl = att.split("prob", [P, 3, HALF])
        y = att("y", [P, T], F32)
        den = att("den", [P, T], F32)
        y_tmp = att("y_tmp", [32, HALF], F32)
        rot = att("rot", [P, T], F32)
        over_tables = att.at
        assert over_tables >= over_w
        cos = att("cos", [P, T], F32)
        sin = att("sin", [P, T], F32)
        wq = [att.split(f"wq{p}", [P, CC, P]) for p in range(3)]
        wq_raw = att("wq_raw", [P, CC, P], F32)
        qst = att("qst", [98, 4, T], F32R)
        kst = att("kst", [98, 4, T], F32R)
        over_vst = att.at
        vst = att("vst", [P, TT, 4, 96], F32R)
        ak_cur = att("ak_cur", [P, 2, 4 * AK], F32R)
        m_part = att("m_part", [P, 2, 16], F32)
        m_row = att.split("m_row", [TT, 2, P])
        assert att.at <= dense.at, "the layer norm's own tensors lie over projected rows only"
        assert att.at <= over_src, "the full attention's output weights are loaded over src"
        src = [att.split(f"src{p}", [P, T]) for p in "qk"]
        turn = att("turn", [P, T], F32)
        over_result = att.at
        vt = att("vt", [P, T], F32)
        rden = vt
        d_col = att("d_col", [P, 32], F32)
        r_col = att("r_col", [P, 32], F32)
        assert adp.at <= over_result
        over = Region(over_tables)
        vsb = over("vsb", [P, TT, NHB, 96], F32R)
        assert over.at <= over_tables + 2 * T * 4 + 4 * CC * P * 4, "vsb must end before wq2"
        over = Region(keep.at)
        prob_b = over("prob_b", [P, 4, HALF], F32)
        phl_b = over.split("prob_b", [P, 4, HALF])
        y_tmp_b = over("y_tmp_b", [32, HALF], F32)
        y_b = over("y_b", [P, T], F32)
        assert over.at <= over_tables
        over = Region(keep.at)
        wb = [wq[2], over.split("wb", [P, CC, P])]
        wb_raw = [wq_raw, over("wb_raw", [P, CC, P], F32)]
        assert over.at <= over_tables
        over = Region(over_vst)
        den_b = over("den_b", [P, T], F32)
        rden_b = over("rden_b", [P, T], F32)
        assert over.at <= over_vst + TT * 4 * 96 * 4

        banks = ctx.enter_context(nc.psum_tensor("banks", [P, 8, HALF], F32))
        AUX = banks[:, 0:2, :].rearrange("p b n -> p (b n)")

        yt_dram = scratch("yt_dram", [B, G, P, T])
        asc_dram = scratch("asc_dram", [B, G * 4 * AK, T])
        rd_dram = scratch("rd_dram", [B, G, 4, T])
        av_dram = [scratch(f"av_dram_{s}", [P, G, P]) for s in ("hi", "lo")]
        x_dram = scratch("x_dram", [B, P, TT, C])

        phase_done = sem("phase_done")
        setup_done = sem("setup_done")
        passed = sem("passed")
        c_set = sem("c_set")
        c_in, at_in = sem("c_in"), sem("at_in")
        sw_in, sw_hi, sw_lo = [sem(f"sw_in{i}") for i in range(3)], sem("sw_hi"), sem("sw_lo")
        s_mm, s_ev, s_tr, s_av = sem("s_mm"), sem("s_ev"), sem("s_tr"), sem("s_av")
        s_zero, s_avd = sem("s_zero"), sem("s_avd")
        x_ld = [sem(f"x_ld{t}") for t in range(4)]
        ln_stat, ln_scale, ln_root, ln_xn = sem("ln_stat"), sem("ln_scale"), sem("ln_root"), sem("ln_xn")
        ln_tr, ln_hi, ln_lo = sem("ln_tr"), sem("ln_hi"), sem("ln_lo")
        LN_STAT, LN_SCALE = 3, 4
        class AttentionSems:
            def __init__(self, n):
                self.max_ready, self.max_used = sem(f"{n}max_ready"), sem(f"{n}max_used")
                self.m_ready, self.mh_done = sem(f"{n}m_ready"), sem(f"{n}mh_done")
                self.aug_in = [sem(f"{n}aug_in{i}") for i in range(2)]
                self.stk_in = [sem(f"{n}stk_in{i}") for i in range(4)]
                self.st_ready, self.exp_done = sem(f"{n}st_ready"), sem(f"{n}exp_done")
                self.hi_done, self.lo_done = sem(f"{n}hi_done"), sem(f"{n}lo_done")
                self.lo_pool = sem(f"{n}lo_pool") if n == "b_" else None
                self.pv_done, self.y_tmp, self.y_done = sem(f"{n}pv_done"), sem(f"{n}y_tmp"), sem(f"{n}y_done")
                self.aux = sem(f"{n}aux")
                self.w_in = sem(f"{n}w_in") if n == "a_" else None
                self.w_hi, self.w_lo = sem(f"{n}w_hi"), sem(f"{n}w_lo")
                self.proj_done, self.raw_in = sem(f"{n}proj_done"), sem(f"{n}raw_in")
                self.src_hi, self.src_lo = sem(f"{n}src_hi"), sem(f"{n}src_lo")
                self.v_hi, self.v_lo = sem(f"{n}v_hi"), sem(f"{n}v_lo")
                self.fill = sem(f"{n}fill")
        a_vt_in = sem("a_vt_in")
        b_w_in = [sem(f"b_w_in{i}") for i in range(2)]
        SA, SB = AttentionSems("a_"), AttentionSems("b_")
        SA.prob, SA.phl, SA.y_lo, SA.y, SA.den = prob, phl, y_tmp, y, den
        SB.prob, SB.phl, SB.y_lo, SB.y, SB.den = prob_b, phl_b, y_tmp_b, y_b, den_b
        tab_in = sem("tab_in")
        turned, sin_done, cos_done, rope_done = sem("turned"), sem("sin_done"), sem("cos_done"), sem("rope_done")
        asc_ready, asc_in, asc_out, ak_in = sem("asc_ready"), sem("asc_in"), sem("asc_out"), sem("ak_in")
        den_in, r_done, rd_out, rden_in = sem("den_in"), sem("r_done"), sem("rd_out"), sem("rden_in")
        y_mul, yt_out = sem("y_mul"), sem("yt_out")
        by_r, by_y, by_hi, by_lo = sem("by_r"), sem("by_y"), sem("by_hi"), sem("by_lo")
        ad_in, av_in = sem("ad_in"), sem("av_in")
        ad_tr, ad_mx, ad_sub, ad_exp, ad_sum = sem("ad_tr"), sem("ad_mx"), sem("ad_sub"), sem("ad_exp"), sem("ad_sum")
        ad_rec, ad_p = sem("ad_rec"), sem("ad_p")
        ad_pt, ad_phi, ad_plo = sem("ad_pt"), sem("ad_phi"), sem("ad_plo")
        ad_yin = [sem(f"ad_yin{i}") for i in range(2)]
        ad_mm, ad_y, ad_hi, ad_lo = sem("ad_mm"), sem("ad_y"), sem("ad_hi"), sem("ad_lo")

        class DenseSems:
            def __init__(self, n, parts):
                self.w_in = [sem(f"{n}w_in{i}") for i in range(parts)]
                self.w_hi, self.w_lo = sem(f"{n}w_hi"), sem(f"{n}w_lo")
                self.tile, self.added = sem(f"{n}tile"), sem(f"{n}added")
        w_free = sem("w_free")
        SD, SO = DenseSems("d_", 4), DenseSems("o_", 1)
        ox_in, o_bias = sem("ox_in"), sem("o_bias")
        f_in = [sem(f"f_in{i}") for i in range(3)]
        f_hi, f_lo, f_h, f_hsb, f_lg = sem("f_hi"), sem("f_lo"), sem("f_h"), sem("f_hsb"), sem("f_lg")
        f_zt, f_dve, f_wt, f_hw, f_hwhi, f_hwlo = (sem(n) for n in ("f_zt", "f_dve", "f_wt", "f_hw", "f_hwhi", "f_hwlo"))
        f_bias = sem("f_bias")
        F_DVE = 14
        x_out = sem("x_out")

        def settle(eng):
            eng.sem_inc(passed, 1)

        def phase_end(eng, b, ph):
            settle(eng)
            eng.drain().then_inc(phase_done, 1)
            eng.wait_ge(phase_done, 5 * PHASES * b + 5 * (ph + 1))
            settle(eng)

        def setup_end(eng):
            eng.drain().then_inc(setup_done, 1)
            eng.wait_ge(setup_done, 5)

        def dve_norm_statistics(dve, i, t):
            n = LN_STAT * (TT * i + t)
            for h in range(2):
                last = dve.bn_stats(stats[:, t, h, :], X[:, t, h * HALF:(h + 1) * HALF])
            last.then_inc(ln_stat, 1)
            dve.wait_ge(ln_stat, n + 1)
            settle(dve)
            dve.bn_aggr(mv[:, t, :], stats[:, t, :, :].rearrange("p h s -> p (h s)")).then_inc(ln_stat, 1)
            dve.wait_ge(ln_stat, n + 2)
            dve.tensor_scalar(rs[:, 0, t:t + 1], mv[:, t, 1:2], EPS, None, ALU.add).then_inc(ln_stat, 1)

        def dve_norm_scale(dve, i, t):
            n = LN_SCALE * (TT * i + t)
            var, root, inv, tmp = (rs[:, j, t:t + 1] for j in range(4))
            dve.wait_ge(ln_root, TT * i + t + 1)
            dve.reciprocal(inv, root).then_inc(ln_scale, 1)
            dve.wait_ge(ln_scale, n + 1)
            dve.scalar_tensor_tensor(out=tmp, in0=inv, scalar=inv, in1=var, op0=ALU.mult,
                                     op1=ALU.mult).then_inc(ln_scale, 1)
            dve.wait_ge(ln_scale, n + 2)
            dve.tensor_scalar(tmp, tmp, -0.5, 1.5, ALU.mult, ALU.add).then_inc(ln_scale, 1)
            dve.wait_ge(ln_scale, n + 3)
            dve.tensor_tensor(inv, inv, tmp, ALU.mult).then_inc(ln_scale, 1)
            if t >= 2:
                dve.wait_ge(ln_tr, TT * i + t - 1)
            dve.wait_ge(ln_scale, n + 4)
            dve.tensor_scalar(xn[:, t % 2, :], X[:, t, :], mv[:, t, 0:1], inv,
                              ALU.subtract, ALU.mult).then_inc(ln_xn, 1)

        def dve_norm_lo(dve, i, t, alone):
            dve.wait_ge(ln_hi, TT * i + t + 1)
            dve.tensor_tensor(xt[1][:, :, t * P:(t + 1) * P], norm_bank(t, alone),
                              raw(xt[0][:, :, t * P:(t + 1) * P]), ALU.subtract).then_inc(ln_lo, 1)

        def dve_norm_step(dve, i, t, alone=False):
            if t < TT:
                dve_norm_statistics(dve, i, t)
            if 1 <= t <= TT:
                dve_norm_scale(dve, i, t - 1)
            if t >= 2:
                dve_norm_lo(dve, i, t - 2, alone)

        def act_norm_step(act, i, t, alone=False):
            if t < TT:
                act.wait_ge(ln_stat, LN_STAT * (TT * i + t) + 3)
                act.activation(rs[:, 1, t:t + 1], rs[:, 0, t:t + 1], ACT.Sqrt).then_inc(ln_root, 1)
            if t >= 2:
                s = t - 2
                act.wait_ge(ln_tr, TT * i + s + 1)
                act.copy(xt[0][:, :, s * P:(s + 1) * P], norm_bank(s, alone)).then_inc(ln_hi, 1)

        def pe_norm_step(pe, i, t, alone=False):
            if t < 2:
                return
            s = t - 2
            pe.wait_ge(ln_xn, TT * i + s + 1)
            if s >= 2:
                pe.wait_ge(ln_lo, TT * i + s - 1)
            for c in range(CC):
                last = pe.transpose(norm_bank(s, alone)[:, c, :], xn[:, s % 2, c * P:(c + 1) * P], ident[:])
            last.then_inc(ln_tr, 1)

        def norm_bank(t, alone):
            q = 2 * (t % 2) + (4 if alone else 0)
            return banks[:, q:q + 2, :].rearrange("p b (c t) -> p (b c) t", t=P)

        def sp_norm(sp, b):
            sp_load_x(sp, x_in[b].rearrange("(t p) c -> p t c", p=P))

        def sp_load_x(sp, source, parts=range(4)):
            for q in parts:
                sp.dma_start(X[:, 2 * q:2 * q + 2, :], source[:, 2 * q:2 * q + 2, :]).then_inc(x_ld[q], 16)

        def dve_norm(dve, b):
            for t in range(TT + 2):
                if t < TT:
                    dve.wait_ge(x_ld[t // 2], 16 * (3 * b + 1))
                dve_norm_step(dve, 4 * b, t, alone=True)

        def act_norm(act, b):
            for t in range(TT + 2):
                act_norm_step(act, 4 * b, t, alone=True)

        def pe_norm(pe, b):
            for t in range(TT + 2):
                pe_norm_step(pe, 4 * b, t, alone=True)
                if t == TT - 2:
                    pe.wait_ge(ln_lo, TT * 4 * b + TT // 2)
                    pe_a_part(pe, b, 0, 0, first=True)
                    for o, a, x, start, stop in pe_project(wq[0], halves=(0,)):
                        pe.matmul(o, a, x, start=start, stop=stop)

        def main_bank(k):
            return banks[:, 4 + k % 2, :]

        def max_index(H, j, i, first):
            if i == 0:
                return 0 if first and j == 0 else H.items * j - 1
            return H.items * j + i

        def turn_index(H, j, last):
            return H.items * j - (1 if last and j == 4 else 0)

        def max_bank(i):
            return banks[:, 2 + i % 2, :]

        def pe_max(pe, H, S, b, g, v, first=False, last=False):
            j, i = divmod(v, H.n)
            if last and v > H.slots + 1:
                return
            if i == 1 and not (first and v == 1):
                n = turn_index(H, j, last)
                pe.wait_ge(S.m_ready, H.heads * b + 4 * g + j)
                pe.wait_ge(S.max_used, H.items * (H.heads * b + 4 * g) + n - 1)
                pe.transpose(max_bank(n)[0:TT, 0:P], m_part[:, (j - 1) % 2, 0:TT], ident[:]).then_inc(S.max_ready, 1)
            if last and j >= 4:
                return
            n = max_index(H, j, i, first)
            if i == 0:
                pe.wait_ge(S.stk_in[j % 4], 96 * (H.groups * b + g + j // 4 + 1))
            if not (first and n < 2):
                pe.wait_ge(S.max_used, H.items * (H.heads * b + 4 * g) + n - 1)
            qt, k0, k1, _ = H.max[i]
            diag = H.causal and k1 == (qt + 1) * P
            bank = max_bank(n)
            mm = pe.matmul(bank[:, 0:k1 - k0], qst[0:96, j % 4, qt * P:(qt + 1) * P], kst[0:96, j % 4, k0:k1],
                           start=True, stop=True)
            if diag:
                mm = pe.matmul(bank[:, k1 - k0 - P:k1 - k0], ident16[:], mask_max[:], start=False, stop=True,
                               skip_group_check=True)
            mm.then_inc(S.max_ready, 1)

        def dve_max(dve, H, S, b, g, v, first=False, last=False):
            j, i = divmod(v, H.n)
            if last and v > H.slots + 1:
                return
            hb = H.heads * b + 4 * g
            if i == 1 and not (first and v == 1):
                n, h = turn_index(H, j, last), j - 1
                dve.wait_ge(S.max_ready, H.items * hb + n + 1)
                if not (first and h < 2):
                    dve.wait_ge(S.aug_in[h % 2], 32 * (H.heads // 2 * b + 2 * g + h // 2))
                bank = max_bank(n)[0:TT, 0:P]
                dve.tensor_scalar(m_row[0][:, h % 2, :], bank, -1.0, None, ALU.mult).then_inc(S.mh_done, 1)
                dve.wait_ge(S.mh_done, hb + h + 1)
                dve.scalar_tensor_tensor(out=m_row[1][:, h % 2, :], in0=bank, scalar=-1.0,
                                         in1=raw(m_row[0][:, h % 2, :]), op0=ALU.mult,
                                         op1=ALU.subtract).then_inc(S.max_used, 1)
            if last and j >= 4:
                return
            n = max_index(H, j, i, first)
            _, k0, k1, col = H.max[i]
            dve.wait_ge(S.max_ready, H.items * hb + n + 1)
            dve.tensor_reduce(m_part[:, j % 2, col:col + 1], max_bank(n)[:, 0:k1 - k0], AX.X,
                              ALU.max).then_inc(S.max_used, 1)
            if i == H.n - 1:
                lo, n2 = (4, 4) if H.causal else (0, TT)
                dve.wait_ge(S.max_used, H.items * hb + n + 1)
                dve.tensor_tensor(m_part[:, j % 2, lo:lo + n2], m_part[:, j % 2, lo:lo + n2],
                                  m_part[:, j % 2, 8:8 + n2], ALU.max).then_inc(S.m_ready, 1)

        def sp_max_rows(sp, H, S, b, g, h, last=False):
            sp.wait_ge(S.max_used, H.items * (H.heads * b + 4 * g) + turn_index(H, h + 1, last) + 1)
            settle(sp)
            for s in range(2):
                sp.dma_start(raw(qst[96 + s:97 + s, h % 4, :]), raw(m_row[s][:, h % 2, :])).then_inc(S.aug_in[h % 2], 16)

        def sp_stack(sp, H, S, b, g, h, first=False):
            width = HD if H.causal else HDB
            at_row = h * width if H.causal else (4 * g + h) * width
            rows = slice(at_row, at_row + width)
            if H.causal:
                sp.wait_ge(S.src_lo, 2 * H.groups * b + 2 * g + 2)
            else:
                sp.wait_ge(S.src_lo, 2 * b + 2)
            if not first:
                settle(sp)
                sp.wait_ge(S.pv_done, H.slots * (H.groups * b + g - 1) + H.n * (h + 1))
            settle(sp)
            for stack, part, order in ((qst, 0, (0, 1, 0)), (kst, 1, (0, 0, 1))):
                for i, s in enumerate(order):
                    sp.dma_start(raw(stack[32 * i:32 * i + width, h, :]),
                                 raw(src[part][s][rows, :])).then_inc(S.stk_in[h], 16)

        def pe_scores(pe, H, S, b, g, k, first=False):
            j, c = divmod(k, H.n)
            u = H.slots * (H.groups * b + g) + k
            if c == 0:
                pe.wait_ge(S.aug_in[j % 2], 32 * (H.heads // 2 * b + 2 * g + j // 2 + 1))
            if not (first and k < 2):
                pe.wait_ge(S.exp_done, u - 1)
            kt, q0, q1 = H.main[c]
            diag = H.causal and q0 == kt * P
            bank = main_bank(k)
            mm = pe.matmul(bank[:, 0:q1 - q0], kst[:, j % 4, kt * P:(kt + 1) * P], qst[:, j % 4, q0:q1],
                           start=True, stop=True)
            if diag:
                mm = pe.matmul(bank[:, 0:P], ident16[:], mask_main[:], start=False, stop=True, skip_group_check=True)
            mm.then_inc(S.st_ready, 1)

        def act_exp(act, H, S, b, g, k, first=False):
            kt, q0, q1 = H.main[k % H.n]
            u = H.slots * (H.groups * b + g) + k
            act.wait_ge(S.st_ready, u + 1)
            if not (first and k < H.ring):
                wait_lo(act, H, S, b, g, k - H.ring)
            act.activation(S.prob[:, k % H.ring, 0:q1 - q0], main_bank(k)[:, 0:q1 - q0], ACT.Exp,
                           scale=H.scale).then_inc(S.exp_done, 1)

        def act_hi(act, H, S, b, g, k, first=False):
            kt, q0, q1 = H.main[k % H.n]
            u = H.slots * (H.groups * b + g) + k
            act.wait_ge(S.exp_done, u + 1)
            if not (first and k < H.ring):
                act.wait_ge(S.pv_done, u - H.ring + 1)
            act.copy(S.phl[0][:, k % H.ring, 0:q1 - q0], S.prob[:, k % H.ring, 0:q1 - q0]).then_inc(S.hi_done, 1)

        def lo_by_pool(H, g, k):
            return not H.causal and (H.slots * g + k) % 3 == 2

        def wait_lo(eng, H, S, b, g, k):
            if H.causal:
                eng.wait_ge(S.lo_done, H.slots * (H.groups * b + g) + k + 1)
                return
            n, per_batch = H.slots * g + k, H.slots * H.groups
            if lo_by_pool(H, g, k):
                eng.wait_ge(S.lo_pool, per_batch // 3 * b + n // 3 + 1)
            else:
                eng.wait_ge(S.lo_done, (per_batch - per_batch // 3) * b + n - n // 3 + 1)

        def a_lo(eng, H, S, b, g, k):
            kt, q0, q1 = H.main[k % H.n]
            u = H.slots * (H.groups * b + g) + k
            eng.wait_ge(S.hi_done, u + 1)
            eng.tensor_tensor(S.phl[1][:, k % H.ring, 0:q1 - q0], S.prob[:, k % H.ring, 0:q1 - q0],
                              raw(S.phl[0][:, k % H.ring, 0:q1 - q0]),
                              ALU.subtract).then_inc(S.lo_pool if lo_by_pool(H, g, k) else S.lo_done, 1)

        def pe_pv(pe, H, S, b, g, k, first=False):
            if k < 0:
                g, k = g - 1, k + H.slots
            j, c = divmod(k, H.n)
            kt, q0, q1 = H.main[c]
            half = q0 // HALF
            u = H.slots * (H.groups * b + g) + k
            wait_lo(pe, H, S, b, g, k)
            if H.causal:
                v_stat = vst[:, kt, j, :]
                if c == 0 and j in (0, 3):
                    pe.wait_ge(S.v_lo, 2 * (H.groups * b + g) + (1 if j == 0 else 2))
            else:
                v_stat = vsb[:, kt, 4 * g + j, :]
            if kt == 0 and j % H.pair == 0 and not (first and j == 0):
                pe.wait_ge(S.y_done, y_index(H, b, g, j, half) - 1)
            for s in range(2):
                mm = pe.matmul(banks[0:96, 6 + half, q0 - half * HALF:q1 - half * HALF], v_stat,
                               S.phl[s][:, k % H.ring, 0:q1 - q0], start=(kt == 0 and s == 0 and j % H.pair == 0),
                               stop=True,
                               skip_group_check=True)
            mm.then_inc(S.pv_done, 1)

        def y_index(H, b, g, j, half):
            per = H.heads // H.pair
            return 2 * (per * b + 4 // H.pair * g + j // H.pair) + 1 - half

        def act_y(act, H, S, b, g, j, half, first=False):
            n = y_index(H, b, g, j, half)
            act.wait_ge(S.pv_done, H.slots * (H.groups * b + g) + H.n * j + H.last[half] + 1)
            if not (first and j // H.pair == 0 and half == 1):
                act.wait_ge(S.y_done, n)
            row = 32 * (j % 4) if H.causal else 32 * ((4 * g + j) // 2)
            act.copy(S.y_lo[:], banks[32:64, 6 + half, :])
            act.copy(S.den[row:row + 32, half * HALF:(half + 1) * HALF], banks[64:96, 6 + half, :]).then_inc(S.y_tmp, 1)

        def dve_y(dve, H, S, b, g, j, half):
            n = y_index(H, b, g, j, half)
            dve.wait_ge(S.y_tmp, n + 1)
            row = 32 * (j % 4) if H.causal else 32 * ((4 * g + j) // 2)
            dve.tensor_tensor(S.y[row:row + 32, half * HALF:(half + 1) * HALF], banks[0:32, 6 + half, :], S.y_lo[:],
                              ALU.add).then_inc(S.y_done, 1)

        def pe_project(weights, halves=(0, 1)):
            for c in range(CC):
                for a, x in PRODUCTS:
                    for h in halves:
                        yield (AUX[:, h * HALF:(h + 1) * HALF], weights[a][:, c, :],
                               xt[x][:, c, h * HALF:(h + 1) * HALF], c == 0 and (a, x) == (0, 0),
                               c == CC - 1 and (a, x) == PRODUCTS[-1])

        Q_SLOTS, K_SLOTS, V_SLOTS = range(3, 11), range(12, 19), range(21, 29)
        COPY_OUT = (11, 19, 29, 37)
        ROPE_DVE, ROPE_HI = (12, 21), (15, 24)
        ADAPTER, TURN_V = 36, 40
        RECIPROCALS = 5
        WEIGHTS, STACKS = (16, 31, 37), (25, 28, 38, 1)
        DENOMINATORS, STORE, ADAPTER_STORE = 4, 12, 39
        PROJECTION = 6 * CC

        def pe_a_part(pe, b, g, p, first=False):
            pe.wait_ge(SA.w_lo, 3 * G * b + 3 * g + p + 1)
            if p == 0:
                if not first:
                    pe.wait_ge(SA.v_lo, 2 * (G * b + g))
            else:
                pe.wait_ge(SA.raw_in, 2 * G * b + 2 * g + p)

        def pe_a_adapter(pe, b, g):
            pe.wait_ge(ak_in, G * b + g + 1)
            pe.wait_ge(SA.src_lo, 2 * G * b + 2 * g + 1)
            pe.wait_ge(a_vt_in, G * b + g + 1)
            for h in range(2):
                for n, (a, x) in enumerate(PRODUCTS):
                    mm = pe.matmul(AUX[0:4 * AK, h * HALF:(h + 1) * HALF], ak_cur[:, a, :],
                                   src[0][x][:, h * HALF:(h + 1) * HALF], start=n == 0, stop=n == 2)
            mm.then_inc(asc_ready, 1)

        def dve_a_adapter_keys(dve, b, g, first=False):
            if not first:
                dve.wait_ge(asc_ready, G * b + g)
            dve.tensor_copy(ak_cur[:], raw(ak_all[:, g, :, :])).then_inc(ak_in, 1)

        def pe_a_values(pe, b, g):
            pe.wait_ge(asc_in, G * b + g + 1)
            for t in range(TT):
                mm = pe.transpose(AUX[:, t * P:(t + 1) * P], vt[:, t * P:(t + 1) * P], ident[:])
            mm.then_inc(SA.aux, 1)

        def turned_values(part):
            heads = slice(0, 3) if part == 0 else slice(3, 4)
            return heads, AUX.rearrange("p (t j d) -> p t j d", t=TT, d=HD)[:, :, heads, :]

        def act_a_values(act, b, g, part, first=False):
            act.wait_ge(SA.aux, G * b + g + 1)
            if not first:
                act.wait_ge(SA.pv_done, HA.slots * (G * b + g - 1) + HA.n * (3 + part))
            if part:
                act.wait_ge(SA.v_lo, 2 * (G * b + g) + 1)
            heads, values = turned_values(part)
            act.copy(vst[:, :, heads, 0:HD], values).then_inc(SA.v_hi, 1)

        def dve_a_values(dve, b, g, part):
            dve.wait_ge(SA.v_hi, 2 * (G * b + g) + part + 1)
            heads, values = turned_values(part)
            dve.tensor_tensor(vst[:, :, heads, HD:2 * HD], values, raw(vst[:, :, heads, 0:HD]),
                              ALU.subtract).then_inc(SA.v_lo, 1)

        def act_a_copy_out(act, b, g, p, first=False, earlier=True):
            if p < 3:
                act.wait_ge(SA.proj_done, 3 * G * b + 3 * g + p + 1)
            else:
                act.wait_ge(asc_ready, G * b + g + 1)
            if p == 2:
                if not first:
                    act.wait_ge(yt_out, 16 * (G * b + g - 1))
                act.copy(vt[:], AUX).then_inc(a_vt_in, 1)
                return
            if p == 0:
                if earlier:
                    act.wait_ge(asc_out, 16 * (G * b + g))
                act.copy(turn[:], AUX).then_inc(SA.raw_in, 1)
            elif p == 1:
                act.wait_ge(SA.src_lo, 2 * G * b + 2 * g + 1)
                act.copy(turn[:], AUX).then_inc(SA.raw_in, 1)
            else:
                act.wait_ge(SA.src_lo, 2 * G * b + 2 * g + 2)
                act.copy(turn[0:4 * AK, :], AUX[0:4 * AK, :]).then_inc(asc_in, 1)

        def act_a_rope_hi(act, b, g, p, first=False):
            act.wait_ge(rope_done, 2 * G * b + 2 * g + p + 1)
            if not first:
                act.wait_ge(SA.stk_in[3], 96 * (G * b + g))
            act.copy(src[p][0][:], turn[:]).then_inc(SA.src_hi, 1)

        def dve_a_rope(dve, b, g, p, first=False):
            n = 2 * G * b + 2 * g + p
            dve.wait_ge(SA.raw_in, n + 1)
            if not first:
                dve.wait_ge(rope_done, n)
            settle(dve)
            dve.stream_shuffle(rot[:], turn[:], [(i + HD // 2) % HD for i in range(HD)]).then_inc(turned, 1)
            dve.wait_ge(turned, n + 1)
            dve.tensor_tensor(rot[:], rot[:], sin[:], ALU.mult).then_inc(sin_done, 1)

        def a_rope(eng, b, g, p):
            n = 2 * G * b + 2 * g + p
            eng.wait_ge(turned, n + 1)
            eng.tensor_tensor(turn[:], turn[:], cos[:], ALU.mult).then_inc(cos_done, 1)
            eng.wait_ge(cos_done, n + 1)
            eng.wait_ge(sin_done, n + 1)
            eng.tensor_tensor(turn[:], turn[:], rot[:], ALU.add).then_inc(rope_done, 1)
            eng.wait_ge(SA.src_hi, n + 1)
            eng.tensor_tensor(src[p][1][:], turn[:], raw(src[p][0][:]), ALU.subtract).then_inc(SA.src_lo, 1)

        def sp_a_weights(sp, b, g, p, first=False):
            n = 3 * G * b + 3 * g + p
            if not first:
                sp.wait_ge(SA.w_lo, n)
                settle(sp)
            sp.dma_start(wq_raw[:], w_qkv[g, p]).then_inc(SA.w_in, 16)

        def pool_a_weights(pool, b, g, p, first=False):
            n = 3 * G * b + 3 * g + p
            pool.wait_ge(SA.w_in, 16 * n + 16)
            if not first:
                pool.wait_ge(SA.proj_done, n - 2)
            settle(pool)
            pool.tensor_copy(wq[p][0][:], wq_raw[:]).then_inc(SA.w_hi, 1)
            pool.wait_ge(SA.w_hi, n + 1)
            pool.tensor_tensor(wq[p][1][:], wq_raw[:], raw(wq[p][0][:]), ALU.subtract).then_inc(SA.w_lo, 1)

        def sp_a_result_denominators(sp, b, g, last=False):
            n = G * b + g
            sp.wait_ge(SA.y_done, 8 * n + 8)
            settle(sp)
            sp.dma_start(d_col[:], den[0:P:32, :]).then_inc(den_in, 16)
            sp.wait_ge(r_done, n + 1)
            settle(sp)
            sp.dma_start(rd_dram[b, g], r_col[:]).then_inc(rd_out, 16)
            sp.wait_ge(rd_out, 16 * n + 16)
            settle(sp)
            if last:
                sp.wait_ge(yt_out, 16 * n)
                settle(sp)
            for j in range(4):
                sp.dma_start(rden[32 * j:32 * j + 32, :],
                             rd_dram[b, g, j:j + 1, :].broadcast_to([32, T])).then_inc(rden_in, 16)

        def dve_a_result_reciprocals(dve, b, g):
            n = G * b + g
            dve.wait_ge(den_in, 16 * n + 16)
            dve.reciprocal(r_col[:], d_col[:]).then_inc(r_done, 1)

        def pool_a_result(pool, b, g):
            n = G * b + g
            pool.wait_ge(rden_in, 64 * n + 64)
            pool.tensor_tensor(rden[:], y[:], rden[:], ALU.mult).then_inc(y_mul, 1)

        def sp_a_result_store(sp, b, g):
            n = G * b + g
            sp.wait_ge(y_mul, n + 1)
            settle(sp)
            sp.dma_start(yt_dram[b, g], rden[:]).then_inc(yt_out, 16)

        def sp_a_adapter_store(sp, b, g):
            sp.wait_ge(asc_in, G * b + g + 1)
            settle(sp)
            sp.dma_start(asc_dram[b, bass.ts(g, 4 * AK), :], turn[0:4 * AK, :]).then_inc(asc_out, 16)

        def pe_a_group(pe, b, g, first, more):
            parts = []
            if more >= 1:
                parts = [(slots, p, pe_project(wq[p])) for slots, p in ((Q_SLOTS, 0), (K_SLOTS, 1), (V_SLOTS, 2))]
            for k in range(HA.slots):
                if k + 1 < HA.slots or more:
                    pe_scores(pe, HA, SA, b, g, k + 1, first)
                pe_max(pe, HA, SA, b, g, k + HA.lead, last=not more)
                for slots, p, products in parts:
                    if k not in slots:
                        continue
                    if k == slots[0]:
                        pe_a_part(pe, b, g + 1, p)
                    at, n = slots.index(k), len(slots)
                    for _ in range(PROJECTION * at // n, PROJECTION * (at + 1) // n):
                        o, a, x, start, stop = next(products)
                        mm = pe.matmul(o, a, x, start=start, stop=stop)
                    if k == slots[-1]:
                        mm.then_inc(SA.proj_done, 1)
                if k == ADAPTER and more:
                    pe_a_adapter(pe, b, g + 1)
                if k == TURN_V and more:
                    pe_a_values(pe, b, g + 1)
                if k >= HA.lag or not first:
                    pe_pv(pe, HA, SA, b, g, k - HA.lag, first)

        def act_a_group(act, b, g, first, more):
            for k in range(HA.slots):
                act_hi(act, HA, SA, b, g, k, first)
                if k + 1 < HA.slots or more:
                    act_exp(act, HA, SA, b, g, k + 1, first)
                for at_k, p in zip(COPY_OUT, range(4)):
                    if k == at_k and more:
                        act_a_copy_out(act, b, g + 1, p, first)
                j, c = divmod(k, HA.n)
                for half, at_c in HA.result:
                    if c == at_c and j > 0:
                        if j == 1 and half == 1 and not first:
                            act.wait_ge(den_in, 16 * (G * b + g))
                        act_y(act, HA, SA, b, g, j - 1, half, first)
                    elif c == at_c and not first:
                        act_y(act, HA, SA, b, g - 1, 3, half)
                if k == 1 and not first:
                    act_a_values(act, b, g, 1)
                if k == TURN_V + 1 and more:
                    act_a_values(act, b, g + 1, 0)
                if more:
                    for at_k, p in zip(ROPE_HI, range(2)):
                        if k == at_k:
                            act_a_rope_hi(act, b, g + 1, p)

        def dve_a_group(dve, b, g, first, more):
            for k in range(HA.slots):
                dve_max(dve, HA, SA, b, g, k + HA.lead, first, last=not more)
                a_lo(dve, HA, SA, b, g, k)
                j, c = divmod(k, HA.n)
                for half, at_c in HA.result:
                    if c == at_c and j > 0:
                        if j == 1 and half == 1 and not first:
                            dve.wait_ge(y_mul, G * b + g)
                        dve_y(dve, HA, SA, b, g, j - 1, half)
                    elif c == at_c and not first:
                        dve_y(dve, HA, SA, b, g - 1, 3, half)
                if k == 1 and not first:
                    dve_a_values(dve, b, g, 1)
                if k == TURN_V + 1 and more:
                    dve_a_values(dve, b, g + 1, 0)
                if k == RECIPROCALS and not first:
                    dve_a_result_reciprocals(dve, b, g - 1)
                if more:
                    if k in ROPE_DVE:
                        dve_a_rope(dve, b, g + 1, ROPE_DVE.index(k))
                    if k == 30:
                        dve_a_adapter_keys(dve, b, g + 1)

        def pool_a_group(pool, b, g, first, more):
            if not first:
                pool_a_result(pool, b, g - 1)
            for p in range(2):
                if more:
                    a_rope(pool, b, g + 1, p)
            for p in range(3):
                if more >= 2:
                    pool_a_weights(pool, b, g + 2, p)

        def sp_a_group(sp, b, g, first, more):
            for k in range(HA.slots):
                if k in WEIGHTS and more >= 2:
                    sp_a_weights(sp, b, g + 2, WEIGHTS.index(k))
                if k == STACKS[3]:
                    sp_stack(sp, HA, SA, b, g, 3, first)
                if k == DENOMINATORS and not first:
                    sp_a_result_denominators(sp, b, g - 1)
                if k == STORE and not first:
                    sp_a_result_store(sp, b, g - 1)
                if k in STACKS[:3] and more:
                    sp_stack(sp, HA, SA, b, g + 1, STACKS.index(k))
                if (k + 5) % HA.n == 0 and ((k + 5) // HA.n < 4 or more):
                    sp_max_rows(sp, HA, SA, b, g, (k + 5) // HA.n, last=not more)
                if k == ADAPTER_STORE and more:
                    sp_a_adapter_store(sp, b, g + 1)

        def groups(eng, b, body):
            body(eng, b, 0, True, G - 1)
            with eng.Fori(1, G - 2) as g:
                body(eng, b, g, False, 2)
            body(eng, b, G - 2, False, 1)
            body(eng, b, G - 1, False, 0)

        def sp_a(sp, b):
            for p in range(3):
                sp_a_weights(sp, b, 0, p, first=p == 0)
                if p == 0:
                    sp.dma_start(cos[:], rope_cos).then_inc(tab_in, 16)
                    sp.dma_start(sin[:], rope_sin).then_inc(tab_in, 16)
            for h in range(3):
                sp_stack(sp, HA, SA, b, 0, h, first=True)
            sp_a_weights(sp, b, 1, 0)
            sp_a_adapter_store(sp, b, 0)
            sp_max_rows(sp, HA, SA, b, 0, 0)
            for p in (1, 2):
                sp_a_weights(sp, b, 1, p)
            groups(sp, b, sp_a_group)

        def pool_a(pool, b):
            pool.memset(raw(kst[96:98, :, :]), 1.0).then_inc(SA.fill, 1)
            pool.wait_ge(SA.fill, 2 * b + 1)
            settle(pool)
            pool.memset(raw(vst[:, :, :, 2 * HD:3 * HD]), 1.0).then_inc(SA.fill, 1)
            for p in range(3):
                pool_a_weights(pool, b, 0, p, first=True)
            for p in range(3):
                pool_a_weights(pool, b, 1, p)
            groups(pool, b, pool_a_group)
            pool_a_result(pool, b, G - 1)

        def pe_a(pe, b):
            pe.wait_ge(ln_lo, TT * (4 * b + 1))
            for p in range(3):
                if p:
                    pe_a_part(pe, b, 0, p, first=True)
                for o, a, x, start, stop in pe_project(wq[p], halves=(0, 1) if p else (1,)):
                    mm = pe.matmul(o, a, x, start=start, stop=stop)
                mm.then_inc(SA.proj_done, 1)
            pe_a_adapter(pe, b, 0)
            pe_a_values(pe, b, 0)
            pe.wait_ge(SA.fill, 2 * b + 2)
            for v in range(HA.lead):
                pe_max(pe, HA, SA, b, 0, v, first=True)
            pe_scores(pe, HA, SA, b, 0, 0, first=True)
            groups(pe, b, pe_a_group)
            for k in range(-HA.lag, 0):
                pe_pv(pe, HA, SA, b, G, k)

        def act_a(act, b):
            act_a_copy_out(act, b, 0, 0, earlier=False)
            act_a_rope_hi(act, b, 0, 0, first=True)
            act_a_copy_out(act, b, 0, 1)
            act_a_rope_hi(act, b, 0, 1, first=True)
            act_a_copy_out(act, b, 0, 2, first=True)
            act_a_copy_out(act, b, 0, 3)
            for part in range(2):
                act_a_values(act, b, 0, part, first=True)
            act_exp(act, HA, SA, b, 0, 0, first=True)
            groups(act, b, act_a_group)
            for half in (1, 0):
                act_y(act, HA, SA, b, G - 1, 3, half)

        def dve_a(dve, b):
            dve.wait_ge(tab_in, 32 * b + 32)
            for p in range(2):
                dve_a_rope(dve, b, 0, p, first=p == 0)
                a_rope(dve, b, 0, p)
            dve_a_adapter_keys(dve, b, 0, first=True)
            for part in range(2):
                dve_a_values(dve, b, 0, part)
            for v in range(HA.lead):
                dve_max(dve, HA, SA, b, 0, v, first=True)
            groups(dve, b, dve_a_group)
            for half in (1, 0):
                dve_y(dve, HA, SA, b, G - 1, 3, half)
            dve_a_result_reciprocals(dve, b, G - 1)

        CH_ROWS = [min(3, G - 3 * c) * 4 * AK for c in range(AH)]

        def sp_adapter(sp, b):
            sp.wait_ge(asc_out, 16 * (G * b + G))
            settle(sp)
            sp.wait_ge(SA.pv_done, HA.slots * G * (b + 1))
            settle(sp)
            for c in range(AH):
                sp.dma_start(asc[0:CH_ROWS[c], c, :],
                             asc_dram[b, 12 * AK * c:12 * AK * c + CH_ROWS[c], :]).then_inc(ad_in, 16)
            for s in range(2):
                sp.dma_start(raw(av[s][:]), av_dram[s]).then_inc(av_in, 16)
            sp_a_result_denominators(sp, b, G - 1, last=True)
            sp_a_result_store(sp, b, G - 1)
            sp.wait_ge(yt_out, 16 * (G * b + G))
            settle(sp)
            sp_dense_weights(sp, Dense("proj", b), 0, first=True)
            sp_load_x(sp, x_in[b].rearrange("(t p) c -> p t c", p=P), (0, 1))
            for g in range(G):
                if g >= 2:
                    sp.wait_ge(ad_y, G * b + g - 1)
                    settle(sp)
                sp.dma_start(yt_in_sb[:, g % 2, :], yt_dram[b, g]).then_inc(ad_yin[g % 2], 16)

        def pe_adapter(pe, b):
            pe.wait_ge(ad_in, 48 * b + 48)
            for t in range(TT + 1):
                if t < TT:
                    if t >= 2:
                        pe.wait_ge(ad_sub, TT * b + t - 1)
                    for c in range(AH):
                        mm = pe.transpose(banks[:, t % 2, 12 * AK * c:12 * AK * c + CH_ROWS[c]],
                                          asc[0:CH_ROWS[c], c, t * P:(t + 1) * P], ident[0:CH_ROWS[c], 0:CH_ROWS[c]])
                    mm.then_inc(ad_tr, 1)
                if t >= 1:
                    s = t - 1
                    pe.wait_ge(ad_p, TT * b + s + 1)
                    if s >= 2:
                        pe.wait_ge(ad_plo, TT * b + s - 1)
                    p_tile = a_e[:, s % 2, :, :].rearrange("p h k -> p (h k)")
                    for c in range(AH):
                        mm = pe.transpose(banks[0:CH_ROWS[c], 2 + s % 2, c * P:(c + 1) * P],
                                          p_tile[:, 12 * AK * c:12 * AK * c + CH_ROWS[c]], ident[:])
                    mm.then_inc(ad_pt, 1)
            pe.wait_ge(av_in, 32 * b + 32)
            pe.wait_ge(ad_plo, TT * b + TT)
            for g in range(G):
                c, rows = g // 3, CH_ROWS[g // 3]
                if g >= 2:
                    pe.wait_ge(ad_y, G * b + g - 1)
                for h in range(2):
                    for n, (a, x) in enumerate(PRODUCTS):
                        mm = pe.matmul(banks[:, 4 + 2 * (g % 2) + h, :], av[a][0:rows, g, :],
                                       pa[x][0:rows, c, h * HALF:(h + 1) * HALF], start=n == 0, stop=n == 2)
                mm.then_inc(ad_mm, 1)

        def dve_adapter(dve, b):
            for t in range(TT + 2):
                if t < TT:
                    n = TT * b + t
                    s_bank = banks[:, t % 2, 0:NH * AK].rearrange("p (h k) -> p h k", k=AK)
                    e, peak = a_e[:, t % 2, :, :], a_s[:, t % 2, 0, :]
                    dve.wait_ge(ad_tr, n + 1)
                    dve.tensor_reduce(peak, s_bank, AX.X, ALU.max).then_inc(ad_mx, 1)
                    dve.wait_ge(ad_mx, n + 1)
                    if t >= 2:
                        dve.wait_ge(ad_pt, n - 1)
                    dve.tensor_tensor(e, s_bank, peak.unsqueeze(2).broadcast_to([P, NH, AK]),
                                      ALU.subtract).then_inc(ad_sub, 1)
                if 1 <= t <= TT:
                    n = TT * b + t - 1
                    e, total, inv = a_e[:, (t - 1) % 2, :, :], *(a_s[:, (t - 1) % 2, i, :] for i in (1, 2))
                    dve.wait_ge(ad_exp, n + 1)
                    dve.tensor_reduce(total, e, AX.X, ALU.add).then_inc(ad_sum, 1)
                    dve.wait_ge(ad_sum, n + 1)
                    dve.reciprocal(inv, total).then_inc(ad_rec, 1)
                    dve.wait_ge(ad_rec, n + 1)
                    dve.scalar_tensor_tensor(out=e, in0=e, scalar=gate[:, 0:1], in1=inv.unsqueeze(2).broadcast_to([P, NH, AK]),
                                             op0=ALU.mult, op1=ALU.mult).then_inc(ad_p, 1)
                if t >= 2:
                    dve_adapter_lo(dve, b, t - 2)
            for g in range(G):
                dve.wait_ge(ad_mm, G * b + g + 1)
                dve.wait_ge(ad_yin[g % 2], 16 * (G // 2 * b + g // 2 + 1))
                if g >= 2:
                    dve.wait_ge(ad_lo, G * b + g - 1)
                q = 4 + 2 * (g % 2)
                dve.tensor_tensor(y_sum[:, g % 2, :], banks[:, q:q + 2, :].rearrange("p b n -> p (b n)"),
                                  yt_in_sb[:, g % 2, :], ALU.add).then_inc(ad_y, 1)
                if 1 <= g <= 4:
                    dense_weights_lo(dve, Dense("proj", b), 0, (g - 1,))

        def adapter_views(t, which):
            r = CH_ROWS[0]
            full = (banks[0:r, 2 + t % 2, 0:2 * P].rearrange("p (c t) -> p c t", c=2),
                    pa[which][0:r, 0:2, t * P:(t + 1) * P])
            r = CH_ROWS[2]
            short = (banks[0:r, 2 + t % 2, 2 * P:3 * P], pa[which][0:r, 2, t * P:(t + 1) * P])
            return full, short

        def dve_adapter_lo(dve, b, t):
            dve.wait_ge(ad_phi, TT * b + t + 1)
            for (bank, lo), (_, hi) in zip(adapter_views(t, 1), adapter_views(t, 0)):
                last = dve.tensor_tensor(lo, bank, raw(hi), ALU.subtract)
            last.then_inc(ad_plo, 1)

        def act_adapter(act, b):
            for t in range(TT + 1):
                if t < TT:
                    e = a_e[:, t % 2, :, :]
                    act.wait_ge(ad_sub, TT * b + t + 1)
                    act.activation(e, e, ACT.Exp, scale=SCALE_ADAPTER).then_inc(ad_exp, 1)
                if t >= 1:
                    act.wait_ge(ad_pt, TT * b + t)
                    for bank, hi in adapter_views(t - 1, 0):
                        last = act.copy(hi, bank)
                    last.then_inc(ad_phi, 1)
            for g in range(G):
                act.wait_ge(ad_y, G * b + g + 1)
                act.copy(xt[0][:, g, :], y_sum[:, g % 2, :]).then_inc(ad_hi, 1)
                if g < 4:
                    act_dense_weights(act, Dense("proj", b), 0, (g,))

        def pool_adapter(pool, b):
            for g in range(G):
                pool.wait_ge(ad_hi, G * b + g + 1)
                pool.tensor_tensor(xt[1][:, g, :], y_sum[:, g % 2, :], raw(xt[0][:, g, :]),
                                   ALU.subtract).then_inc(ad_lo, 1)

        class Dense:
            def __init__(self, name, b, f=0):
                self.ffn = name == "ffn"
                self.wide = name != "wo"
                self.S = SD if self.wide else SO
                self.cc = CC if self.wide else 1
                self.parts = 4 if self.wide else 1
                self.loads = 2 if self.wide else 1
                self.i = 3 * b + (0 if name == "proj" else 1 + f) if self.wide else b
                self.f, self.f0 = 2 * b + f, f
                self.dram = {"proj": w_proj, "ffn": w_base, "wo": wb_out}[name]
                self.name = name
                self.norm = {"proj": 4 * b + 1, "wo": 4 * b + 3, "ffn": 4 * b + 2 if f == 0 else None}[name]

            def place(self, i):
                return divmod(i, TT) if self.wide else (i % 2, i // 2)

            def norm_step(self, i):
                o, t = self.place(i)
                return t if self.norm is not None and o == 1 else None

            def finished(self, i):
                return (() if i < LAG else range(LAG + 1) if i == LAG else (i,)) if self.ffn else (i,)

            def chunks(self, part, s=None):
                if not self.wide:
                    return (h_sb if s is None else hw[s])[:].rearrange("p (o n) -> p o n", o=2)
                t = w_raw if s is None else w[s]
                return t[:, 2 * part:2 * part + 2, :]

            def weights(self, s, c, o):
                return w[s][:, c, :] if self.wide else hw[s][:, o * HALF:(o + 1) * HALF]

            def load_index(self, o):
                return self.loads * self.i + o

        def sp_dense_weights(sp, d, o, first=False):
            for q in range(d.parts):
                if not first:
                    sp.wait_ge(d.S.w_lo, d.parts * (d.load_index(o) - 1) + q + 1)
                    settle(sp)
                src_ap = d.dram[o, :, 2 * q:2 * q + 2, :] if d.wide else d.dram
                sp.dma_start(d.chunks(q), src_ap).then_inc(d.S.w_in[q], 16)

        def sp_dense(sp, b, d):
            if d.name == "proj":
                sp.wait_ge(ad_lo, G * (b + 1))
                settle(sp)
                sp_load_x(sp, x_in[b].rearrange("(t p) c -> p t c", p=P), (2, 3))
                sp_lora(sp)
                sp.dma_start(bias_row[:], b_base.broadcast_to([P, C])).then_inc(f_in[2], 16)
                sp_dense_weights(sp, d, 1)
            elif d.name == "wo":
                sp_load_x(sp, x_dram[b])
                sp_lora(sp)
                sp_dense_weights(sp, Dense("ffn", b, 1), 0)
                sp.wait_ge(o_bias, TT * (b + 1))
                settle(sp)
                sp.dma_start(bias_row[:], b_base.broadcast_to([P, C])).then_inc(f_in[2], 16)
            else:
                if d.f0 == 0:
                    sp_dense_weights(sp, d, 0)
                sp_dense_weights(sp, d, 1)
                for t in range(TT):
                    sp.wait_ge(SD.added, 2 * TT * d.i + TT + t + 1)
                    settle(sp)
                    to = x_dram[b, :, t, :] if d.f0 == 0 else out[b, t * P:(t + 1) * P, :]
                    sp.dma_start(to, X[:, t, :]).then_inc(x_out, 16)
                sp.wait_ge(x_out, 16 * TT * (d.f + 1))

        def sp_lora(sp):
            sp.dma_start(la_raw[:], w_lora_in).then_inc(f_in[0], 16)
            sp.dma_start(lb_raw[:], w_lora_out).then_inc(f_in[1], 16)

        def pool_dense(pool, b, d):
            if d.name == "proj":
                return
            if d.ffn:
                pool.wait_ge(f_in[2], 16 * d.f + 16)
            else:
                pool.wait_ge(ox_in, 16 * b + 16)
            for t in range(TT):
                if d.ffn:
                    pool.wait_ge(ln_xn, TT * (4 * b + 1 + 2 * d.f0) + t + 1)
                else:
                    pool.wait_ge(x_ld[t // 2], 16 * (3 * b + 3))
                pool.tensor_tensor(X[:, t, :], X[:, t, :], bias_row[:], ALU.add).then_inc(f_bias if d.ffn else o_bias, 1)
            if d.name == "wo":
                for i in range(2):
                    lora_lo(pool, 2 * b + 1, i)
                dense_weights_lo(pool, Dense("ffn", b, 1), 0)

        def act_dense(act, b, d):
            if d.name == "ffn":
                if d.f0 == 0:
                    act_dense_weights(act, d, 0)
                act.wait_ge(f_h, d.f + 1)
                act.activation(logit_t[:], banks[0:NE, 2:4, :].rearrange("p b n -> p (b n)"), ACT.Identity,
                               bias=b_rout[:, 0:1]).then_inc(f_lg, 1)
                act.copy(h_sb[:], AUX).then_inc(f_hsb, 1)
                act.wait_ge(f_hw, d.f + 1)
                act.copy(hw[0][:], h_sb[:]).then_inc(f_hwhi, 1)
                act_dense_weights(act, d, 1)
            elif d.name == "proj":
                for i in range(2):
                    act_lora(act, 2 * b, i)
                act_dense_weights(act, d, 1)
            else:
                act_dense_weights(act, d, 0)
            if d.norm is not None:
                for t in range(TT + 2):
                    act_norm_step(act, d.norm, t)
                    if d.name == "wo" and 1 <= t <= 2:
                        act_lora(act, 2 * b + 1, t - 1)
                    if d.name == "wo" and 3 <= t <= 6:
                        act_dense_weights(act, Dense("ffn", b, 1), 0, (t - 3,))

        lora_weights = ((la, la_raw), (lb, lb_raw))

        def act_lora(act, f, i):
            (hi, _), source = lora_weights[i]
            act.wait_ge(f_in[i], 16 * f + 16)
            act.copy(hi[:], source[:]).then_inc(f_hi, 1)

        def lora_lo(eng, f, i):
            (hi, lo), source = lora_weights[i]
            eng.wait_ge(f_hi, 2 * f + i + 1)
            eng.tensor_tensor(lo[:], source[:], raw(hi[:]), ALU.subtract).then_inc(f_lo, 1)

        def act_dense_weights(act, d, o, parts=None):
            for q in parts or range(d.parts):
                at_load = d.load_index(o)
                act.wait_ge(d.S.w_in[q], 16 * at_load + 16)
                if d.wide and not (d.name == "proj" and o == 0):
                    if q < d.parts - 1:
                        act.wait_ge(w_free, (d.parts - 1) * (at_load - 1) + q + 1)
                    else:
                        act.wait_ge(SD.tile, TT * at_load)
                act.copy(d.chunks(q, 0), d.chunks(q)).then_inc(d.S.w_hi, 1)

        def dense_weights_lo(eng, d, o, parts=None):
            for q in parts or range(d.parts):
                eng.wait_ge(d.S.w_hi, d.parts * d.load_index(o) + q + 1)
                eng.tensor_tensor(d.chunks(q, 1), d.chunks(q), raw(d.chunks(q, 0)), ALU.subtract).then_inc(d.S.w_lo, 1)

        def dve_routing(dve, f):
            step = [0]

            def done(ins):
                step[0] += 1
                ins.then_inc(f_dve, 1)
                dve.wait_ge(f_dve, F_DVE * f + step[0])

            z, cum, cnt, t0, t1, k1, s1, tau = (sp_buf[:, i, :] for i in range(8))

            def by_tile(a):
                return a.rearrange("p (t e) -> p t e", e=NE)

            ge, zge = pairs[:, 0], pairs[:, 1]
            dve.wait_ge(f_zt, f + 1)
            done(dve.tensor_copy(z, banks[:, 2, 0:TT * NE]))
            zi = by_tile(z).unsqueeze(3).broadcast_to([P, TT, NE, NE])
            zj = by_tile(z).unsqueeze(2).broadcast_to([P, TT, NE, NE])
            done(dve.tensor_tensor(ge, zj, zi, ALU.is_ge))
            dve.tensor_reduce(cnt, ge.rearrange("p t i j -> p (t i) j"), AX.X, ALU.add)
            done(dve.tensor_tensor(zge, ge, zj, ALU.mult))
            done(dve.tensor_reduce(cum, zge.rearrange("p t i j -> p (t i) j"), AX.X, ALU.add))
            done(dve.tensor_tensor(t0, cnt, z, ALU.mult))
            done(dve.tensor_scalar(t0, t0, 1.0, None, ALU.add))
            done(dve.tensor_tensor(t0, t0, cum, ALU.is_gt))
            done(dve.tensor_tensor(t1, t0, z, ALU.mult))
            dve.tensor_reduce(k1[:, 0:TT], by_tile(t0), AX.X, ALU.add)
            done(dve.tensor_reduce(s1[:, 0:TT], by_tile(t1), AX.X, ALU.add))
            done(dve.reciprocal(k1[:, TT:2 * TT], k1[:, 0:TT]))
            done(dve.scalar_tensor_tensor(out=tau[:, 0:TT], in0=s1[:, 0:TT], scalar=-1.0, in1=k1[:, TT:2 * TT],
                                          op0=ALU.add, op1=ALU.mult))
            done(dve.tensor_tensor(by_tile(t1), by_tile(z), tau[:, 0:TT].unsqueeze(2).broadcast_to([P, TT, NE]),
                                   ALU.subtract))
            done(dve.tensor_scalar(t0, t1, 0.0, None, ALU.max))
            spread = pairs[:].rearrange("p a t i j -> p (a t i j)")
            done(dve.tensor_copy(spread.rearrange("p (e r) -> p e r", r=R),
                                 t0.unsqueeze(2).broadcast_to([P, TT * NE, R])))
            assert step[0] == F_DVE, step[0]

        def dve_dense(dve, b, d):
            if d.ffn:
                if d.f0 == 0:
                    dense_weights_lo(dve, d, 0)
                dve_routing(dve, d.f)
                dve.wait_ge(f_wt, d.f + 1)
                dve.wait_ge(f_hsb, d.f + 1)
                dve.tensor_tensor(h_sb[:], AUX, h_sb[:], ALU.mult).then_inc(f_hw, 1)
                dve.wait_ge(f_hwhi, d.f + 1)
                dve.tensor_tensor(hw[1][:], h_sb[:], raw(hw[0][:]), ALU.subtract).then_inc(f_hwlo, 1)
            elif d.name == "wo":
                dense_weights_lo(dve, d, 0)
            n = 2 * TT
            for i in range(n):
                if i == TT - 2 and d.name == "proj":
                    for j in range(2):
                        lora_lo(dve, 2 * b, j)
                if i == TT - 1 and d.wide:
                    dense_weights_lo(dve, d, 1, range(d.parts - 1))
                for m in d.finished(i):
                    o, t = d.place(m)
                    if o == 0:
                        if d.name == "proj":
                            dve.wait_ge(x_ld[t // 2], 16 * (3 * b + 2))
                        else:
                            dve.wait_ge(f_bias if d.ffn else o_bias, TT * (d.f if d.ffn else b) + t + 1)
                    dve.wait_ge(d.S.tile, n * d.i + m + 1)
                    x = X[:, t, o * HALF:(o + 1) * HALF]
                    dve.tensor_tensor(x, banks[:, 4 + m % RING, :], x, ALU.add).then_inc(d.S.added, 1)
                    if i == TT - 1 and d.wide:
                        dense_weights_lo(dve, d, 1, (d.parts - 1,))
                if d.norm_step(i) is not None:
                    dve.wait_ge(d.S.added, n * d.i + i + 1)
                    dve_norm_step(dve, d.norm, d.norm_step(i))
            if d.norm is not None:
                for t in (TT, TT + 1):
                    dve_norm_step(dve, d.norm, t)

        def pe_lora_in(pe, f):
            pe.wait_ge(f_lo, 2 * f + 1)
            pe.wait_ge(ln_lo, TT * (2 * f + 2))
            for bank, rows in ((2, slice(P, P + NE)), (0, slice(0, P))):
                m = rows.stop - rows.start
                for c in range(CC):
                    for a, x in PRODUCTS:
                        for h in range(2):
                            mm = pe.matmul(banks[0:m, bank + h, :], la[a][:, c, rows], xt[x][:, c, h * HALF:(h + 1) * HALF],
                                           start=c == 0 and (a, x) == (0, 0), stop=c == CC - 1 and (a, x) == PRODUCTS[-1])
            mm.then_inc(f_h, 1)

        def pe_turn_logits(pe, f):
            pe.wait_ge(f_lg, f + 1)
            settle(pe)
            for t in range(TT):
                mm = pe.transpose(banks[:, 2, t * NE:(t + 1) * NE], logit_t[:, t * P:(t + 1) * P], ident[0:NE, 0:NE])
            mm.then_inc(f_zt, 1)

        def pe_turn_weights(pe, f):
            pe.wait_ge(f_dve, F_DVE * (f + 1))
            pe.wait_ge(f_hsb, f + 1)
            spread = pairs[:].rearrange("p a t i j -> p (a t i j)")
            for t in range(TT):
                mm = pe.transpose(AUX[:, t * P:(t + 1) * P], spread[:, t * P:(t + 1) * P], ident[:])
            mm.then_inc(f_wt, 1)

        def pe_dense(pe, b, d):
            if d.ffn:
                pe_lora_in(pe, d.f)
            elif d.name == "proj":
                pe.wait_ge(ad_lo, G * (b + 1))
            n = 2 * TT
            for i in range(n):
                o, t = d.place(i)
                if i >= RING:
                    pe.wait_ge(d.S.added, n * d.i + i - RING + 1)
                for q in range(d.parts):
                    if t == 0 and (d.wide or o == 0):
                        pe.wait_ge(d.S.w_lo, d.parts * d.load_index(min(o, d.loads - 1)) + q + 1)
                    for c in range(q * d.cc // d.parts, (q + 1) * d.cc // d.parts):
                        for m, (x, a) in enumerate(PRODUCTS):
                            mm = pe.matmul(banks[:, 4 + i % RING, :], xt[x][:, c, t * P:(t + 1) * P], d.weights(a, c, o),
                                           start=c == 0 and m == 0, stop=not d.ffn and c == d.cc - 1 and m == 2)
                    if d.wide and t == TT - 1 and q < d.parts - 1:
                        mm.then_inc(w_free, 1)
                if not d.ffn:
                    mm.then_inc(d.S.tile, 1)
                if d.ffn and i == 0:
                    pe_turn_logits(pe, d.f)
                if d.ffn and i == LAG - 1:
                    pe_turn_weights(pe, d.f)
                if d.ffn and i == LAG:
                    pe.wait_ge(f_hwlo, d.f + 1)
                    pe.wait_ge(f_lo, 2 * d.f + 2)
                if d.ffn:
                    for m_i in d.finished(i):
                        o, t = d.place(m_i)
                        for m, (x, a) in enumerate(PRODUCTS):
                            mm = pe.matmul(banks[:, 4 + m_i % RING, :], hw[x][:, t * P:(t + 1) * P],
                                           lb[a][:, o * HALF:(o + 1) * HALF], start=False, stop=m == 2)
                        mm.then_inc(d.S.tile, 1)
                if d.norm_step(i) is not None:
                    pe_norm_step(pe, d.norm, d.norm_step(i))
            if d.norm is not None:
                for t in (TT, TT + 1):
                    pe_norm_step(pe, d.norm, t)

        def sp_b(sp, b):
            for p in range(3):
                if p == 2:
                    sp.wait_ge(SB.w_lo, 3 * b + 1)
                    settle(sp)
                sp.dma_start(wb_raw[p % 2][:], wb_qkv[p]).then_inc(b_w_in[p % 2], 16)
            sp.wait_ge(SB.fill, 8 * (b + 1))
            settle(sp)
            for h in range(4):
                sp_stack(sp, HB, SB, b, 0, h, first=True)
            sp_max_rows(sp, HB, SB, b, 0, 0)
            for g in range(GB):
                for k in range(HB.slots):
                    if g + 1 < GB and k in (18, 34, 50):
                        sp_stack(sp, HB, SB, b, g + 1, (18, 34, 50).index(k))
                    if g and k == 1:
                        sp_stack(sp, HB, SB, b, g, 3)
                    if (k + 5) % HB.n == 0 and ((k + 5) // HB.n < 4 or g + 1 < GB):
                        sp_max_rows(sp, HB, SB, b, g, (k + 5) // HB.n, last=g + 1 == GB)
            for h in range(4):
                sp.wait_ge(SB.stk_in[h], 96 * GB * (b + 1))
                settle(sp)
            sp_dense_weights(sp, Dense("wo", b), 0, first=True)
            sp.dma_start(bias_row[:], bb_out.broadcast_to([P, C])).then_inc(ox_in, 16)

        def pool_b(pool, b):
            for i, (part, value) in enumerate(((qst[0:96, :, :], 0.0), (kst[0:96, :, :], 0.0), (kst[96:98, :, :], 1.0))):
                pool.memset(raw(part), value).then_inc(SB.fill, 1)
                pool.wait_ge(SB.fill, 8 * b + i + 1)
                settle(pool)
            pool.memset(raw(vsb[:]), 0.0).then_inc(SB.fill, 1)
            pool.wait_ge(SB.fill, 8 * b + 4)
            settle(pool)
            for odd in range(2):
                c0 = 64 + HDB * odd
                pool.memset(raw(vsb[:, :, odd::2, c0:c0 + HDB]), 1.0).then_inc(SB.fill, 2)
            for g in range(GB):
                for k in range(HB.slots):
                    if lo_by_pool(HB, g, k):
                        a_lo(pool, HB, SB, b, g, k)

        def pe_b(pe, b):
            for p in range(3):
                pe.wait_ge(SB.w_lo, 3 * b + p + 1)
                if p:
                    pe.wait_ge(SB.raw_in, 3 * b + p)
                for o, a, x, start, stop in pe_project(wb[p % 2]):
                    mm = pe.matmul(o, a, x, start=start, stop=stop)
                mm.then_inc(SB.proj_done, 1)
            pe.wait_ge(SB.raw_in, 3 * b + 3)
            for t in range(TT):
                mm = pe.transpose(AUX[:, t * P:(t + 1) * P], vt[:, t * P:(t + 1) * P], ident[:])
            mm.then_inc(SB.aux, 1)
            pe.wait_ge(SB.fill, 8 * b + 8)
            for v in range(HB.lead):
                pe_max(pe, HB, SB, b, 0, v, first=True)
            pe_scores(pe, HB, SB, b, 0, 0, first=True)
            pe.wait_ge(SB.v_lo, b + 1)
            for g in range(GB):
                for k in range(HB.slots):
                    if k + 1 < HB.slots or g + 1 < GB:
                        pe_scores(pe, HB, SB, b, g, k + 1, g == 0)
                    pe_max(pe, HB, SB, b, g, k + HB.lead, last=g == GB - 1)
                    if k >= HB.lag or g:
                        pe_pv(pe, HB, SB, b, g, k - HB.lag, g == 0)
            for k in range(-HB.lag, 0):
                pe_pv(pe, HB, SB, b, GB, k)

        def act_b_weights(act, b, p):
            act.wait_ge(b_w_in[p % 2], 32 * b + 16 * (p // 2) + 16 if p % 2 == 0 else 16 * b + 16)
            if p == 2:
                act.wait_ge(SB.proj_done, 3 * b + 1)
            act.copy(wb[p % 2][0][:], wb_raw[p % 2][:]).then_inc(SB.w_hi, 1)

        def act_b(act, b):
            for p in range(3):
                if p == 0:
                    act_b_weights(act, b, 0)
                if p < 2:
                    act_b_weights(act, b, p + 1)
                act.wait_ge(SB.proj_done, 3 * b + p + 1)
                if p == 1:
                    act.wait_ge(SB.src_lo, 2 * b + 1)
                dst = vt if p == 2 else turn
                act.activation(dst[:], AUX, ACT.Identity, bias=b_qkv[:, p:p + 1]).then_inc(SB.raw_in, 1)
                if p < 2:
                    act.wait_ge(SB.raw_in, 3 * b + p + 1)
                    act.copy(src[p][0][:], turn[:]).then_inc(SB.src_hi, 1)
            act.wait_ge(SB.fill, 8 * b + 8)
            act.wait_ge(SB.aux, b + 1)
            for odd in range(2):
                act.copy(vsb[:, :, odd::2, HDB * odd:HDB * odd + HDB], turned_b(odd)).then_inc(SB.v_hi, 1)
            act_exp(act, HB, SB, b, 0, 0, first=True)
            for g in range(GB):
                for k in range(HB.slots):
                    if k + 1 < HB.slots or g + 1 < GB:
                        act_exp(act, HB, SB, b, g, k + 1, g == 0)
                    act_hi(act, HB, SB, b, g, k, g == 0)
                    for half, at_c in HB.result:
                        if k % (2 * HB.n) == at_c and (k > at_c or g):
                            act_y(act, HB, SB, b, *((g, k // HB.n - 1) if k > at_c else (g - 1, 3)), half, g == 0)
            for half in (1, 0):
                act_y(act, HB, SB, b, GB - 1, 3, half)
            act.wait_ge(by_y, b + 1)
            act.copy(xt[0][:, 0, :], y_b[:]).then_inc(by_hi, 1)

        def turned_b(odd):
            return AUX.rearrange("p (t j d) -> p t j d", t=TT, d=HDB)[:, :, odd::2, :]

        def dve_b_weights(dve, b, p):
            (hi, lo), source = wb[p % 2], wb_raw[p % 2]
            dve.wait_ge(SB.w_hi, 3 * b + p + 1)
            dve.tensor_tensor(lo[:], source[:], raw(hi[:]), ALU.subtract).then_inc(SB.w_lo, 1)

        def dve_b(dve, b):
            for p in range(3):
                if p == 0:
                    dve_b_weights(dve, b, 0)
                if p < 2:
                    dve_b_weights(dve, b, p + 1)
                if p < 2:
                    dve.wait_ge(SB.src_hi, 2 * b + p + 1)
                    dve.tensor_tensor(src[p][1][:], turn[:], raw(src[p][0][:]), ALU.subtract).then_inc(SB.src_lo, 1)
            dve.wait_ge(SB.v_hi, 2 * b + 2)
            for odd in range(2):
                c0 = HDB * odd
                last = dve.tensor_tensor(vsb[:, :, odd::2, 32 + c0:32 + c0 + HDB], turned_b(odd),
                                         raw(vsb[:, :, odd::2, c0:c0 + HDB]), ALU.subtract)
            last.then_inc(SB.v_lo, 1)
            for v in range(HB.lead):
                dve_max(dve, HB, SB, b, 0, v, first=True)
            for g in range(GB):
                for k in range(HB.slots):
                    dve_max(dve, HB, SB, b, g, k + HB.lead, g == 0, last=g == GB - 1)
                    if not lo_by_pool(HB, g, k):
                        a_lo(dve, HB, SB, b, g, k)
                    for half, at_c in HB.result:
                        if k % (2 * HB.n) == at_c and (k > at_c or g):
                            dve_y(dve, HB, SB, b, *((g, k // HB.n - 1) if k > at_c else (g - 1, 3)), half)
            for half in (1, 0):
                dve_y(dve, HB, SB, b, GB - 1, 3, half)
            dve.wait_ge(SB.y_done, NHB * (b + 1))
            dve.reciprocal(rden_b[:], den_b[:]).then_inc(by_r, 1)
            dve.wait_ge(by_r, b + 1)
            dve.scalar_tensor_tensor(out=y_b[:], in0=y_b[:], scalar=SCALE_B_OUT, in1=rden_b[:], op0=ALU.mult,
                                     op1=ALU.mult).then_inc(by_y, 1)
            dve.wait_ge(by_hi, b + 1)
            dve.tensor_tensor(xt[1][:, 0, :], y_b[:], raw(xt[0][:, 0, :]), ALU.subtract).then_inc(by_lo, 1)

        def setup_block(n):
            return 2 - n // 2, n % 2

        def setup_raw(n):
            if n % 3 == 0:
                return w_raw[:]
            return X[:, 4 * (n % 3) - 4:4 * (n % 3), :].rearrange("p t (o n) -> p (t o) n", o=2)

        def setup_w(s, n):
            return xt[s][:, :, (n % 2) * HALF:(n % 2 + 1) * HALF]

        def sp_setup(sp):
            sp.dma_start(at_raw[:], adapter).then_inc(at_in, 16)
            for n in range(4):
                part, gh = setup_block(n)
                if n == 3:
                    sp.wait_ge(sw_lo, 2)
                for i in range(4):
                    sp.dma_start(setup_raw(n)[:, :, i * P:(i + 1) * P], w_qkv[4 * gh + i, part]).then_inc(sw_in[n % 3], 16)
            sp.dma_start(gate[:], gating.broadcast_to([P, 1])).then_inc(c_in, 16)
            sp.dma_start(b_rout[:], b_router).then_inc(c_in, 16)
            sp.dma_start(b_qkv[:], bb_qkv).then_inc(c_in, 16)
            sp.wait_ge(s_zero, 1)
            for s in range(2):
                sp.dma_start(av_dram[s], zeros[:].rearrange("p (g n) -> p g n", g=G)).then_inc(s_avd, 16)
            sp.wait_ge(s_avd, 32)
            sp.wait_ge(s_av, 2)
            for s in range(2):
                v = raw(avs[s][:]).rearrange("p (g j d) -> p g j d", g=G, d=HD)
                for g3 in range(3):
                    for j in range(4):
                        r0 = (4 * g3 + j) * AK
                        sp.dma_start(av_dram[s][r0:r0 + AK, g3::3, HD * j:HD * j + HD], v[:, g3::3, j, :]).then_inc(s_avd, 16)
            sp.wait_ge(s_avd, 32 + 24 * 16)
            sp.wait_ge(c_in, 48)

        def pool_setup(pool):
            pool.memset(ident[:], 0.0).then_inc(c_set, 1)
            pool.memset(mask_main[:], 0.0).then_inc(c_set, 1)
            pool.memset(mask_max[:], 0.0).then_inc(c_set, 1)
            pool.memset(raw(ak_all[:]), 0.0).then_inc(c_set, 1)
            pool.memset(zeros[:], 0.0).then_inc(s_zero, 1)
            pool.wait_ge(c_set, 4)
            row_minus_column = dict(base=0, pattern=[[-1, P]], channel_multiplier=1)
            pool.affine_select(out=ident[:], in_=ident[:], compare_op=ALU.not_equal, fill=1.0,
                               **row_minus_column).then_inc(c_set, 1)
            pool.affine_select(out=mask_main[:], in_=mask_main[:], compare_op=ALU.is_ge, fill=MASKED,
                               base=0, pattern=[[1, P]], channel_multiplier=-1).then_inc(c_set, 1)
            pool.affine_select(out=mask_max[:], in_=mask_max[:], compare_op=ALU.is_ge, fill=MASKED,
                               **row_minus_column).then_inc(c_set, 1)

        def act_setup(act):
            act.wait_ge(at_in, 16)
            act.copy(at[0][:], at_raw[:]).then_inc(sw_hi, 1)
            for n in range(5):
                if n < 4:
                    act.wait_ge(sw_in[n % 3], 64 * (n // 3 + 1))
                    if n >= 2:
                        act.wait_ge(s_mm, n - 1)
                    act.copy(setup_w(0, n), setup_raw(n)).then_inc(sw_hi, 1)
                if n >= 1:
                    m = n - 1
                    part, gh = setup_block(m)
                    act.wait_ge(s_mm, m + 1)
                    act.copy(akv[:, part - 1, gh * HALF:(gh + 1) * HALF], banks[0:AK, m % 2, :]).then_inc(s_ev, 1)
                if n == 2:
                    act.wait_ge(s_ev, 2)
                    act.copy(avs[0][:], akv[:, 1, :]).then_inc(s_av, 1)

        def dve_setup(dve):
            dve.wait_ge(c_set, 7)
            dve.tensor_copy(ident16[:], ident[:])
            dve.wait_ge(sw_hi, 1)
            dve.tensor_tensor(at[1][:], at_raw[:], raw(at[0][:]), ALU.subtract).then_inc(sw_lo, 1)
            for n in range(4):
                dve.wait_ge(sw_hi, n + 2)
                dve.tensor_tensor(setup_w(1, n), setup_raw(n), raw(setup_w(0, n)), ALU.subtract).then_inc(sw_lo, 1)
                if n == 2:
                    dve.wait_ge(s_av, 1)
                    dve.tensor_tensor(avs[1][:], akv[:, 1, :], raw(avs[0][:]), ALU.subtract).then_inc(s_av, 1)
            dve.wait_ge(s_tr, 1)
            turned_keys = banks[:, 2, 0:G * AK].rearrange("p (g k) -> p g k", k=AK)
            for j in range(4):
                rows, cols = slice(32 * j, 32 * j + 32), slice(AK * j, AK * j + AK)
                dve.tensor_copy(ak_all[rows, :, 0, cols], turned_keys[rows]).then_inc(s_tr, 1)
            dve.wait_ge(s_tr, 5)
            for j in range(4):
                rows, cols = slice(32 * j, 32 * j + 32), slice(AK * j, AK * j + AK)
                dve.tensor_tensor(ak_all[rows, :, 1, cols], turned_keys[rows], raw(ak_all[rows, :, 0, cols]), ALU.subtract)

        def pe_setup(pe):
            pe.wait_ge(c_set, 7)
            for n in range(4):
                pe.wait_ge(sw_lo, n + 2)
                if n >= 2:
                    pe.wait_ge(s_ev, n - 1)
                for c in range(CC):
                    for m, (x, a) in enumerate(PRODUCTS):
                        mm = pe.matmul(banks[0:AK, n % 2, :], at[x][:, c, :], setup_w(a, n)[:, c, :], start=c == 0 and m == 0,
                                       stop=c == CC - 1 and m == 2)
                mm.then_inc(s_mm, 1)
            pe.wait_ge(s_ev, 4)
            for g in range(G):
                mm = pe.transpose(banks[:, 2, g * AK:(g + 1) * AK], akv[:, 0, g * P:(g + 1) * P], ident[0:AK, 0:AK])
            mm.then_inc(s_tr, 1)

        def nothing(eng, *_):
            pass

        def program(eng, setup, norm_, attention_a, adapter_, dense_, attention_b):
            setup(eng)
            setup_end(eng)
            with eng.Fori(0, B) as b:
                norm_(eng, b)
                attention_a(eng, b)
                adapter_(eng, b)
                dense_(eng, b, Dense("proj", b))
                dense_(eng, b, Dense("ffn", b, 0))
                phase_end(eng, b, 0)
                attention_b(eng, b)
                phase_end(eng, b, 1)
                dense_(eng, b, Dense("wo", b))
                dense_(eng, b, Dense("ffn", b, 1))
                phase_end(eng, b, 2)

        block = ctx.enter_context(nc.Block())

        @block.sync
        def _(sp):
            program(sp, sp_setup, sp_norm, sp_a, sp_adapter, sp_dense, sp_b)

        @block.gpsimd
        def _(pool):
            program(pool, pool_setup, nothing, pool_a, pool_adapter, pool_dense, pool_b)

        @block.scalar
        def _(act):
            program(act, act_setup, act_norm, act_a, act_adapter, act_dense, act_b)

        @block.vector
        def _(dve):
            program(dve, dve_setup, dve_norm, dve_a, dve_adapter, dve_dense, dve_b)

        @block.tensor
        def _(pe):
            program(pe, pe_setup, pe_norm, pe_a, pe_adapter, pe_dense, pe_b)


def kernel(L0_attn_a_x, L0_attn_a_w_attn, L0_attn_a_w_proj, L0_attn_a_adapter_wte, L0_attn_a_gating,
           L0_attn_b_Wqk_w, L0_attn_b_Wqk_b, L0_attn_b_Wv_w, L0_attn_b_Wv_b, L0_attn_b_Wo_w, L0_attn_b_Wo_b,
           L0_ffn_W_base, L0_ffn_b_base, L0_ffn_W_router, L0_ffn_b_router, L0_ffn_lora_A, L0_ffn_lora_B):
    import numpy as np
    import concourse.bacc as bacc
    from concourse.bass_utils import run_bass_kernel_spmd

    def chunked(w_t):
        return w_t.reshape(-1, P, w_t.shape[1]).transpose(1, 0, 2)

    f32 = lambda a: np.ascontiguousarray(np.asarray(a))
    w_attn = f32(L0_attn_a_w_attn).reshape(3, G, P, CC, P)
    halves = lambda w_: f32(w_).reshape(2, HALF, CC, P).transpose(0, 3, 2, 1)
    wqk = f32(L0_attn_b_Wqk_w).reshape(P, 2, C)
    bqk = f32(L0_attn_b_Wqk_b).reshape(P, 2)
    wb = [chunked(a.T) for a in (wqk[:, 0], wqk[:, 1], f32(L0_attn_b_Wv_w))]
    lora_in = np.concatenate([f32(L0_ffn_lora_A).transpose(1, 0, 2).reshape(C, NE * R), f32(L0_ffn_W_router).T], 1)
    theta = (np.float32(1.0) / np.float32(10000.0) ** (np.arange(0, HD, 2, dtype=np.float32) / np.float32(HD))).astype(np.float32)
    angle = np.outer(theta, np.arange(T, dtype=np.float32)).astype(np.float32)
    cos_t, sin_t = np.cos(angle), np.sin(angle)
    arrays = {
        "x_in": f32(L0_attn_a_x),
        "w_qkv": w_attn.transpose(1, 0, 4, 3, 2),
        "w_proj": halves(L0_attn_a_w_proj),
        "adapter": chunked(f32(L0_attn_a_adapter_wte).T),
        "gating": f32(L0_attn_a_gating).reshape(1, 1),
        "rope_cos": np.tile(np.concatenate([cos_t, cos_t]), (4, 1)),
        "rope_sin": np.tile(np.concatenate([-sin_t, sin_t]), (4, 1)),
        "w_base": halves(L0_ffn_W_base),
        "b_base": f32(L0_ffn_b_base).reshape(1, C),
        "w_lora_in": chunked(lora_in),
        "b_router": f32(L0_ffn_b_router).reshape(NE, 1),
        "w_lora_out": f32(L0_ffn_lora_B).reshape(NE * R, C),
        "wb_qkv": np.stack(wb),
        "bb_qkv": np.stack([bqk[:, 0], bqk[:, 1], f32(L0_attn_b_Wv_b)], 1),
        "wb_out": f32(L0_attn_b_Wo_w).T.reshape(P, 2, HALF),
        "bb_out": f32(L0_attn_b_Wo_b).reshape(1, C),
    }
    nc = bacc.Bacc("TRN2", target_bir_lowering=False, num_devices=1)
    args = {}
    for name, a in arrays.items():
        arrays[name] = np.ascontiguousarray(a)
        args[name] = nc.dram_tensor(name + "_dram", a.shape, F32, kind="ExternalInput").ap()
    args["out"] = nc.dram_tensor("out_dram", (B, T, C), F32, kind="ExternalOutput").ap()
    build_program(nc, **args)
    r = run_bass_kernel_spmd(nc, [{n + "_dram": a for n, a in arrays.items()}], core_ids=[0])
    return r.results[0]["out_dram"]
```
